# Optimizing a Trainium2 kernel written in Bass

```python
import numpy as np
import jax
import jax.numpy as jnp

def _softmax(x, axis=-1):
    return jax.nn.softmax(x, axis=axis)

def _gelu(x):
    return jax.nn.gelu(x, approximate=True)

def _silu(x):
    return jax.nn.silu(x)

def _sigmoid(x):
    return jax.nn.sigmoid(x)

def _layernorm(x, axis=-1, eps=1e-05):
    m = jnp.mean(x, axis=axis, keepdims=True)
    v = jnp.var(x, axis=axis, keepdims=True)
    return (x - m) / jnp.sqrt(v + eps)

def _scatter_add(tgt, idx, src, axis=0):
    return tgt.at[idx].add(src)

def _segment_sum(src, seg, n):
    return jax.ops.segment_sum(src, seg, n)
kernel_name = 'mk_macaron_d1_jaxref_r4_7463c1'

def setup_inputs(seed: int=0):
    np.random.seed(seed)
    _w = jnp.asarray

    def _L0_attn_setup():
        import jax, jax.numpy as jnp
        import numpy as np
        EMBED_DIM = 256
        NUM_HEADS = 16
        HEAD_DIM = EMBED_DIM // NUM_HEADS
        LAMBDA_ENTANGLE = 0.35
        key = jax.random.key(seed)
        ks = jax.random.split(key, 10)
        B, S, D = (2, 512, EMBED_DIM)
        init = 1.0 / np.sqrt(D)
        x = jax.random.normal(ks[0], (B, S, D), dtype=jnp.float32)
        Wq = jax.random.uniform(ks[1], (D, D), jnp.float32, -init, init)
        bq = jax.random.uniform(ks[2], (D,), jnp.float32, -init, init)
        Wk = jax.random.uniform(ks[3], (D, D), jnp.float32, -init, init)
        bk = jax.random.uniform(ks[4], (D,), jnp.float32, -init, init)
        Wv = jax.random.uniform(ks[5], (D, D), jnp.float32, -init, init)
        bv = jax.random.uniform(ks[6], (D,), jnp.float32, -init, init)
        Wo = jax.random.uniform(ks[7], (D, D), jnp.float32, -init, init)
        bo = jax.random.uniform(ks[8], (D,), jnp.float32, -init, init)
        J_attn = jax.random.normal(ks[9], (NUM_HEADS, HEAD_DIM, HEAD_DIM), dtype=jnp.float32) * 0.02
        lambda_attn = jnp.asarray(LAMBDA_ENTANGLE, dtype=jnp.float32)
        return {'x': x, 'Wq': Wq, 'bq': bq, 'Wk': Wk, 'bk': bk, 'Wv': Wv, 'bv': bv, 'Wo': Wo, 'bo': bo, 'J_attn': J_attn, 'lambda_attn': lambda_attn}
    _L0_attn_in = _L0_attn_setup()

    def _L0_ffn_setup():
        import math
        import jax, jax.numpy as jnp
        import numpy as np
        B, T, H = (4, 512, 256)
        E, K, F = (8, 2, 512)
        CAP_FACTOR = 1.25

        def _moe_forward(x, Wg, W_in, W_out):
            b, t, h = x.shape
            xf = x.reshape(-1, h)
            S = xf.shape[0]
            C = int(math.ceil(K * S / E * CAP_FACTOR))
            logits = xf @ Wg
            probs = jax.nn.softmax(logits, axis=-1)
            top_vals, top_idx = jax.lax.top_k(probs, K)
            flat_idx = top_idx.T.reshape(-1)
            onehot = jax.nn.one_hot(flat_idx, E, dtype=jnp.int32)
            cum = jnp.cumsum(onehot, axis=0) - 1
            loc = jnp.take_along_axis(cum, flat_idx[:, None], axis=1)[:, 0]
            loc = loc.reshape(K, S).T
            keep = loc < C
            gates = top_vals * keep.astype(top_vals.dtype)
            denom = jnp.maximum(gates.sum(-1, keepdims=True), 1e-09)
            gates = gates / denom
            loc_c = jnp.where(keep, loc, C)
            e_flat = top_idx.reshape(-1)
            l_flat = loc_c.reshape(-1)
            xk = jnp.broadcast_to(xf[:, None, :], (S, K, h)).reshape(-1, h)
            xk = jnp.where(keep.reshape(-1, 1), xk, 0.0)
            buf = jnp.zeros((E, C + 1, h), x.dtype).at[e_flat, l_flat].set(xk)
            inp = buf[:, :C]
            hid = jnp.einsum('ech,ehf->ecf', inp, W_in)
            a, g = jnp.split(hid, 2, axis=-1)
            hid = jax.nn.gelu(a, approximate=False) * g
            out_e = jnp.einsum('ecf,efh->ech', hid, W_out)
            out_pad = jnp.concatenate([out_e, jnp.zeros((E, 1, h), out_e.dtype)], axis=1)
            gathered = out_pad[e_flat, l_flat].reshape(S, K, h)
            y = (gathered * gates[..., None]).sum(axis=1)
            return y.reshape(b, t, h)
        key = jax.random.key(seed)
        k1, k2, k3, k4 = jax.random.split(key, 4)
        x = jax.random.normal(k1, (B, T, H), dtype=jnp.float32)
        Wg = jax.random.normal(k2, (H, E), dtype=jnp.float32) * 0.02
        W_in = jax.random.normal(k3, (E, H, 2 * F), dtype=jnp.float32) * (1.0 / math.sqrt(H))
        W_out = jax.random.normal(k4, (E, F, H), dtype=jnp.float32) * (1.0 / math.sqrt(F))
        return {'x': x, 'Wg': Wg, 'W_in': W_in, 'W_out': W_out}
    _L0_ffn_in = _L0_ffn_setup()
    _d = {'L0_attn_x': _L0_attn_in['x'], 'L0_attn_Wq': _L0_attn_in['Wq'], 'L0_attn_bq': _L0_attn_in['bq'], 'L0_attn_Wk': _L0_attn_in['Wk'], 'L0_attn_bk': _L0_attn_in['bk'], 'L0_attn_Wv': _L0_attn_in['Wv'], 'L0_attn_bv': _L0_attn_in['bv'], 'L0_attn_Wo': _L0_attn_in['Wo'], 'L0_attn_bo': _L0_attn_in['bo'], 'L0_attn_J_attn': _L0_attn_in['J_attn'], 'L0_attn_lambda_attn': _L0_attn_in['lambda_attn'], 'L0_ffn_Wg': _L0_ffn_in['Wg'], 'L0_ffn_W_in': _L0_ffn_in['W_in'], 'L0_ffn_W_out': _L0_ffn_in['W_out']}
    _x0 = _d['L0_attn_x']
    _d['L0_attn_x'] = jax.random.normal(jax.random.fold_in(jax.random.key(seed), 1), (4, 1024, 256), dtype=_x0.dtype)
    del _x0
    return _d

def reference(L0_attn_x, L0_attn_Wq, L0_attn_bq, L0_attn_Wk, L0_attn_bk, L0_attn_Wv, L0_attn_bv, L0_attn_Wo, L0_attn_bo, L0_attn_J_attn, L0_attn_lambda_attn, L0_ffn_Wg, L0_ffn_W_in, L0_ffn_W_out):

    def _L0_attn_ref(x, Wq, bq, Wk, bk, Wv, bv, Wo, bo, J_attn, lambda_attn):
        import jax, jax.numpy as jnp
        import numpy as np
        EMBED_DIM = 256
        NUM_HEADS = 16
        HEAD_DIM = EMBED_DIM // NUM_HEADS
        LAMBDA_ENTANGLE = 0.35
        B, S, D = x.shape
        H, Hd = (NUM_HEADS, HEAD_DIM)
        scale = jnp.sqrt(jnp.asarray(Hd, dtype=x.dtype))

        def heads(W, b):
            y = jnp.einsum('bsd,ed->bse', x, W) + b
            return y.reshape(B, S, H, Hd).transpose(0, 2, 1, 3)
        Q = heads(Wq, bq)
        K = heads(Wk, bk)
        V = heads(Wv, bv)
        scores = jnp.einsum('bhid,bhjd->bhij', Q, K) / scale
        QJ = jnp.einsum('bhid,hde->bhie', jnp.tanh(Q), J_attn)
        delta = jnp.einsum('bhie,bhje->bhij', QJ, jnp.tanh(K))
        scores = scores + lambda_attn * delta
        causal = jnp.triu(jnp.ones((S, S), dtype=bool), k=1)
        scores = jnp.where(causal, -jnp.inf, scores)
        probs = jax.nn.softmax(scores, axis=-1)
        out = jnp.einsum('bhij,bhjd->bhid', probs, V)
        out = out.transpose(0, 2, 1, 3).reshape(B, S, D)
        return jnp.einsum('bsd,ed->bse', out, Wo) + bo

    def _L0_ffn_ref(x, Wg, W_in, W_out):
        import math
        import jax, jax.numpy as jnp
        import numpy as np
        B, T, H = (4, 512, 256)
        E, K, F = (8, 2, 512)
        CAP_FACTOR = 1.25

        def _moe_forward(x, Wg, W_in, W_out):
            b, t, h = x.shape
            xf = x.reshape(-1, h)
            S = xf.shape[0]
            C = int(math.ceil(K * S / E * CAP_FACTOR))
            logits = xf @ Wg
            probs = jax.nn.softmax(logits, axis=-1)
            top_vals, top_idx = jax.lax.top_k(probs, K)
            flat_idx = top_idx.T.reshape(-1)
            onehot = jax.nn.one_hot(flat_idx, E, dtype=jnp.int32)
            cum = jnp.cumsum(onehot, axis=0) - 1
            loc = jnp.take_along_axis(cum, flat_idx[:, None], axis=1)[:, 0]
            loc = loc.reshape(K, S).T
            keep = loc < C
            gates = top_vals * keep.astype(top_vals.dtype)
            denom = jnp.maximum(gates.sum(-1, keepdims=True), 1e-09)
            gates = gates / denom
            loc_c = jnp.where(keep, loc, C)
            e_flat = top_idx.reshape(-1)
            l_flat = loc_c.reshape(-1)
            xk = jnp.broadcast_to(xf[:, None, :], (S, K, h)).reshape(-1, h)
            xk = jnp.where(keep.reshape(-1, 1), xk, 0.0)
            buf = jnp.zeros((E, C + 1, h), x.dtype).at[e_flat, l_flat].set(xk)
            inp = buf[:, :C]
            hid = jnp.einsum('ech,ehf->ecf', inp, W_in)
            a, g = jnp.split(hid, 2, axis=-1)
            hid = jax.nn.gelu(a, approximate=False) * g
            out_e = jnp.einsum('ecf,efh->ech', hid, W_out)
            out_pad = jnp.concatenate([out_e, jnp.zeros((E, 1, h), out_e.dtype)], axis=1)
            gathered = out_pad[e_flat, l_flat].reshape(S, K, h)
            y = (gathered * gates[..., None]).sum(axis=1)
            return y.reshape(b, t, h)
        return _moe_forward(x, Wg, W_in, W_out)
    x = L0_attn_x
    x = x + 0.5 * _L0_ffn_ref(_layernorm(x, axis=-1), L0_ffn_Wg, L0_ffn_W_in, L0_ffn_W_out)
    x = x + _L0_attn_ref(_layernorm(x, axis=-1), L0_attn_Wq, L0_attn_bq, L0_attn_Wk, L0_attn_bk, L0_attn_Wv, L0_attn_bv, L0_attn_Wo, L0_attn_bo, L0_attn_J_attn, L0_attn_lambda_attn)
    x = x + 0.5 * _L0_ffn_ref(_layernorm(x, axis=-1), L0_ffn_Wg, L0_ffn_W_in, L0_ffn_W_out)
    return x

_drawn_inputs = setup_inputs


def setup_inputs(seed=0):
    import zlib

    import numpy as np

    out = dict(_drawn_inputs(seed))
    spreads = {}
    factors = {'L0_attn_Wq': 2.742, 'L0_attn_bq': 31.771, 'L0_attn_bk': 64.0, 'L0_attn_J_attn': 23.214}
    for name, (base, spread) in spreads.items():
        noise = np.random.default_rng([zlib.crc32(name.encode()), seed]).standard_normal(out[name].shape)
        drawn = base * np.exp(spread * noise) if base else spread * noise
        out[name] = jnp.asarray(drawn.astype(out[name].dtype))
    for name, factor in factors.items():
        out[name] = (out[name] * factor).astype(out[name].dtype)
    return out
```

```python
from contextlib import ExitStack

import concourse.bass as bass
from concourse import mybir

F32 = mybir.dt.float32
F32R = mybir.dt.float32r
BF16 = mybir.dt.bfloat16
I32 = mybir.dt.int32
ALU = mybir.AluOpType
ACT = mybir.ActivationFunctionType
AX = mybir.AxisListType

P = 128
BATCH, SEQ, D = 4, 1024, 256
TOK = BATCH * SEQ
NT = TOK // P
KD = D // P
EXP, TOPK, FF = 8, 2, 512
CAP = 1280
ST = CAP // P
KF = FF // P
ROW = D + 1
NOWHERE = 1 << 20
LN_EPS = 1e-5
CHUNKS = [(0, 512), (512, 512), (1024, 256)]


class Kit:

    def __init__(self, nc, ctx):
        self.nc, self.ctx = nc, ctx
        self.steps, self.step_sems = {}, {}

    def step_sem(self, name):
        if name not in self.step_sems:
            self.step_sems[name] = self.sem(name)
        return self.step_sems[name]

    def sb(self, name, shape, dt=F32, ctx=None):
        return (ctx or self.ctx).enter_context(self.nc.sbuf_tensor(name, shape, dt))

    def ps(self, name, shape, ctx=None, dt=F32):
        return (ctx or self.ctx).enter_context(self.nc.psum_tensor(f"{name}_psum", shape, dt))

    def sem(self, name):
        return self.ctx.enter_context(self.nc.semaphore(name))

    def sems(self, prefix, names):
        return [self.sem(f"{prefix}_{n}") for n in names.split()]


def chain(kit, eng, sem):

    def link(ins):
        kit.steps[sem] = kit.steps.get(sem, 0) + 1
        ins.then_inc(kit.step_sem(sem), 1)
        eng.wait_ge(kit.step_sem(sem), kit.steps[sem])

    return link


def constants(kit):
    nc = kit.nc
    c = {
        "ident": kit.sb("ident", [P, P]),
        "ident_bf": kit.sb("ident_bf", [P, P], BF16),
        "before_bf": kit.sb("before_bf", [P, P], BF16),
        "ones_bf": kit.sb("ones_bf", [P, P], BF16),
        "mask_qk": kit.sb("mask_qk", [P, P], BF16),
        "mask_kq": kit.sb("mask_kq", [P, P], BF16),
        "rank": kit.sb("rank", [P, EXP]),
        "x": kit.sb("x_res", [P, NT * D]),
    }
    return c


MASKED = -1e38
HEADS, HD = 16, 16
GH = 4
NG = HEADS // GH
HP = 32
PACK = 6 * HD
KT = SEQ // P
QC = 512


def build_constants(kit, c, x_dram):
    nc = kit.nc
    x_in, = kit.sems("const", "x_in")
    rank_i = kit.sb("rank_i", [P, EXP], I32)
    with nc.Block() as block:

        @block.sync
        def _(sp):
            xv = x_dram.rearrange("(t p) d -> p t d", p=P)
            for q in range(4):
                n = NT // 4
                sp.dma_start(c["x"][:, q * n * D:(q + 1) * n * D].rearrange("p (t d) -> p t d", d=D),
                             xv[:, q * n:(q + 1) * n, :]).then_inc(x_in, 16)
            sp.wait_ge(x_in, 64)

        @block.gpsimd
        def _(pool):
            link = chain(kit, pool, "pool_step")
            for name, v in (("ident", 0.0), ("ident_bf", 0.0), ("before_bf", 1.0), ("ones_bf", 1.0),
                            ("mask_qk", 0.0), ("mask_kq", 0.0)):
                link(nc.gpsimd.memset(c[name][:], v))
            for name in ("ident", "ident_bf"):
                link(nc.gpsimd.affine_select(out=c[name][:], in_=c[name][:], compare_op=ALU.not_equal, fill=1.0,
                                             base=0, pattern=[[-1, P]], channel_multiplier=1))
            link(nc.gpsimd.affine_select(out=c["before_bf"][:], in_=c["before_bf"][:], compare_op=ALU.is_ge, fill=0.0,
                                         base=-1, pattern=[[1, P]], channel_multiplier=-1))
            link(nc.gpsimd.affine_select(out=c["mask_qk"][:], in_=c["mask_qk"][:], compare_op=ALU.is_ge, fill=MASKED,
                                         base=0, pattern=[[-1, P]], channel_multiplier=1))
            link(nc.gpsimd.affine_select(out=c["mask_kq"][:], in_=c["mask_kq"][:], compare_op=ALU.is_ge, fill=MASKED,
                                         base=0, pattern=[[1, P]], channel_multiplier=-1))
            link(nc.gpsimd.iota(rank_i[:], pattern=[[-1, EXP]], base=EXP, channel_multiplier=0))
            link(nc.gpsimd.tensor_copy(c["rank"][:], rank_i[:]))


def rstd_of(nc, link, mean, rstd, stats, tmp, root_ready, act_ready):
    me, qe, mo, qo = stats[:, :, 1], stats[:, :, 2], stats[:, :, 4], stats[:, :, 5]
    a, b, ve = tmp
    link(nc.vector.tensor_tensor(mean, me, mo, ALU.add))
    link(nc.vector.tensor_scalar(mean, mean, 0.5, None, ALU.mult))
    link(nc.vector.tensor_tensor(a, me, mo, ALU.subtract))
    link(nc.vector.tensor_tensor(a, a, a, ALU.mult))
    link(nc.vector.tensor_tensor(b, qe, qo, ALU.add))
    link(nc.vector.tensor_scalar(b, b, 1.0 / D, LN_EPS, ALU.mult, ALU.add))
    nc.vector.scalar_tensor_tensor(ve, a, 0.25, b, ALU.mult, ALU.add).then_inc(root_ready, 1)
    nc.vector.wait_ge(act_ready, 1)
    link(nc.vector.reciprocal(a, rstd))
    link(nc.vector.tensor_tensor(b, a, a, ALU.mult))
    link(nc.vector.tensor_tensor(b, b, ve, ALU.mult))
    link(nc.vector.tensor_scalar(b, b, -0.5, 1.5, ALU.mult, ALU.add))
    link(nc.vector.tensor_tensor(rstd, a, b, ALU.mult))


def route(kit, c, r, wg_dram, disp, ydram, gates):
    nc, x = kit.nc, c["x"]
    U = 4
    with ExitStack() as ctx:
        sb = lambda n, s, dt=F32: kit.sb(f"r{r}_{n}", s, dt, ctx)
        ps = lambda n, s: kit.ps(f"r{r}_{n}", s, ctx)
        wg = sb("wg", [P, KD, EXP])
        blank = sb("blank", [P, ST * ROW])
        stats = sb("stats", [P, NT, 6])
        mean, rstd = sb("mean", [P, NT]), sb("rstd", [P, NT])
        tmp = [sb(f"tmp{i}", [P, NT]) for i in range(3)]
        stage = [sb(f"stage{u}", [P, D]) for u in range(U)]
        rows = sb("rows", [P, NT * ROW])
        rows3 = rows[:].rearrange("p (t c) -> p t c", c=ROW)
        xnT = [sb(f"xnT{u}", [P, KD, P]) for u in range(2)]
        logits = sb("logits", [P, NT * EXP])
        lg = logits[:].rearrange("p (t e) -> p t e", e=EXP)
        prob = sb("prob", [P, NT, EXP])
        pick = sb("pick", [P, NT, EXP])
        hot = sb("hot", [P, TOPK, NT, EXP])
        hot_bf = sb("hot_bf", [P, TOPK * NT * EXP], BF16)
        cum = sb("cum", [P, TOPK * NT * EXP])
        ahead = sb("ahead", [P, TOPK * NT * EXP])
        one64 = sb("one64", [P, TOPK * NT])
        best, rk = sb("best", [P, TOPK, NT]), sb("rk", [P, TOPK, NT])
        slot, keep, dest = (sb(n, [P, TOPK, NT]) for n in ("slot", "keep", "dest"))
        dest_i = sb("dest_i", [P, TOPK * NT], I32)
        id_i = sb("id_i", [P, NT], I32)
        den = sb("den", [P, NT])
        tp = [ps(f"tp{u}", [P, KD, P]) for u in range(2)]
        lg_ps = [ps(f"lg{u}", [P, 512]) for u in range(2)]
        within_ps = ps("within", [P, TOPK * NT * EXP])
        total_ps = ps("total", [P, TOPK * NT * EXP])

        (wg_in, blank_ready, filled, stats_done, root_ready, root_done, normed, row_kept,
         tposed, xnT_ready, logits_done, lg_free, centred, powered, hot_ready, counted,
         ids_ready, routed, sent0, ids_moved, sent1) = kit.sems(
            f"r{r}", "wg_in blank_ready filled stats_done root_ready root_done normed row_kept "
            "tposed xnT_ready logits_done lg_free centred powered hot_ready counted "
            "ids_ready routed sent0 ids_moved sent1")

        with nc.Block() as block:

            @block.sync
            def _(sp):
                sp.dma_start(wg[:], wg_dram.rearrange("(k p) e -> p k e", p=P)).then_inc(wg_in, 16)
                sp.wait_ge(blank_ready, 2)
                n = 0
                for e in range(EXP):
                    sp.dma_start(disp[e * CAP:(e + 1) * CAP, :].rearrange("(p j) c -> p (j c)", p=P),
                                 blank[:]).then_inc(filled, 16)
                    n += 1
                if r == 0:
                    zero = blank[:].rearrange("p (j c) -> p j c", c=ROW)[:, 0:8, 0:D]
                    for q in range(TOPK * NT // 8):
                        sp.dma_start(ydram[q * 8 * P:(q + 1) * 8 * P, :].rearrange("(p j) c -> p j c", p=P),
                                     zero).then_inc(filled, 16)
                        n += 1
                sp.wait_ge(filled, 16 * n)

            @block.gpsimd
            def _(pool):
                nc.gpsimd.memset(blank[:], 0.0).then_inc(blank_ready, 1)
                pool.wait_ge(blank_ready, 1)
                nc.gpsimd.memset(blank[:].rearrange("p (j c) -> p j c", c=ROW)[:, :, D].bitcast(I32),
                                 NOWHERE).then_inc(blank_ready, 1)
                nc.gpsimd.iota(id_i[:], pattern=[[P, NT]], base=0, channel_multiplier=1).then_inc(ids_ready, 1)
                pool.wait_ge(routed, 1)
                pool.wait_ge(row_kept, NT + U)
                pool.wait_ge(filled, 16 * (EXP + (8 if r == 0 else 0)))
                for k, sent in enumerate((sent0, sent1)):
                    if k:
                        pool.wait_ge(ids_moved, 1)
                    for t in range(NT):
                        nc.gpsimd.indirect_dma_start(
                            disp, bass.IndirectOffsetOnAxis(ap=dest_i[:, k * NT + t:k * NT + t + 1], axis=0),
                            rows3[:, t, :], None, bounds_check=EXP * CAP - 1, oob_is_err=False).then_inc(sent, 16)
                pool.wait_ge(sent1, 16 * NT)

            @block.vector
            def _(dve):
                link = chain(kit, dve, "dve_step")
                with nc.vector.Fori(0, NT // U) as i:
                    for u in range(U):
                        t = i * U + u
                        nc.vector.bn_stats(stats[:].rearrange("p t s -> p (t s)")[:, bass.ds(t * 6, 6)],
                                           x[:, bass.ds(t * D, D)]).then_inc(stats_done, 1)
                dve.wait_ge(stats_done, NT)
                rstd_of(nc, link, mean[:], rstd[:], stats, [a[:] for a in tmp], root_ready, root_done)
                dve.sem_inc(tposed, U)
                dve.sem_inc(row_kept, U)
                with nc.vector.Fori(0, NT // U) as i:
                    def norm(u):
                        t = i * U + u
                        dve.wait_ge(tposed, t + 1)
                        dve.wait_ge(row_kept, t + 1)
                        nc.vector.tensor_scalar(stage[u][:], x[:, bass.ds(t * D, D)], mean[:, bass.ds(t, 1)],
                                                rstd[:, bass.ds(t, 1)], ALU.subtract, ALU.mult).then_inc(normed, 1)
                    def keep_logits(u):
                        t = i * U + u
                        dve.wait_ge(logits_done, t + 3)
                        nc.vector.tensor_copy(logits[:, bass.ds(t * EXP, EXP)], lg_ps[u % 2][:, 0:EXP]).then_inc(lg_free, 1)

                    for u in range(U + 2):
                        if u < U:
                            norm(u)
                        if u >= 2:
                            keep_logits(u - 2)
                dve.wait_ge(lg_free, NT + 2)
                wide = lambda a: a.unsqueeze(2).to_broadcast([P, NT, EXP])
                link(nc.vector.reduce_max(den[:], lg, AX.X))
                nc.vector.tensor_tensor(prob[:], lg, wide(den[:]), ALU.subtract).then_inc(centred, 1)
                dve.wait_ge(powered, 1)
                link(nc.vector.reduce_sum(den[:], prob[:], AX.X))
                link(nc.vector.reciprocal(den[:], den[:]))
                link(nc.vector.tensor_tensor(prob[:], prob[:], wide(den[:]), ALU.mult))
                rank = c["rank"][:].unsqueeze(1).to_broadcast([P, NT, EXP])
                for k in range(TOPK):
                    link(nc.vector.reduce_max(best[:, k, :], prob[:], AX.X))
                    link(nc.vector.tensor_tensor(pick[:], prob[:], wide(best[:, k, :]), ALU.is_ge))
                    link(nc.vector.tensor_tensor(pick[:], pick[:], rank, ALU.mult))
                    link(nc.vector.reduce_max(rk[:, k, :], pick[:], AX.X))
                    link(nc.vector.tensor_tensor(hot[:, k, :, :], rank, wide(rk[:, k, :]), ALU.is_equal))
                    if k == 0:
                        link(nc.vector.scalar_tensor_tensor(prob[:], hot[:, 0, :, :], -2.0, prob[:], ALU.mult, ALU.add))
                hot_flat = hot[:].rearrange("p k t e -> p (k t e)")
                nc.vector.tensor_copy(hot_bf[:], hot_flat).then_inc(hot_ready, 1)
                link(nc.vector.memset(one64[:], 1.0))
                dve.wait_ge(counted, 1)
                link(nc.vector.tensor_copy(ahead[:], total_ps[:]))
                for e in range(EXP):
                    by = lambda a: a.rearrange("p (s e) -> p s e", e=EXP)[:, :, e]
                    link(nc.vector.tensor_tensor_scan(by(cum[:]), one64[:], by(ahead[:]), 0.0, ALU.mult, ALU.add))
                link(nc.vector.tensor_tensor(cum[:], cum[:], ahead[:], ALU.subtract))
                link(nc.vector.tensor_tensor(cum[:], cum[:], within_ps[:], ALU.add))
                link(nc.vector.tensor_tensor(cum[:], cum[:], hot_flat, ALU.mult))
                link(nc.vector.reduce_sum(slot[:].rearrange("p k t -> p (k t)"),
                                          cum[:].rearrange("p (s e) -> p s e", e=EXP), AX.X))
                link(nc.vector.tensor_scalar(keep[:], slot[:], float(CAP), None, ALU.is_lt))
                link(nc.vector.tensor_scalar(dest[:], rk[:], -float(CAP), float(EXP * CAP + NOWHERE), ALU.mult, ALU.add))
                link(nc.vector.tensor_tensor(dest[:], dest[:], slot[:], ALU.add))
                link(nc.vector.scalar_tensor_tensor(dest[:], keep[:], -float(NOWHERE), dest[:], ALU.mult, ALU.add))
                link(nc.vector.tensor_copy(dest_i[:], dest[:].rearrange("p k t -> p (k t)")))
                dve.wait_ge(ids_ready, 1)
                ids = rows3[:, :, D].bitcast(I32)
                nc.vector.tensor_copy(ids, id_i[:]).then_inc(routed, 1)
                link(nc.vector.tensor_tensor(best[:], best[:], keep[:], ALU.mult))
                link(nc.vector.tensor_tensor(den[:], best[:, 0, :], best[:, 1, :], ALU.add))
                link(nc.vector.tensor_scalar(den[:], den[:], 1e-9, None, ALU.max))
                link(nc.vector.reciprocal(den[:], den[:]))
                link(nc.vector.tensor_scalar(den[:], den[:], 0.5, None, ALU.mult))
                for k in range(TOPK):
                    link(nc.vector.tensor_tensor(gates[:, k, :], best[:, k, :], den[:], ALU.mult))
                dve.wait_ge(sent0, 16 * NT)
                nc.vector.tensor_scalar(ids, ids, TOK, None, ALU.add).then_inc(ids_moved, 1)

            @block.scalar
            def _(act):
                act.wait_ge(root_ready, 1)
                nc.scalar.activation(rstd[:], tmp[2][:], ACT.Sqrt).then_inc(root_done, 1)
                act.sem_inc(logits_done, 2)
                with nc.scalar.Fori(0, NT // U) as i:
                    for u in range(U):
                        t = i * U + u
                        act.wait_ge(tposed, t + 1 + U)
                        act.wait_ge(logits_done, t + 1)
                        nc.scalar.copy(xnT[u % 2][:], tp[u % 2][:]).then_inc(xnT_ready, 1)
                        nc.scalar.copy(rows[:, bass.ds(t * ROW, D)], stage[u][:]).then_inc(row_kept, 1)
                act.wait_ge(centred, 1)
                nc.scalar.activation(prob[:], prob[:], ACT.Exp).then_inc(powered, 1)

            @block.tensor
            def _(pe):
                pe.wait_ge(wg_in, 16)
                pe.sem_inc(lg_free, 2)
                pe.sem_inc(xnT_ready, 2)

                def transposes(t, u):
                    pe.wait_ge(normed, t + 1)
                    pe.wait_ge(xnT_ready, t + 1)
                    for k in range(KD):
                        last = nc.tensor.transpose(tp[u % 2][:, k, :], stage[u][:, k * P:(k + 1) * P], c["ident"][:])
                    last.then_inc(tposed, 1)

                def project(t, u):
                    pe.wait_ge(xnT_ready, t + 3)
                    pe.wait_ge(lg_free, t + 1)
                    for k in range(KD):
                        last = nc.tensor.matmul(lg_ps[u % 2][:, 0:EXP], xnT[u % 2][:, k, :], wg[:, k, :],
                                                start=(k == 0), stop=(k == KD - 1))
                    last.then_inc(logits_done, 1)

                with nc.tensor.Fori(0, NT // U) as i:
                    for u in range(U):
                        transposes(i * U + u, u)
                        if u:
                            project(i * U + u - 1, u - 1)
                    project(i * U + U - 1, U - 1)
                pe.wait_ge(hot_ready, 1)
                nc.tensor.matmul(within_ps[:], c["before_bf"][:], hot_bf[:], start=True, stop=True)
                nc.tensor.matmul(total_ps[:], c["ones_bf"][:], hot_bf[:], start=True, stop=True).then_inc(counted, 1)


def experts(kit, c, r, w_in_dram, w_out_dram, disp, ydram, spare):
    nc = kit.nc
    with ExitStack() as ctx:
        sb = lambda n, s, dt=F32: kit.sb(f"e{r}_{n}", s, dt, ctx)
        ps = lambda n, s: kit.ps(f"e{r}_{n}", s, ctx)
        NIN, NOUT = KD * 2 * FF, KF * D
        w_raw = sb("w_raw", [P, NIN + NOUT])
        w_hi = [sb(f"w_hi{u}", [P, NIN + NOUT], F32R) for u in range(2)]
        w_lo = [sb(f"w_lo{u}", [P, NIN + NOUT], F32R) for u in range(2)]
        slots = [sb(f"slots{u}", [P, ST * ROW]) for u in range(2)]
        s_hi, s_lo = sb("s_hi", [P, KD, CAP], F32R), sb("s_lo", [P, KD, CAP], F32R)
        act_a = [sb(f"act_a{u}", [P, 512]) for u in range(2)]
        hid = [sb(f"hid{u}", [P, 512]) for u in range(2)]
        h_hi = [sb(f"h_hi{u}", [P, KF, 512], F32R) for u in range(2)]
        h_lo = [sb(f"h_lo{u}", [P, KF, 512], F32R) for u in range(2)]
        res = [sb(f"res{u}", [P, D]) for u in range(4)]
        tp = ps("tp", [P, KD, 512])
        a_ps = [ps(f"a{u}", [P, 512]) for u in range(2)]
        g_ps = [ps(f"g{u}", [P, 512]) for u in range(2)]
        o_ps = [ps(f"o{u}", [P, 512]) for u in range(2)]
        (w_loaded, w_split, w_rest, s_tposed, s_hi_done, s_lo_done, a_done, g_done, gelu_done, hid_done,
         h_hi_done, h_lo_done, o_done, res_ready, slots_free, send_turn) = kit.sems(
            f"e{r}", "w_loaded w_split w_rest s_tposed s_hi_done s_lo_done a_done g_done gelu_done hid_done "
            "h_hi_done h_lo_done o_done res_ready slots_free send_turn")
        slots_in = kit.sems(f"e{r}_slots_in", "0 1")
        y_sent = kit.sems(f"e{r}_y_sent", "0 1 2 3")
        NC = len(CHUNKS)
        w_in_at = lambda w, k, f: w[:, k * 2 * FF + f * P:k * 2 * FF + (f + 1) * P]
        w_out_at = lambda w, k: w[:, NIN + k * D:NIN + (k + 1) * D]
        SPLIT0, HID0, O0, RES0, Y0 = 1, 2, 2 * ST, 2, 16
        RB = len(res)
        sent_in = lambda q, n: len([m for m in range(n) if m % RB == q])
        BODY = 2 * ST
        SENT = sent_in(0, BODY) * 16
        assert all(sent_in(q, BODY) * 16 == SENT for q in range(RB))
        m_ = lambda u, ci, f: (u * NC + ci) * KF + f

        with nc.Block() as block:

            @block.sync
            def _(sp):
                sp.sem_inc(w_rest, SPLIT0)
                sp.sem_inc(slots_free, 2)
                w_in_v = w_in_dram.rearrange("e (k p) f -> p (e k) f", p=P)
                w_out_v = w_out_dram.rearrange("e (k p) d -> p (e k) d", p=P)
                disp_v = disp.rearrange("(q j) c -> q (j c)", j=ST)
                with nc.sync.Fori(0, EXP // 2) as i:
                    for u in range(2):
                        e = i * 2 + u
                        sp.wait_ge(slots_free, e + 1)
                        sp.dma_start(slots[u][:], disp_v[bass.ds(e * P, P), :]).then_inc(slots_in[u], 16)
                        sp.wait_ge(w_rest, e + 1)
                        sp.dma_start(w_raw[:, 0:NIN].rearrange("p (k f) -> p k f", k=KD),
                                     w_in_v[:, bass.ds(e * KD, KD), :]).then_inc(w_loaded, 16)
                        sp.dma_start(w_raw[:, NIN:].rearrange("p (k d) -> p k d", k=KF),
                                     w_out_v[:, bass.ds(e * KF, KF), :]).then_inc(w_loaded, 16)

            @block.gpsimd
            def _(pool):
                last_row = nc.gpsimd.to_reg(TOPK * TOK - 1)
                link = chain(kit, pool, "pool_step")
                for q in range(RB):
                    link(nc.gpsimd.memset(res[q][:], 0.0))
                for q in range(RB):
                    nc.gpsimd.dma_start(spare[q], res[q][:, 0:16]).then_inc(y_sent[q], Y0)
                with nc.gpsimd.Fori(0, EXP // 2) as i:
                    for u in range(2):
                        e = i * 2 + u

                        def rests(ci):
                            n = CHUNKS[ci][1]
                            for f in range(KF):
                                m = e * NC * KF + ci * KF + f
                                pool.wait_ge(h_hi_done, m + 1)
                                hh = h_hi[(u * NC + ci) % 2][:, f, 0:n]
                                nc.gpsimd.tensor_tensor(h_lo[(u * NC + ci) % 2][:, f, 0:n], hid[m_(u, ci, f) % 2][:, 0:n],
                                                        hh.bitcast(F32), ALU.subtract).then_inc(h_lo_done, 1)

                        def send(ci):
                            c0, n = CHUNKS[ci]
                            for j in range(c0 // P, (c0 + n) // P):
                                pool.wait_ge(res_ready, e * ST + j + 1 + RES0)
                                pool.sem_inc(send_turn, 1)
                                at = bass.IndirectOffsetOnAxis(
                                    ap=slots[u][:, j * ROW + D:j * ROW + D + 1].bitcast(I32), axis=0)
                                nc.gpsimd.indirect_dma_start(ydram, at, res[(u * ST + j) % RB][:], None,
                                                             bounds_check=last_row,
                                                             oob_is_err=False).then_inc(y_sent[(u * ST + j) % RB], 16)

                        pool.wait_ge(w_split, e + 1)
                        nc.gpsimd.tensor_tensor(w_lo[u][:], w_raw[:], w_hi[u][:].bitcast(F32),
                                                ALU.subtract).then_inc(w_rest, 1)
                        rests(0)
                        rests(1)
                        send(0)
                        rests(2)
                        send(1)
                        send(2)
                        for q in range(RB):
                            pool.wait_ge(y_sent[q], Y0 + i * SENT + sent_in(q, (u + 1) * ST) * 16)
                        pool.sem_inc(slots_free, 1)

            @block.vector
            def _(dve):
                dve.sem_inc(o_done, O0)
                with nc.vector.Fori(0, EXP // 2) as i:
                    for u in range(2):
                        e = i * 2 + u

                        def slots_lo(ci):
                            c0, n = CHUNKS[ci]
                            dve.wait_ge(s_hi_done, e * NC + ci + 1)
                            nc.vector.tensor_tensor(s_lo[:, :, c0:c0 + n], tp[:, :, 0:n],
                                                    s_hi[:, :, c0:c0 + n].bitcast(F32),
                                                    ALU.subtract).then_inc(s_lo_done, 1)

                        def hidden(ci):
                            n = CHUNKS[ci][1]
                            h = (u * NC + ci) % 2
                            c0 = CHUNKS[ci - 2][0] + CHUNKS[ci - 2][1] - (0 if ci >= 2 else CAP)
                            dve.wait_ge(o_done, e * ST + c0 // P + O0)
                            for f in range(KF):
                                m = e * NC * KF + ci * KF + f
                                q = m_(u, ci, f) % 2
                                dve.wait_ge(gelu_done, m + 1)
                                dve.wait_ge(g_done, m + 1)
                                dve.wait_ge(h_lo_done, m + 1)
                                nc.vector.tensor_tensor(hid[q][:, 0:n], act_a[q][:, 0:n], g_ps[q][:, 0:n],
                                                        ALU.mult).then_inc(hid_done, 1)
                                dve.wait_ge(hid_done, m + 1 + HID0)
                                nc.vector.tensor_copy(h_hi[h][:, f, 0:n], hid[q][:, 0:n]).then_inc(h_hi_done, 1)

                        dve.wait_ge(w_loaded, (e + 1) * 32)
                        dve.wait_ge(o_done, (e - 1) * ST + O0)
                        nc.vector.tensor_copy(w_hi[u][:], w_raw[:]).then_inc(w_split, 1)
                        slots_lo(0)
                        slots_lo(1)
                        hidden(0)
                        slots_lo(2)
                        hidden(1)
                        hidden(2)

            @block.scalar
            def _(act):
                act.sem_inc(hid_done, HID0)
                act.sem_inc(h_lo_done, HID0)
                with nc.scalar.Fori(0, EXP // 2) as i:
                    for u in range(2):
                        e = i * 2 + u

                        def slots_hi(ci):
                            c0, n = CHUNKS[ci]
                            act.wait_ge(s_tposed, e * NC + ci + 1)
                            nc.scalar.copy(s_hi[:, :, c0:c0 + n], tp[:, :, 0:n]).then_inc(s_hi_done, 1)

                        def gelu(ci):
                            n = CHUNKS[ci][1]
                            for f in range(KF):
                                m = e * NC * KF + ci * KF + f
                                q = m_(u, ci, f) % 2
                                act.wait_ge(a_done, m + 1)
                                act.wait_ge(hid_done, m + 1)
                                nc.scalar.activation(act_a[q][:, 0:n], a_ps[q][:, 0:n], ACT.Gelu).then_inc(gelu_done, 1)

                        def results(ci):
                            c0, n = CHUNKS[ci]
                            for j in range(c0 // P, (c0 + n) // P):
                                m = e * ST + j
                                act.wait_ge(o_done, m + 1 + O0)
                                b = u * ST + j
                                act.wait_ge(y_sent[b % RB], Y0 + SENT * i + b // RB * 16)
                                nc.scalar.copy(res[b % RB][:], o_ps[(u * ST + j) % 2][:, 0:D]).then_inc(res_ready, 1)

                        slots_hi(0)
                        slots_hi(1)
                        gelu(0)
                        slots_hi(2)
                        gelu(1)
                        results(0)
                        gelu(2)
                        results(1)
                        results(2)

            @block.tensor
            def _(pe):
                pe.sem_inc(s_lo_done, 1)
                pe.sem_inc(res_ready, RES0)
                with nc.tensor.Fori(0, EXP // 2) as i:
                    for u in range(2):
                        e = i * 2 + u

                        def transposes(ci):
                            c0, n = CHUNKS[ci]
                            if ci == 0:
                                pe.wait_ge(slots_in[u], (i + 1) * 16)
                            pe.wait_ge(s_lo_done, e * NC + ci + 1)
                            for j in range(n // P):
                                for k in range(KD):
                                    at = (c0 // P + j) * ROW + k * P
                                    last = nc.tensor.transpose(tp[:, k, j * P:(j + 1) * P], slots[u][:, at:at + P],
                                                               c["ident"][:])
                            last.then_inc(s_tposed, 1)

                        def up(ci):
                            c0, n = CHUNKS[ci]
                            pe.wait_ge(s_lo_done, e * NC + ci + 2)
                            if ci == 0:
                                pe.wait_ge(w_rest, e + 1 + SPLIT0)
                            for f in range(KF):
                                m = e * NC * KF + ci * KF + f
                                q = m_(u, ci, f) % 2
                                pe.wait_ge(hid_done, m + 1)
                                for half, bank, done in ((0, a_ps, a_done), (KF, g_ps, g_done)):
                                    terms = [(w, s, k) for k in range(KD)
                                             for w, s in ((w_hi[u], s_hi), (w_hi[u], s_lo), (w_lo[u], s_hi))]
                                    for z, (w, s, k) in enumerate(terms):
                                        last = nc.tensor.matmul(bank[q][:, 0:n], w_in_at(w, k, half + f),
                                                                s[:, k, c0:c0 + n], start=(z == 0),
                                                                stop=(z == len(terms) - 1))
                                    last.then_inc(done, 1)

                        def down(ci):
                            c0, n = CHUNKS[ci]
                            h = (u * NC + ci) % 2
                            pe.wait_ge(h_lo_done, e * NC * KF + (ci + 1) * KF + HID0)
                            for j in range(n // P):
                                m = e * ST + c0 // P + j
                                pe.wait_ge(res_ready, m + 1)
                                terms = [(w, s, k) for k in range(KF)
                                         for w, s in ((w_hi[u], h_hi[h]), (w_lo[u], h_hi[h]), (w_hi[u], h_lo[h]))]
                                for z, (w, s, k) in enumerate(terms):
                                    last = nc.tensor.matmul(o_ps[(u * ST + c0 // P + j) % 2][:, 0:D],
                                                            s[:, k, j * P:(j + 1) * P], w_out_at(w, k),
                                                            start=(z == 0), stop=(z == len(terms) - 1))
                                last.then_inc(o_done, 1)

                        transposes(0)
                        transposes(1)
                        up(0)
                        transposes(2)
                        up(1)
                        down(0)
                        up(2)
                        down(1)
                        down(2)


def combine(kit, c, r, ydram, gates, out_dram):
    nc, x = kit.nc, c["x"]
    U = 4
    with ExitStack() as ctx:
        y = [kit.sb(f"c{r}_y{u}", [P, TOPK, U, D], F32, ctx) for u in range(2)]
        mixed, first, stored = kit.sems(f"c{r}", "mixed first stored")
        y_in = kit.sems(f"c{r}_y_in", "0 1")
        with nc.Block() as block:

            @block.sync
            def _(sp):
                yv = ydram.rearrange("(k t p) d -> p k t d", k=TOPK, p=P)
                sp.sem_inc(mixed, 2 * U)
                with nc.sync.Fori(0, NT // U // 2) as i:
                    for u in range(2):
                        s = i * 2 + u
                        sp.wait_ge(mixed, (s + 1) * U)
                        for k in range(TOPK):
                            sp.dma_start(y[u][:, k, :, :], yv[:, k, bass.ds(s * U, U), :]).then_inc(y_in[u], 16)

            @block.vector
            def _(dve):
                with nc.vector.Fori(0, NT // U // 2) as i:
                    for u in range(2):
                        s = i * 2 + u
                        dve.wait_ge(y_in[u], (i + 1) * 16 * TOPK)
                        for k in range(TOPK):
                            if k:
                                dve.wait_ge(first, (s + 1) * U)
                            for v in range(U):
                                t = s * U + v
                                xt = x[:, bass.ds(t * D, D)]
                                nc.vector.scalar_tensor_tensor(
                                    xt, y[u][:, k, v, :], gates[:].rearrange("p k t -> p (k t)")[:, bass.ds(t + k * NT, 1)],
                                    xt, ALU.mult, ALU.add).then_inc(mixed if k else first, 1)

            if out_dram is not None:
                @block.scalar
                def _(act):
                    ov = out_dram.rearrange("(t p) d -> p t d", p=P)
                    with nc.scalar.Fori(0, NT // U) as i:
                        act.wait_ge(mixed, (i + 3) * U)
                        act.dma_start(ov[:, bass.ds(i * U, U), :],
                                      x[:].rearrange("p (t d) -> p t d", d=D)[:, bass.ds(i * U, U), :]).then_inc(stored, 16)
                    act.wait_ge(stored, NT // U * 16)



def project(kit, c, w, packs, v_dram):
    nc, x = kit.nc, c["x"]
    U = QC // P
    with ExitStack() as ctx:
        sb = lambda n, s, dt=F32: kit.sb(f"q_{n}", s, dt, ctx)
        ps = lambda n, s: kit.ps(f"q_{n}", s, ctx)
        stats = sb("stats", [P, NT, 6])
        mean, rstd = sb("mean", [P, NT]), sb("rstd", [P, NT])
        tmp = [sb(f"tmp{i}", [P, NT]) for i in range(3)]
        NW = 3 * KD * D
        w_raw = sb("w_raw", [P, NW + KD * P])
        w_hi, w_lo = (sb(n, [P, NW + KD * P], F32R) for n in ("w_hi", "w_lo"))
        bias = sb("bias", [P, 3, KD])
        bv = sb("bv", [P, D])
        lam = sb("lam", [P, 1])
        stage = [sb(f"stage{u}", [P, D]) for u in range(U)]
        x_hi, x_lo = (sb(n, [P, KD, QC], F32R) for n in ("x_hi", "x_lo"))
        full = {n: [sb(f"{n}{u}", [P, QC]) for u in range(KD)] for n in ("q", "tq", "t", "k", "tk")}
        tq_hi, tq_lo = ([sb(f"{n}{u}", [P, QC], F32R) for u in range(KD)] for n in ("tq_hi", "tq_lo"))
        pack = [sb(f"pack{u}", [P, 8, QC], F32R) for u in range(KD)]
        vals = sb("vals", [P, U, HEADS, HP])
        tp = ps("tp", [P, KD, QC])
        y_ps = [ps(f"y{u}", [P, QC]) for u in range(2)]
        t_ps = [ps(f"t{u}", [P, QC]) for u in range(KD)]
        v_ps = [ps(f"v{u}", [P, QC]) for u in range(2)]
        (w_in, w_split, j_zero, v_ready, bias_done, stats_done, root_ready, root_done, normed, tposed, x_hi_done, x_lo_done,
         y_done, y_read, full_done, hi_done, lo_done, tq_rest, t_done, t_read, v_done, v_read, chunk_out, v_out, pool_lo, pack_turn) = kit.sems(
            "q", "w_in w_split j_zero v_ready bias_done stats_done root_ready root_done normed tposed x_hi_done x_lo_done "
            "y_done y_read full_done hi_done lo_done tq_rest t_done t_read v_done v_read chunk_out v_out pool_lo pack_turn")
        wt = lambda a, m, k, e0, n: a[:, (m * KD + k) * D + e0:(m * KD + k) * D + e0 + n]
        jt = lambda a, g: a[:, NW + g * P:NW + (g + 1) * P]
        N_W = 3 + 2 * KD + 2 + HEADS
        Q_HI, Q_LO, T_HI, T_LO, K_HI, K_LO, TK_HI, TK_LO = range(8)

        with nc.Block() as block:

            @block.sync
            def _(sp):
                for m, name in enumerate(("WqT", "WkT", "WvT")):
                    sp.dma_start(w_raw[:, m * KD * D:(m + 1) * KD * D].rearrange("p (k e) -> p k e", k=KD),
                                 w[name].rearrange("(k p) e -> p k e", p=P)).then_inc(w_in, 16)
                for m, name in enumerate(("bq", "bk")):
                    for k in range(KD):
                        sp.dma_start(bias[:, m, k:k + 1], w[name][k * P:(k + 1) * P].rearrange("(p o) -> p o", o=1)).then_inc(w_in, 16)
                sp.dma_start(bv[:], w["bv"].partition_broadcast(P)).then_inc(w_in, 16)
                sp.dma_start(lam[:], w["lam"].partition_broadcast(P)).then_inc(w_in, 16)
                sp.wait_ge(j_zero, 1)
                for h in range(HEADS):
                    r0 = h * HD % P
                    sp.dma_start(w_raw[r0:r0 + HD, NW + h * HD:NW + (h + 1) * HD], w["J"][h]).then_inc(w_in, 16)
                for sem, n in ((pool_lo, 6), (tq_rest, 2), (lo_done, 2), (t_read, 2), (full_done, 8), (chunk_out, 16), (v_out, 16)):
                    sp.sem_inc(sem, n)
                with nc.sync.Fori(0, BATCH) as b:
                    for half in range(2):
                        i = b * 2 + half
                        for g in range(KD):
                            sp.wait_ge(pool_lo, 6 + (i + 1) * 6 - (3 if g == 0 else 0))
                            sp.sem_inc(pack_turn, 1)
                            sp.wait_ge(lo_done, 2 + (i + 1) * 2 - (1 if g == 0 else 0))
                            sp.dma_start(packs.rearrange("a b (g p) c -> b g p a c", p=P)[bass.ds(b, 1), g, :, :, half * QC:(half + 1) * QC]
                                         .rearrange("o p a c -> (o p) a c"),
                                         pack[g][:].bitcast(F32)).then_inc(chunk_out, 16)
                        sp.wait_ge(v_read, (i + 1) * U + 2)
                        for g in range(NG):
                            sp.dma_start(v_dram.rearrange("(b g) t p c -> b g t p c", g=NG)
                                         [bass.ds(b, 1), g, half * U:(half + 1) * U, :, :].rearrange("o t p c -> p (o t) c"),
                                         vals[:, :, g * GH:(g + 1) * GH, :].rearrange("p u h c -> p u (h c)")).then_inc(v_out, 16)
                sp.wait_ge(chunk_out, 16 + 2 * BATCH * KD * 16)
                sp.wait_ge(v_out, 16 + 2 * BATCH * NG * 16)

            @block.gpsimd
            def _(pool):
                nc.gpsimd.memset(w_raw[:, NW:], 0.0).then_inc(j_zero, 1)
                nc.gpsimd.memset(vals[:], 0.0).then_inc(v_ready, 1)
                pool.wait_ge(v_ready, 1)
                nc.gpsimd.memset(vals[:, :, :, HD:HD + 1], 1.0).then_inc(v_ready, 1)
                with nc.gpsimd.Fori(0, 2 * BATCH) as i:
                    for g in range(KD):
                        for n, (name, hi, lo) in enumerate((("q", Q_HI, Q_LO), ("k", K_HI, K_LO), ("tk", TK_HI, TK_LO))):
                            pool.wait_ge(hi_done, i * 10 + g * 5 + (1, 3, 4)[n])
                            nc.gpsimd.tensor_tensor(pack[g][:, lo, :], full[name][g][:], pack[g][:, hi, :].bitcast(F32),
                                                    ALU.subtract).then_inc(pool_lo, 1)

            @block.vector
            def _(dve):
                link = chain(kit, dve, "dve_step")
                with nc.vector.Fori(0, NT // 4) as i:
                    for u in range(4):
                        t = i * 4 + u
                        nc.vector.bn_stats(stats[:].rearrange("p t s -> p (t s)")[:, bass.ds(t * 6, 6)],
                                           x[:, bass.ds(t * D, D)]).then_inc(stats_done, 1)
                dve.wait_ge(stats_done, NT)
                rstd_of(nc, link, mean[:], rstd[:], stats, [a[:] for a in tmp], root_ready, root_done)
                dve.wait_ge(w_in, N_W * 16)
                link(nc.vector.tensor_copy(w_hi[:], w_raw[:]))
                nc.vector.tensor_tensor(w_lo[:], w_raw[:], w_hi[:].bitcast(F32), ALU.subtract).then_inc(w_split, 1)
                nc.vector.tensor_scalar(bias[:, 2, :], bias[:, 0, :], 0.25, None, ALU.mult).then_inc(bias_done, 1)
                dve.wait_ge(v_ready, 2)
                dve.sem_inc(tposed, 1)
                with nc.vector.Fori(0, 2 * BATCH) as i:
                    dve.wait_ge(tposed, i + 1)
                    for u in range(U):
                        t = i * U + u
                        nc.vector.tensor_scalar(stage[u][:], x[:, bass.ds(t * D, D)], mean[:, bass.ds(t, 1)],
                                                rstd[:, bass.ds(t, 1)], ALU.subtract, ALU.mult).then_inc(normed, 1)
                    dve.wait_ge(x_hi_done, i + 1)
                    nc.vector.tensor_tensor(x_lo[:], tp[:], x_hi[:].bitcast(F32), ALU.subtract).then_inc(x_lo_done, 1)
                    dve.wait_ge(chunk_out, 16 + i * KD * 16)
                    for g in range(KD):
                        for n, (name, to) in enumerate((("q", pack[g][:, Q_HI, :]), ("tq", tq_hi[g][:]),
                                                        ("k", pack[g][:, K_HI, :]), ("tk", pack[g][:, TK_HI, :]))):
                            dve.wait_ge(full_done, 8 + i * 8 + g * 4 + n + 1)
                            nc.vector.tensor_copy(to, full[name][g][:]).then_inc(hi_done, 1)
                            if name == "tq":
                                dve.wait_ge(hi_done, i * 10 + g * 5 + 2)
                                nc.vector.tensor_tensor(tq_lo[g][:], full["tq"][g][:], tq_hi[g][:].bitcast(F32),
                                                        ALU.subtract).then_inc(tq_rest, 1)
                        dve.wait_ge(t_done, i * 2 + g + 1)
                        dve.wait_ge(lo_done, i * 2 + 2)
                        nc.vector.tensor_scalar(full["t"][g][:], t_ps[g][:], lam[:, 0:1], None, ALU.mult).then_inc(t_read, 1)
                        dve.wait_ge(t_read, i * 2 + g + 1 + 2)
                        nc.vector.tensor_copy(pack[g][:, T_HI, :], full["t"][g][:]).then_inc(hi_done, 1)
                        dve.wait_ge(hi_done, i * 10 + g * 5 + 5)
                        nc.vector.tensor_tensor(pack[g][:, T_LO, :], full["t"][g][:], pack[g][:, T_HI, :].bitcast(F32),
                                                ALU.subtract).then_inc(lo_done, 1)
                    dve.wait_ge(v_out, 16 + i * NG * 16)
                    for u in range(U):
                        dve.wait_ge(v_done, i * U + u + 1)
                        nc.vector.tensor_tensor(vals[:, u, :, 0:HD], v_ps[u % 2][:, 0:D].rearrange("p (h c) -> p h c", c=HD),
                                                bv[:].rearrange("p (h c) -> p h c", c=HD), ALU.add).then_inc(v_read, 1)

            @block.scalar
            def _(act):
                act.wait_ge(root_ready, 1)
                nc.scalar.activation(rstd[:], tmp[2][:], ACT.Sqrt).then_inc(root_done, 1)
                act.wait_ge(bias_done, 1)
                with nc.scalar.Fori(0, 2 * BATCH) as i:
                    act.wait_ge(tposed, i + 2)
                    nc.scalar.copy(x_hi[:], tp[:]).then_inc(x_hi_done, 1)
                    for g in range(KD):
                        for m in range(2):
                            n = g * 2 + m
                            names = (("q", "tq"), ("k", "tk"))[m]
                            act.wait_ge(y_done, i * 4 + n + 1)
                            act.wait_ge(pool_lo, i * 6 + 6)
                            act.wait_ge(tq_rest, i * 2 + 2)
                            if m == 0:
                                nc.scalar.activation(full["q"][g][:], y_ps[n % 2][:], ACT.Identity, bias=bias[:, 2, g:g + 1],
                                                     scale=0.25).then_inc(full_done, 1)
                            else:
                                nc.scalar.activation(full["k"][g][:], y_ps[n % 2][:], ACT.Identity,
                                                     bias=bias[:, 1, g:g + 1]).then_inc(full_done, 1)
                            nc.scalar.activation(full[names[1]][g][:], y_ps[n % 2][:], ACT.Tanh,
                                                 bias=bias[:, m, g:g + 1]).then_inc(full_done, 1)

            @block.tensor
            def _(pe):
                pe.wait_ge(w_split, 1)
                pe.sem_inc(x_lo_done, 1)
                pe.sem_inc(v_read, 2)

                def split_product(out, terms, last_sem):
                    for z, (a, b) in enumerate(terms):
                        last = nc.tensor.matmul(out, a, b, start=(z == 0), stop=(z == len(terms) - 1))
                    last.then_inc(last_sem, 1)

                with nc.tensor.Fori(0, 2 * BATCH) as i:
                    pe.wait_ge(x_lo_done, i + 1)
                    for u in range(U):
                        pe.wait_ge(normed, i * U + u + 1)
                        for k in range(KD):
                            last = nc.tensor.transpose(tp[:, k, u * P:(u + 1) * P], stage[u][:, k * P:(k + 1) * P], c["ident"][:])
                    last.then_inc(tposed, 1)
                    pe.wait_ge(x_lo_done, i + 2)

                    def q_or_k(g, m):
                        n = g * 2 + m
                        if n >= 2:
                            pe.wait_ge(full_done, 8 + i * 8 + (n - 1) * 2)
                        else:
                            pe.wait_ge(full_done, 8 + i * 8)
                        split_product(y_ps[n % 2][:], [(wt(a, m, k, g * P, P), b[:, k, :]) for k in range(KD)
                                                       for a, b in ((w_hi, x_hi), (w_hi, x_lo), (w_lo, x_hi))], y_done)

                    def tangents(g):
                        pe.wait_ge(tq_rest, 2 + i * 2 + g + 1)
                        pe.wait_ge(t_read, i * 2 + 2)
                        split_product(t_ps[g][:], [(jt(w_hi, g), tq_hi[g][:]), (jt(w_hi, g), tq_lo[g][:]),
                                                   (jt(w_lo, g), tq_hi[g][:])], t_done)

                    def values(u):
                        pe.wait_ge(v_read, i * U + u + 1)
                        split_product(v_ps[u % 2][:, 0:D], [(a[:, k, u * P:(u + 1) * P], wt(b, 2, k, 0, D)) for k in range(KD)
                                                            for a, b in ((x_hi, w_hi), (x_lo, w_hi), (x_hi, w_lo))], v_done)

                    q_or_k(0, 0)
                    q_or_k(0, 1)
                    tangents(0)
                    q_or_k(1, 0)
                    q_or_k(1, 1)
                    tangents(1)
                    for u in range(U):
                        values(u)


def attend(kit, c, packs, v_dram, o_dram, bo_dram, spare):
    nc, x = kit.nc, c["x"]
    GROUPS = BATCH * NG
    NB = 3
    def diagonal(k0):
        return [(k0, 0, 0, QC, 0), (k0 + 3, 7 * P, 3 * P, P, P), (k0 + 1, 4 * P, P, 3 * P, 0)], [(k0 + 2, 0, 2 * P, 2 * P, 0)]
    A0, B0 = diagonal(0)
    A1, B1 = diagonal(4)
    full_pair = lambda k0: [(k0, 0, 0, QC, 0), (k0 + 1, QC, 0, QC, 0)]
    STEPS = [(0, A0), (0, B0), (1, full_pair(0)), (1, full_pair(2)), (1, A1), (1, B1)]
    WIDTH = [1024, 256, 1024, 1024, 1024, 256]
    NS = len(STEPS)
    UNITS = [(qt, part) for qt in range(KT) for part in range(1 + (qt >= 4))]
    NU = len(UNITS)
    with ExitStack() as ctx:
        sb = lambda n, s, dt=F32: kit.sb(f"a_{n}", s, dt, ctx)
        ps = lambda n, s: kit.ps(f"a_{n}", s, ctx)
        qp = [sb(f"qp{u}", [PACK + 1, GH, SEQ], F32R) for u in range(NB)]
        kp = [sb(f"kp{u}", [PACK + 1, GH, SEQ], F32R) for u in range(NB)]
        vg = [sb(f"vg{u}", [P, KT, GH, HP]) for u in range(NB)]
        wts = [sb(f"wts{u}", [P, GH, 2 * QC]) for u in range(2)]
        parts = [sb(f"parts{u}", [P, KT, 2]) for u in range(2)]
        tops = [sb(f"tops{u}", [P, KT]) for u in range(2)]
        neg = [sb(f"neg{u}", [KT, P], F32R) for u in range(2)]
        o_sb, o_out = ([sb(f"{n}{u}", [P, QC]) for u in range(2)] for n in ("o_sb", "o_out"))
        inv = sb("inv", [P, QC])
        sums_of = sb("sums_of", [P, P])
        bo = sb("bo", [P, D])
        s_ps = [ps(f"s{u}", [P, 2 * QC]) for u in range(2)]
        m_ps = [ps(f"m{u}", [P, QC]) for u in range(2)]
        o_ps = ps("o", [P, QC])
        t_ps = ps("t", [P, QC])
        (made, bo_in, scored, weighed, mixed, maxed, max_read, topped, turned, negated, o_taken, summed, o_ready,
         inverted, out_turn, bo_added) = kit.sems(
            "a", "made bo_in scored weighed mixed maxed max_read topped turned negated o_taken summed o_ready "
            "inverted out_turn bo_added")
        loaded = kit.sems("a_loaded", "0 1 2")
        row_in = kit.sems("a_row_in", "0 1 2 3")
        stored = kit.sems("a_stored", "0 1")
        NL = 13
        MIX0, INV0, ORDY0 = 2, 1, 1
        m_b = lambda h, z: (h * NU + z) % 2
        TURNS = (8, 15, 20)
        SPREAD = 13

        def groups(eng, body, last):
            assert GROUPS % NB == 1
            with eng.Fori(0, GROUPS // NB) as i:
                for u in range(NB):
                    body(i, u, False)
            body(GROUPS // NB, 0, True)

        with nc.Block() as block:

            @block.sync
            def _(sp):
                sp.dma_start(bo[:], bo_dram.partition_broadcast(P)).then_inc(bo_in, 16)

                def load(gi, u):
                    for block_row, (qa, ka) in enumerate(((0, 4), (0, 5), (1, 4), (2, 6), (2, 7), (3, 6))):
                        for t, a in ((qp, qa), (kp, ka)):
                            sp.dma_start(t[u][block_row * HD:(block_row + 1) * HD, :, :].bitcast(F32),
                                         packs[a].rearrange("b (g j r) c -> (b g) r j c", g=NG, j=GH)[bass.ds(gi, 1), :, :, :]
                                         .rearrange("o r j c -> (o r) j c")).then_inc(loaded[u], 16)
                    sp.dma_start(vg[u][:].rearrange("p t h c -> p t (h c)"),
                                 v_dram[bass.ds(gi, 1), :, :, :].rearrange("o t p c -> p (o t) c")).then_inc(loaded[u], 16)

                def rows(gi, u):
                    for h in range(GH):
                        sp.wait_ge(negated, gi * GH + h + 1)
                        sp.dma_start(qp[u][PACK:PACK + 1, h, :].bitcast(F32), neg[h % 2][:].bitcast(F32)).then_inc(row_in[h], 16)

                def next_groups(g, u, more):
                    rows(g + 1, (u + 1) % NB)
                    if more:
                        sp.wait_ge(mixed, MIX0 + (g + 1) * NS)
                        load(g + NB, u)

                for g in range(NB):
                    load(g, g)
                rows(0, 0)
                FULL = (GROUPS - NB) // NB
                with nc.sync.Fori(0, FULL) as i:
                    for u in range(NB):
                        next_groups(i * NB + u, u, True)
                for g in range(FULL * NB, GROUPS - 1):
                    next_groups(g, g % NB, g + NB < GROUPS)

            @block.gpsimd
            def _(pool):
                link = chain(kit, pool, "pool_step")
                for u in range(NB):
                    link(nc.gpsimd.memset(kp[u][PACK:PACK + 1, :, :].bitcast(F32), 1.0))
                for u in range(2):
                    link(nc.gpsimd.memset(parts[u][:], -3e38))
                link(nc.gpsimd.memset(sums_of[:], 0.0))
                for h in range(GH):
                    cols = sums_of[:, h * HP:(h + 1) * HP]
                    link(nc.gpsimd.affine_select(out=cols, in_=cols, compare_op=ALU.not_equal, fill=1.0,
                                                 base=-(h * HP + HD), pattern=[[0, HP]], channel_multiplier=1))
                pool.sem_inc(made, 1)
                pool.wait_ge(bo_in, 16)
                xv = x[:].rearrange("p (t d) -> p t d", d=D)
                nc.gpsimd.tensor_tensor(xv, xv, bo[:].unsqueeze(1).to_broadcast([P, NT, D]), ALU.add).then_inc(bo_added, 1)

                def body(i, u, last):
                    g = i * NB + u
                    for ch in range(2):
                        pool.wait_ge(o_ready, ORDY0 + g * 2 + ch + 1)
                        pool.sem_inc(out_turn, 1)
                        nc.gpsimd.dma_start(o_dram.rearrange("g p c -> (g p) c")[bass.ds(g * P, P), ch * QC:(ch + 1) * QC],
                                            o_out[ch][:]).then_inc(stored[ch], 16)

                for ch in range(2):
                    nc.gpsimd.dma_start(spare[ch], sums_of[:, 0:16]).then_inc(stored[ch], 16)
                groups(nc.gpsimd, body, None)
                for ch in range(2):
                    pool.wait_ge(stored[ch], 16 + GROUPS * 16)

            @block.vector
            def _(dve):
                dve.wait_ge(made, 1)
                dve.sem_inc(turned, 2)
                dve.sem_inc(inverted, INV0)
                dve.sem_inc(o_ready, ORDY0)

                def maxima(n, h, units):
                    for z in units:
                        qt, part = UNITS[z]
                        m = n * GH * NU + h * NU + z
                        dve.wait_ge(maxed, m + 1)
                        width = (qt + 1) * P - part * QC if part or qt < 4 else QC
                        ins = nc.vector.reduce_max(parts[h % 2][:, qt, part:part + 1], m_ps[m_b(h, z)][:, 0:width], AX.X)
                        ins.then_inc(max_read, 1)
                        if z == NU - 1:
                            dve.wait_ge(max_read, m + 1 + 2)
                            dve.wait_ge(turned, n * GH + h + 1)
                            nc.vector.reduce_max(tops[h % 2][:], parts[h % 2][:], AX.X).then_inc(topped, 1)
                            dve.wait_ge(topped, n * GH + h + 1)

                def normalise(g, ch):
                    dve.wait_ge(summed, g * 2 + ch + 1)
                    dve.wait_ge(o_ready, ORDY0 + g * 2 + ch)
                    nc.vector.reciprocal(inv[:], t_ps[:]).then_inc(inverted, 1)
                    dve.wait_ge(inverted, INV0 + g * 2 + ch + 1)
                    dve.wait_ge(stored[ch], 16 + g * 16)
                    nc.vector.tensor_tensor(o_out[ch][:], o_sb[ch][:], inv[:], ALU.mult).then_inc(o_ready, 1)

                def body(i, u, last):
                    g = i * NB + u
                    for s in range(NS):
                        for j in range(GH):
                            q = s * GH + j
                            if not last:
                                maxima(g + 1, q // 6, (2 * (q % 6), 2 * (q % 6) + 1))
                            if q == SPREAD:
                                normalise(g, 0)
                    normalise(g, 1)

                for h in range(GH):
                    maxima(0, h, range(NU))
                groups(nc.vector, body, None)

            @block.scalar
            def _(act):
                act.sem_inc(mixed, 2)

                def negate(n, h):
                    act.wait_ge(turned, n * GH + h + 1 + 2)
                    if h >= 2:
                        act.wait_ge(row_in[h - 2], (n + 1) * 16)
                    else:
                        act.wait_ge(row_in[h + 2], n * 16)
                    nc.scalar.activation(neg[h % 2][:], t_ps[0:KT, 0:P], ACT.Copy, scale=-1.0).then_inc(negated, 1)

                def take(g, ch):
                    act.wait_ge(mixed, 2 + g * NS + (2, 6)[ch])
                    act.wait_ge(o_ready, ORDY0 + g * 2 + ch)
                    nc.scalar.copy(o_sb[ch][:], o_ps[:]).then_inc(o_taken, 1)

                def body(i, u, last):
                    g = i * NB + u
                    for s in range(NS):
                        for j in range(GH):
                            q = s * GH + j
                            act.wait_ge(scored, g * NS * GH + q + 1)
                            if j == 0:
                                act.wait_ge(mixed, g * NS + s + 1)
                            w = WIDTH[s]
                            nc.scalar.activation(wts[(u * NS + s) % 2][:, j, 0:w], s_ps[q % 2][:, 0:w], ACT.Exp).then_inc(weighed, 1)
                            if s == 2 and j == 3:
                                take(g, 0)
                            if not last and q in TURNS:
                                negate(g + 1, TURNS.index(q))
                    take(g, 1)
                    if not last:
                        negate(g + 1, 3)

                for h in range(GH):
                    negate(0, h)
                groups(nc.scalar, body, None)

            @block.tensor
            def _(pe):
                pe.wait_ge(made, 1)
                pe.sem_inc(weighed, 2)
                pe.sem_inc(max_read, 2)
                pe.sem_inc(o_taken, 1)

                def max_unit(n, ub, h, z):
                    qt, part = UNITS[z]
                    m = n * GH * NU + h * NU + z
                    pe.wait_ge(max_read, m + 1)
                    bank = m_ps[m_b(h, z)]
                    width = (qt + 1) * P - part * QC if part or qt < 4 else QC
                    stream = max(width, 2 * P)
                    diag = (qt + 1) * P - part * QC - P
                    masked = 0 <= diag < QC
                    last = nc.tensor.matmul(bank[:, 0:stream], qp[ub][0:PACK, h, qt * P:(qt + 1) * P],
                                            kp[ub][0:PACK, h, part * QC:part * QC + stream], start=True, stop=not masked)
                    if masked:
                        last = nc.tensor.matmul(bank[:, diag:diag + P], c["ident_bf"][:], c["mask_qk"][:], start=False, stop=True)
                    last.then_inc(maxed, 1)

                def turn(n, h, sums):
                    pe.wait_ge(topped, n * GH + h + 1)
                    pe.wait_ge(negated, n * GH + h)
                    pe.wait_ge(inverted, INV0 + sums)
                    nc.tensor.transpose(t_ps[0:KT, 0:P], tops[h % 2][:], c["ident"][:]).then_inc(turned, 1)

                def spread(g, ch, heads):
                    pe.wait_ge(o_taken, 1 + g * 2 + ch + 1)
                    pe.wait_ge(negated, heads)
                    pe.wait_ge(inverted, INV0 + g * 2 + ch)
                    nc.tensor.matmul(t_ps[:], sums_of[:], o_sb[ch][:], start=True, stop=True).then_inc(summed, 1)

                def score(g, u, s, j):
                    ch, blocks = STEPS[s]
                    q = s * GH + j
                    if s == 0:
                        pe.wait_ge(row_in[j], (g + 1) * 16)
                    pe.wait_ge(weighed, g * NS * GH + q + 1)
                    for kt, col, q0, w, lead in blocks:
                        at = ch * QC + q0
                        last = nc.tensor.matmul(s_ps[q % 2][:, col - lead:col + w], kp[u][:, j, kt * P:(kt + 1) * P],
                                                qp[u][:, j, at - lead:at + w], start=True, stop=kt // 4 != ch)
                        if kt // 4 == ch:
                            last = nc.tensor.matmul(s_ps[q % 2][:, col:col + P], c["ident_bf"][:], c["mask_kq"][:],
                                                    start=False, stop=True)
                    last.then_inc(scored, 1)

                def mix(g, u, s, blocks, done):
                    ch = STEPS[s][0]
                    for kt, col, q0, w, lead in blocks:
                        if kt == 0:
                            pe.wait_ge(o_taken, 1 + g * 2 + ch)
                        for j in range(GH):
                            pe.wait_ge(weighed, 2 + g * NS * GH + s * GH + j + 1)
                            last = nc.tensor.matmul(o_ps[j * HP:(j + 1) * HP, q0:q0 + w], vg[u][:, kt, j, :],
                                                    wts[(u * NS + s) % 2][:, j, col:col + w], start=(kt == 0),
                                                    stop=(kt == ch * 4 + 2), skip_group_check=True)
                    if done:
                        last.then_inc(mixed, 1)

                def body(i, u, last):
                    g = i * NB + u
                    if not last:
                        pe.wait_ge(loaded[(u + 1) % NB], (i + (u + 1) // NB + 1) * NL * 16)
                    for s in range(NS):
                        for j in range(GH):
                            q = s * GH + j
                            score(g, u, s, j)
                            if not last:
                                for z in (2 * (q % 6), 2 * (q % 6) + 1):
                                    max_unit(g + 1, (u + 1) % NB, q // 6, z)
                            if s and j % 2:
                                blocks = STEPS[s - 1][1]
                                cut = (len(blocks) + 1) // 2
                                part = blocks[:cut] if j == 1 else blocks[cut:]
                                if len(blocks) == 1:
                                    part = blocks if j == 3 else []
                                if part:
                                    mix(g, u, s - 1, part, j == 3)
                            if q == SPREAD:
                                spread(g, 0, (g + 1) * GH + (0 if last else 1))
                            if not last and q in TURNS:
                                turn(g + 1, TURNS.index(q), g * 2 + (q > SPREAD))
                    mix(g, u, NS - 1, STEPS[NS - 1][1], True)
                    spread(g, 1, (g + 1) * GH + (0 if last else 3))
                    if not last:
                        turn(g + 1, 3, g * 2 + 2)

                pe.wait_ge(loaded[0], NL * 16)
                for h in range(GH):
                    for z in range(NU):
                        max_unit(0, 0, h, z)
                    turn(0, h, 0)
                groups(nc.tensor, body, None)


def project_out(kit, c, o_dram, wo_dram):
    nc, x = kit.nc, c["x"]
    U = QC // P
    with ExitStack() as ctx:
        wo = kit.sb("p_wo", [P, NG, D], F32, ctx)
        o = [kit.sb(f"p_o{u}", [P, NG, QC], F32, ctx) for u in range(2)]
        y_ps = [kit.ps(f"p_y{u}", [P, QC], ctx) for u in range(2)]
        wo_zero, wo_in, y_done, y_read = kit.sems("p", "wo_zero wo_in y_done y_read")
        o_in = kit.sems("p_o_in", "0 1")
        with nc.Block() as block:

            @block.sync
            def _(sp):
                sp.wait_ge(wo_zero, 1)
                for j in range(GH):
                    sp.dma_start(wo[j * HP:j * HP + HD, :, :],
                                 wo_dram.rearrange("(g j r) d -> r j g d", g=NG, j=GH)[:, j, :, :]).then_inc(wo_in, 16)
                sp.sem_inc(y_read, 2 * U)
                with nc.sync.Fori(0, BATCH) as b:
                    for half in range(2):
                        i = b * 2 + half
                        sp.wait_ge(y_read, (i + 1) * U)
                        sp.dma_start(o[half][:], o_dram[bass.ds(b * NG, NG), :, half * QC:(half + 1) * QC]
                                     .rearrange("g p c -> p g c")).then_inc(o_in[half], 16)

            @block.vector
            def _(dve):
                nc.vector.memset(wo[:], 0.0).then_inc(wo_zero, 1)
                with nc.vector.Fori(0, 2 * BATCH) as i:
                    for u in range(U):
                        t = i * U + u
                        dve.wait_ge(y_done, t + 1)
                        xt = x[:, bass.ds(t * D, D)]
                        nc.vector.tensor_tensor(xt, y_ps[u % 2][:, 0:D], xt, ALU.add).then_inc(y_read, 1)
                dve.wait_ge(y_read, NT + 2 * U)

            @block.tensor
            def _(pe):
                pe.wait_ge(wo_in, GH * 16)
                with nc.tensor.Fori(0, BATCH) as b:
                    for half in range(2):
                        pe.wait_ge(o_in[half], (b + 1) * 16)
                        for u in range(U):
                            t = (b * 2 + half) * U + u
                            pe.wait_ge(y_read, t - 1 + 2 * U)
                            for g in range(NG):
                                last = nc.tensor.matmul(y_ps[u % 2][:, 0:D], o[half][:, g, u * P:(u + 1) * P], wo[:, g, :],
                                                        start=(g == 0), stop=(g == NG - 1))
                            last.then_inc(y_done, 1)


def program(nc, x, w, out):
    with ExitStack() as ctx:
        kit = Kit(nc, ctx)
        c = constants(kit)
        gates = kit.sb("gates", [P, TOPK, NT])
        scratch = lambda name, shape: nc.dram_tensor(name, shape, F32, kind="Internal").ap()
        disp = [scratch(f"disp{r}", (EXP * CAP, ROW)) for r in range(2)]
        ydram = scratch("choice_rows", (TOPK * TOK, D))
        spare = scratch("spare", (4, P, 16))
        packs = scratch("packs", (8, BATCH, D, SEQ))
        v_dram = scratch("values", (BATCH * NG, KT, P, GH * HP))
        o_dram = scratch("attended", (BATCH * NG, P, SEQ))
        build_constants(kit, c, x)

        def mixture(r, to):
            route(kit, c, r, w["Wg"], disp[r], ydram, gates)
            experts(kit, c, r, w["W_in"], w["W_out"], disp[r], ydram, spare)
            combine(kit, c, r, ydram, gates, to)

        mixture(0, None)
        project(kit, c, w, packs, v_dram)
        attend(kit, c, packs, v_dram, o_dram, w["bo"], spare)
        project_out(kit, c, o_dram, w["WoT"])
        mixture(1, out)


_NAMES = ["Wg", "W_in", "W_out", "WqT", "WkT", "WvT", "WoT", "bq", "bk", "bv", "bo", "J", "lam"]


def kernel(**inputs):
    import numpy as np
    import concourse.bacc as bacc
    from concourse.bass_utils import run_bass_kernel_spmd

    a = lambda n: np.asarray(inputs[n])
    arrays = {"x": a("L0_attn_x").reshape(TOK, D), "Wg": a("L0_ffn_Wg"), "W_in": a("L0_ffn_W_in"), "W_out": a("L0_ffn_W_out"),
              "J": a("L0_attn_J_attn"), "lam": a("L0_attn_lambda_attn").reshape(1)}
    for n in ("q", "k", "v", "o"):
        arrays[f"W{n}T"] = a(f"L0_attn_W{n}").T
        arrays[f"b{n}"] = a(f"L0_attn_b{n}")
    arrays = {n: np.ascontiguousarray(v) for n, v in arrays.items()}
    nc = bacc.Bacc("TRN2", target_bir_lowering=False, num_devices=1)
    dram = {n: nc.dram_tensor(f"in_{n}", v.shape, mybir.dt.from_np(v.dtype), kind="ExternalInput").ap() for n, v in arrays.items()}
    out = nc.dram_tensor("out", (TOK, D), F32, kind="ExternalOutput").ap()
    program(nc, dram["x"], {n: dram[n] for n in _NAMES}, out)
    got = run_bass_kernel_spmd(nc, [{f"in_{n}": v for n, v in arrays.items()}], core_ids=[0])
    return got.results[0]["out"].reshape(BATCH, SEQ, D)
```

```python
from contextlib import ExitStack

import concourse.bass as bass
from concourse import mybir

F32 = mybir.dt.float32
F32R = mybir.dt.float32r
BF16 = mybir.dt.bfloat16
I32 = mybir.dt.int32
ALU = mybir.AluOpType
ACT = mybir.ActivationFunctionType
AX = mybir.AxisListType

P = 128
BATCH, SEQ, D = 4, 1024, 256
TOK = BATCH * SEQ
NT = TOK // P
KD = D // P
EXP, TOPK, FF = 8, 2, 512
CAP = 1280
ST = CAP // P
KF = FF // P
ROW = D + 1
NOWHERE = 1 << 20
LN_EPS = 1e-5
CHUNKS = [(0, 512), (512, 512), (1024, 256)]


class Kit:

    def __init__(self, nc, ctx):
        self.nc, self.ctx = nc, ctx
        self.kept = {}
        self.steps, self.step_sems = {}, {}

    def step_sem(self, name):
        if name not in self.step_sems:
            self.step_sems[name] = self.sem(name)
        return self.step_sems[name]

    def part(self, eng):
        eng.sem_inc(self.step_sem("parted"), 1)

    def sb(self, name, shape, dt=F32, ctx=None):
        return (ctx or self.ctx).enter_context(self.nc.sbuf_tensor(name, shape, dt))

    def ps(self, name, shape, ctx=None, dt=F32):
        return (ctx or self.ctx).enter_context(self.nc.psum_tensor(f"{name}_psum", shape, dt))

    def sems_again(self, prefix, names):
        if prefix not in self.kept:
            self.kept[prefix] = self.sems(prefix, names)
        else:
            with self.nc.Block() as block:

                @block.sync
                def _(sp):
                    for sem in self.kept[prefix]:
                        sp.sem_clear(sem)

        return self.kept[prefix]

    def sem(self, name):
        return self.ctx.enter_context(self.nc.semaphore(name))

    def sems(self, prefix, names):
        return [self.sem(f"{prefix}_{n}") for n in names.split()]


def chain(kit, eng, sem):

    def link(ins):
        kit.steps[sem] = kit.steps.get(sem, 0) + 1
        ins.then_inc(kit.step_sem(sem), 1)
        eng.wait_ge(kit.step_sem(sem), kit.steps[sem])

    return link


def constants(kit):
    nc = kit.nc
    c = {
        "ident": kit.sb("ident", [P, P]),
        "ident_bf": kit.sb("ident_bf", [P, P], BF16),
        "before_bf": kit.sb("before_bf", [P, P], BF16),
        "ones_bf": kit.sb("ones_bf", [P, P], BF16),
        "mask": kit.sb("mask", [P, QC]),
        "rank": kit.sb("rank", [P, EXP]),
        "x": kit.sb("x_res", [P, NT * D]),
    }
    return c


MASKED = -1e38
HEADS, HD = 16, 16
GH = 4
NG = HEADS // GH
HP = 32
PACK = 6 * HD
KT = SEQ // P
QC = 512


def build_constants(kit, c, x_dram):
    nc = kit.nc
    x_in, = kit.sems("const", "x_in")
    rank_i = kit.sb("rank_i", [P, EXP], I32)
    with nc.Block() as block:

        @block.sync
        def _(sp):
            xv = x_dram.rearrange("(t p) d -> p t d", p=P)
            for q in range(4):
                n = NT // 4
                sp.dma_start(c["x"][:, q * n * D:(q + 1) * n * D].rearrange("p (t d) -> p t d", d=D),
                             xv[:, q * n:(q + 1) * n, :]).then_inc(x_in, 16)
            sp.wait_ge(x_in, 64)

        @block.gpsimd
        def _(pool):
            link = chain(kit, pool, "pool_step")
            for name, v in (("ident", 0.0), ("ident_bf", 0.0), ("before_bf", 1.0), ("ones_bf", 1.0),
                            ("mask", 0.0)):
                link(nc.gpsimd.memset(c[name][:], v))
            for name in ("ident", "ident_bf"):
                link(nc.gpsimd.affine_select(out=c[name][:], in_=c[name][:], compare_op=ALU.not_equal, fill=1.0,
                                             base=0, pattern=[[-1, P]], channel_multiplier=1))
            link(nc.gpsimd.affine_select(out=c["before_bf"][:], in_=c["before_bf"][:], compare_op=ALU.is_ge, fill=0.0,
                                         base=-1, pattern=[[1, P]], channel_multiplier=-1))
            link(nc.gpsimd.affine_select(out=c["mask"][:, QC - P:], in_=c["mask"][:, QC - P:], compare_op=ALU.is_ge,
                                         fill=MASKED, base=0, pattern=[[-1, P]], channel_multiplier=1))
            link(nc.gpsimd.iota(rank_i[:], pattern=[[-1, EXP]], base=EXP, channel_multiplier=0))
            link(nc.gpsimd.tensor_copy(c["rank"][:], rank_i[:]))


def rstd_of(nc, link, mean, rstd, stats, tmp, root_ready, act_ready):
    me, qe, mo, qo = stats[:, :, 1], stats[:, :, 2], stats[:, :, 4], stats[:, :, 5]
    a, b, ve = tmp
    link(nc.vector.tensor_tensor(mean, me, mo, ALU.add))
    link(nc.vector.tensor_scalar(mean, mean, 0.5, None, ALU.mult))
    link(nc.vector.tensor_tensor(a, me, mo, ALU.subtract))
    link(nc.vector.tensor_tensor(a, a, a, ALU.mult))
    link(nc.vector.tensor_tensor(b, qe, qo, ALU.add))
    link(nc.vector.tensor_scalar(b, b, 1.0 / D, LN_EPS, ALU.mult, ALU.add))
    nc.vector.scalar_tensor_tensor(ve, a, 0.25, b, ALU.mult, ALU.add).then_inc(root_ready, 1)
    nc.vector.wait_ge(act_ready, 1)
    link(nc.vector.reciprocal(a, rstd))
    link(nc.vector.tensor_tensor(b, a, a, ALU.mult))
    link(nc.vector.tensor_tensor(b, b, ve, ALU.mult))
    link(nc.vector.tensor_scalar(b, b, -0.5, 1.5, ALU.mult, ALU.add))
    link(nc.vector.tensor_tensor(rstd, a, b, ALU.mult))


NIN, NOUT = KD * 2 * FF, KF * D
W_PARTS = [(z * NIN // 2, (z + 1) * NIN // 2) for z in range(2)] + [(NIN, NIN + NOUT)]


def expert_weights(kit, ctx, r):
    sb = lambda n, dt=F32: kit.sb(f"e{r}_{n}", [P, NIN + NOUT], dt, ctx)
    return {"raw": sb("w_raw"), "hi": [sb(f"w_hi{u}", F32R) for u in range(2)], "lo": [sb(f"w_lo{u}", F32R) for u in range(2)]}


def load_weights(eng, weights, w_in_dram, w_out_dram, e, sem):
    eng.dma_start(weights["raw"][:, 0:NIN].rearrange("p (k f) -> p k f", k=KD),
                  w_in_dram.rearrange("e (k p) f -> p (e k) f", p=P)[:, bass.ds(e * KD, KD), :]).then_inc(sem, 16)
    eng.dma_start(weights["raw"][:, NIN:].rearrange("p (k d) -> p k d", k=KF),
                  w_out_dram.rearrange("e (k p) d -> p (e k) d", p=P)[:, bass.ds(e * KF, KF), :]).then_inc(sem, 16)


def route(kit, c, r, wg_dram, w_in_dram, w_out_dram, disp, ydram, gates, weights):
    nc, x = kit.nc, c["x"]
    U = 4
    with ExitStack() as ctx:
        sb = lambda n, s, dt=F32: kit.sb(f"r{r}_{n}", s, dt, ctx)
        ps = lambda n, s: kit.ps(f"r{r}_{n}", s, ctx)
        wg = sb("wg", [P, KD, EXP])
        blank = sb("blank", [P, ST * ROW])
        stats = sb("stats", [P, NT, 6])
        mean, rstd = sb("mean", [P, NT]), sb("rstd", [P, NT])
        tmp = [sb(f"tmp{i}", [P, NT]) for i in range(3)]
        stage = [sb(f"stage{u}", [P, D]) for u in range(U)]
        rows = sb("rows", [P, NT * ROW])
        rows3 = rows[:].rearrange("p (t c) -> p t c", c=ROW)
        xnT = [sb(f"xnT{u}", [P, KD, P]) for u in range(2)]
        logits = sb("logits", [P, NT * EXP])
        lg = logits[:].rearrange("p (t e) -> p t e", e=EXP)
        prob = sb("prob", [P, NT, EXP])
        pick = sb("pick", [P, NT, EXP])
        hot = sb("hot", [P, TOPK, NT, EXP])
        hot_bf = sb("hot_bf", [P, TOPK * NT * EXP], BF16)
        cum = sb("cum", [P, TOPK * NT * EXP])
        ahead = sb("ahead", [P, TOPK * NT * EXP])
        one64 = sb("one64", [P, TOPK * NT])
        best, rk = sb("best", [P, TOPK, NT]), sb("rk", [P, TOPK, NT])
        slot, keep, dest = (sb(n, [P, TOPK, NT]) for n in ("slot", "keep", "dest"))
        dest_i = sb("dest_i", [P, TOPK * NT], I32)
        id_i = sb("id_i", [P, NT], I32)
        den = sb("den", [P, NT])
        tp = [ps(f"tp{u}", [P, KD, P]) for u in range(2)]
        lg_ps = [ps(f"lg{u}", [P, 512]) for u in range(2)]
        within_ps = ps("within", [P, TOPK * NT * EXP])
        total_ps = ps("total", [P, TOPK * NT * EXP])

        (wg_in, blank_ready, filled, stats_done, root_ready, root_done, normed, row_kept,
         tposed, xnT_ready, logits_done, lg_free, centred, powered, hot_ready, counted,
         ids_ready, routed, ids_moved, w_loaded, w_split, w_rest) = kit.sems_again(
            "route", "wg_in blank_ready filled stats_done root_ready root_done normed row_kept "
            "tposed xnT_ready logits_done lg_free centred powered hot_ready counted "
            "ids_ready routed ids_moved w_loaded w_split w_rest")
        sent0, sent1 = kit.sems(f"r{r}_sent", "0 1")

        with nc.Block() as block:

            @block.sync
            def _(sp):
                sp.dma_start(wg[:], wg_dram.rearrange("(k p) e -> p k e", p=P)).then_inc(wg_in, 16)
                load_weights(nc.sync, weights, w_in_dram, w_out_dram, 0, w_loaded)
                sp.wait_ge(blank_ready, 2)
                n = 0
                for e in range(EXP):
                    sp.dma_start(disp[e * CAP:(e + 1) * CAP, :].rearrange("(p j) c -> p (j c)", p=P),
                                 blank[:]).then_inc(filled, 16)
                    n += 1
                if r == 0:
                    zero = blank[:].rearrange("p (j c) -> p j c", c=ROW)[:, 0:8, 0:D]
                    for q in range(TOPK * NT // 8):
                        sp.dma_start(ydram[q * 8 * P:(q + 1) * 8 * P, :].rearrange("(p j) c -> p j c", p=P),
                                     zero).then_inc(filled, 16)
                        n += 1
                sp.wait_ge(filled, 16 * n)

            @block.gpsimd
            def _(pool):
                nc.gpsimd.memset(blank[:], 0.0).then_inc(blank_ready, 1)
                pool.wait_ge(blank_ready, 1)
                nc.gpsimd.memset(blank[:].rearrange("p (j c) -> p j c", c=ROW)[:, :, D].bitcast(I32),
                                 NOWHERE).then_inc(blank_ready, 1)
                nc.gpsimd.iota(id_i[:], pattern=[[P, NT]], base=0, channel_multiplier=1).then_inc(ids_ready, 1)
                pool.wait_ge(routed, 1)
                pool.wait_ge(row_kept, NT + U)
                pool.wait_ge(filled, 16 * (EXP + (8 if r == 0 else 0)))
                for k, sent in enumerate((sent0, sent1)):
                    if k:
                        pool.wait_ge(ids_moved, 1)
                    for t in range(NT):
                        nc.gpsimd.indirect_dma_start(
                            disp, bass.IndirectOffsetOnAxis(ap=dest_i[:, k * NT + t:k * NT + t + 1], axis=0),
                            rows3[:, t, :], None, bounds_check=EXP * CAP - 1, oob_is_err=False).then_inc(sent, 16)
                pool.wait_ge(sent1, 16 * NT)

            @block.vector
            def _(dve):
                link = chain(kit, dve, "dve_step")
                with nc.vector.Fori(0, NT // U) as i:
                    for u in range(U):
                        t = i * U + u
                        nc.vector.bn_stats(stats[:].rearrange("p t s -> p (t s)")[:, bass.ds(t * 6, 6)],
                                           x[:, bass.ds(t * D, D)]).then_inc(stats_done, 1)
                dve.wait_ge(stats_done, NT)
                rstd_of(nc, link, mean[:], rstd[:], stats, [a[:] for a in tmp], root_ready, root_done)
                dve.sem_inc(tposed, U)
                dve.sem_inc(row_kept, U)
                with nc.vector.Fori(0, NT // U) as i:
                    def norm(u):
                        t = i * U + u
                        dve.wait_ge(tposed, t + 1)
                        dve.wait_ge(row_kept, t + 1)
                        nc.vector.tensor_scalar(stage[u][:], x[:, bass.ds(t * D, D)], mean[:, bass.ds(t, 1)],
                                                rstd[:, bass.ds(t, 1)], ALU.subtract, ALU.mult).then_inc(normed, 1)
                    def keep_logits(u):
                        t = i * U + u
                        dve.wait_ge(logits_done, t + 3)
                        nc.vector.tensor_copy(logits[:, bass.ds(t * EXP, EXP)], lg_ps[u % 2][:, 0:EXP]).then_inc(lg_free, 1)

                    for u in range(U + 2):
                        if u < U:
                            norm(u)
                        if u >= 2:
                            keep_logits(u - 2)
                dve.wait_ge(lg_free, NT + 2)
                wide = lambda a: a.unsqueeze(2).to_broadcast([P, NT, EXP])
                link(nc.vector.reduce_max(den[:], lg, AX.X))
                nc.vector.tensor_tensor(prob[:], lg, wide(den[:]), ALU.subtract).then_inc(centred, 1)
                dve.wait_ge(powered, 1)
                link(nc.vector.reduce_sum(den[:], prob[:], AX.X))
                link(nc.vector.reciprocal(den[:], den[:]))
                link(nc.vector.tensor_tensor(prob[:], prob[:], wide(den[:]), ALU.mult))
                rank = c["rank"][:].unsqueeze(1).to_broadcast([P, NT, EXP])
                for k in range(TOPK):
                    link(nc.vector.reduce_max(best[:, k, :], prob[:], AX.X))
                    link(nc.vector.tensor_tensor(pick[:], prob[:], wide(best[:, k, :]), ALU.is_ge))
                    link(nc.vector.tensor_tensor(pick[:], pick[:], rank, ALU.mult))
                    link(nc.vector.reduce_max(rk[:, k, :], pick[:], AX.X))
                    link(nc.vector.tensor_tensor(hot[:, k, :, :], rank, wide(rk[:, k, :]), ALU.is_equal))
                    if k == 0:
                        link(nc.vector.scalar_tensor_tensor(prob[:], hot[:, 0, :, :], -2.0, prob[:], ALU.mult, ALU.add))
                hot_flat = hot[:].rearrange("p k t e -> p (k t e)")
                nc.vector.tensor_copy(hot_bf[:], hot_flat).then_inc(hot_ready, 1)
                link(nc.vector.memset(one64[:], 1.0))
                dve.wait_ge(counted, 1)
                link(nc.vector.tensor_copy(ahead[:], total_ps[:]))
                for e in range(EXP):
                    by = lambda a: a.rearrange("p (s e) -> p s e", e=EXP)[:, :, e]
                    link(nc.vector.tensor_tensor_scan(by(cum[:]), one64[:], by(ahead[:]), 0.0, ALU.mult, ALU.add))
                link(nc.vector.tensor_tensor(cum[:], cum[:], ahead[:], ALU.subtract))
                link(nc.vector.tensor_tensor(cum[:], cum[:], within_ps[:], ALU.add))
                link(nc.vector.tensor_tensor(cum[:], cum[:], hot_flat, ALU.mult))
                link(nc.vector.reduce_sum(slot[:].rearrange("p k t -> p (k t)"),
                                          cum[:].rearrange("p (s e) -> p s e", e=EXP), AX.X))
                link(nc.vector.tensor_scalar(keep[:], slot[:], float(CAP), None, ALU.is_lt))
                link(nc.vector.tensor_scalar(dest[:], rk[:], -float(CAP), float(EXP * CAP + NOWHERE), ALU.mult, ALU.add))
                link(nc.vector.tensor_tensor(dest[:], dest[:], slot[:], ALU.add))
                link(nc.vector.scalar_tensor_tensor(dest[:], keep[:], -float(NOWHERE), dest[:], ALU.mult, ALU.add))
                link(nc.vector.tensor_copy(dest_i[:], dest[:].rearrange("p k t -> p (k t)")))
                dve.wait_ge(ids_ready, 1)
                ids = rows3[:, :, D].bitcast(I32)
                nc.vector.tensor_copy(ids, id_i[:]).then_inc(routed, 1)
                link(nc.vector.tensor_tensor(best[:], best[:], keep[:], ALU.mult))
                link(nc.vector.tensor_tensor(den[:], best[:, 0, :], best[:, 1, :], ALU.add))
                link(nc.vector.tensor_scalar(den[:], den[:], 1e-9, None, ALU.max))
                link(nc.vector.reciprocal(den[:], den[:]))
                link(nc.vector.tensor_scalar(den[:], den[:], 0.5, None, ALU.mult))
                for k in range(TOPK):
                    link(nc.vector.tensor_tensor(gates[:, k, :], best[:, k, :], den[:], ALU.mult))
                dve.wait_ge(w_split, 1)
                nc.vector.tensor_tensor(weights["lo"][0][:], weights["raw"][:], weights["hi"][0][:].bitcast(F32),
                                        ALU.subtract).then_inc(w_rest, 1)
                dve.wait_ge(sent0, 16 * NT)
                nc.vector.tensor_scalar(ids, ids, TOK, None, ALU.add).then_inc(ids_moved, 1)

            @block.scalar
            def _(act):
                act.wait_ge(root_ready, 1)
                nc.scalar.activation(rstd[:], tmp[2][:], ACT.Sqrt).then_inc(root_done, 1)
                act.sem_inc(logits_done, 2)
                with nc.scalar.Fori(0, NT // U) as i:
                    for u in range(U):
                        t = i * U + u
                        act.wait_ge(tposed, t + 1 + U)
                        act.wait_ge(logits_done, t + 1)
                        nc.scalar.copy(xnT[u % 2][:], tp[u % 2][:]).then_inc(xnT_ready, 1)
                        nc.scalar.copy(rows[:, bass.ds(t * ROW, D)], stage[u][:]).then_inc(row_kept, 1)
                act.wait_ge(centred, 1)
                nc.scalar.activation(prob[:], prob[:], ACT.Exp).then_inc(powered, 1)
                act.wait_ge(w_loaded, 32)
                nc.scalar.copy(weights["hi"][0][:], weights["raw"][:]).then_inc(w_split, 1)

            @block.tensor
            def _(pe):
                pe.wait_ge(wg_in, 16)
                pe.sem_inc(lg_free, 2)
                pe.sem_inc(xnT_ready, 2)

                def transposes(t, u):
                    pe.wait_ge(normed, t + 1)
                    pe.wait_ge(xnT_ready, t + 1)
                    for k in range(KD):
                        last = nc.tensor.transpose(tp[u % 2][:, k, :], stage[u][:, k * P:(k + 1) * P], c["ident"][:])
                    last.then_inc(tposed, 1)

                def project(t, u):
                    pe.wait_ge(xnT_ready, t + 3)
                    pe.wait_ge(lg_free, t + 1)
                    for k in range(KD):
                        last = nc.tensor.matmul(lg_ps[u % 2][:, 0:EXP], xnT[u % 2][:, k, :], wg[:, k, :],
                                                start=(k == 0), stop=(k == KD - 1))
                    last.then_inc(logits_done, 1)

                with nc.tensor.Fori(0, NT // U) as i:
                    for u in range(U):
                        transposes(i * U + u, u)
                        if u:
                            project(i * U + u - 1, u - 1)
                    project(i * U + U - 1, U - 1)
                pe.wait_ge(hot_ready, 1)
                nc.tensor.matmul(within_ps[:], c["before_bf"][:], hot_bf[:], start=True, stop=True)
                nc.tensor.matmul(total_ps[:], c["ones_bf"][:], hot_bf[:], start=True, stop=True).then_inc(counted, 1)


def experts(kit, c, r, w_in_dram, w_out_dram, disp, ydram, spare, weights):
    nc = kit.nc
    with ExitStack() as ctx:
        sb = lambda n, s, dt=F32: kit.sb(f"e{r}_{n}", s, dt, ctx)
        ps = lambda n, s: kit.ps(f"e{r}_{n}", s, ctx)
        w_raw, w_hi, w_lo = weights["raw"], weights["hi"], weights["lo"]
        slots = [sb(f"slots{u}", [P, ST * ROW]) for u in range(2)]
        s_hi, s_lo = sb("s_hi", [P, KD, CAP], F32R), sb("s_lo", [P, KD, CAP], F32R)
        act_a = [sb(f"act_a{u}", [P, 512]) for u in range(2)]
        hid = [sb(f"hid{u}", [P, 512]) for u in range(2)]
        h_hi = [sb(f"h_hi{u}", [P, KF, 512], F32R) for u in range(2)]
        h_lo = [sb(f"h_lo{u}", [P, KF, 512], F32R) for u in range(2)]
        res = [sb(f"res{u}", [P, D]) for u in range(4)]
        tp = ps("tp", [P, KD, 512])
        a_ps = [ps(f"a{u}", [P, 512]) for u in range(2)]
        g_ps = [ps(f"g{u}", [P, 512]) for u in range(2)]
        o_ps = [ps(f"o{u}", [P, 512]) for u in range(2)]
        (w_loaded, w_split, w_rest, s_tposed, s_hi_done, s_lo_done, a_done, g_done, gelu_done, hid_done,
         h_hi_done, h_lo_done, o_done, res_ready, slots_free) = kit.sems_again(
            "experts", "w_loaded w_split w_rest s_tposed s_hi_done s_lo_done a_done g_done gelu_done hid_done "
            "h_hi_done h_lo_done o_done res_ready slots_free")
        slots_in = kit.sems_again("experts_slots_in", "0 1")
        y_sent = kit.sems(f"e{r}_y_sent", "0 1 2 3")
        NC, NW = len(CHUNKS), len(W_PARTS)
        w_in_at = lambda w, k, f: w[:, k * 2 * FF + f * P:k * 2 * FF + (f + 1) * P]
        w_out_at = lambda w, k: w[:, NIN + k * D:NIN + (k + 1) * D]
        HID0, O0, RES0, Y0 = 2, 2 * ST, 2, 16
        RB = len(res)
        sent_in = lambda q, n: len([m for m in range(n) if m % RB == q])
        BODY = 2 * ST
        SENT = sent_in(0, BODY) * 16
        assert all(sent_in(q, BODY) * 16 == SENT for q in range(RB))
        m_ = lambda u, ci, f: (u * NC + ci) * KF + f

        def in_turn(eng, body):
            with eng.Fori(0, EXP // 2 - 1) as i:
                body(i, 0, True)
                body(i, 1, True)
            body(EXP // 2 - 1, 0, True)
            body(EXP // 2 - 1, 1, False)

        with nc.Block() as block:

            @block.sync
            def _(sp):
                sp.sem_inc(w_rest, NW)
                disp_v = disp.rearrange("(q j) c -> q (j c)", j=ST)

                def load_slots(e, u):
                    sp.dma_start(slots[u][:], disp_v[bass.ds(e * P, P), :]).then_inc(slots_in[u], 16)

                def load_next(e, u, first=False):
                    sp.wait_ge(w_rest, e * NW)
                    load_weights(nc.sync, weights, w_in_dram, w_out_dram, e, w_loaded)
                    if not first:
                        sp.wait_ge(slots_free, e)
                    load_slots(e, u)

                load_slots(0, 0)
                load_next(1, 1, first=True)
                with nc.sync.Fori(0, EXP // 2 - 1) as i:
                    load_next(i * 2 + 2, 0)
                    load_next(i * 2 + 3, 1)

            @block.gpsimd
            def _(pool):
                last_row = nc.gpsimd.to_reg(TOPK * TOK - 1)
                link = chain(kit, pool, "pool_step")
                for q in range(RB):
                    link(nc.gpsimd.memset(res[q][:], 0.0))
                for q in range(RB):
                    nc.gpsimd.dma_start(spare[q], res[q][:, 0:16]).then_inc(y_sent[q], Y0)

                def body(i, u, more):
                    e = i * 2 + u

                    def rests(ci):
                        n = CHUNKS[ci][1]
                        for f in range(KF):
                            m = e * NC * KF + ci * KF + f
                            pool.wait_ge(h_hi_done, m + 1)
                            hh = h_hi[(u * NC + ci) % 2][:, f, 0:n]
                            nc.gpsimd.tensor_tensor(h_lo[(u * NC + ci) % 2][:, f, 0:n], hid[m_(u, ci, f) % 2][:, 0:n],
                                                    hh.bitcast(F32), ALU.subtract).then_inc(h_lo_done, 1)

                    def send(ci):
                        c0, n = CHUNKS[ci]
                        for j in range(c0 // P, (c0 + n) // P):
                            pool.wait_ge(res_ready, e * ST + j + 1 + RES0)
                            kit.part(pool)
                            at = bass.IndirectOffsetOnAxis(
                                ap=slots[u][:, j * ROW + D:j * ROW + D + 1].bitcast(I32), axis=0)
                            nc.gpsimd.indirect_dma_start(ydram, at, res[(u * ST + j) % RB][:], None,
                                                         bounds_check=last_row,
                                                         oob_is_err=False).then_inc(y_sent[(u * ST + j) % RB], 16)

                    rests(0)
                    for q in range(RB):
                        pool.wait_ge(y_sent[q], Y0 + i * SENT + sent_in(q, u * ST) * 16)
                    pool.sem_inc(slots_free, 1)
                    rests(1)
                    send(0)
                    rests(2)
                    send(1)
                    send(2)

                in_turn(nc.gpsimd, body)
                for q in range(RB):
                    pool.wait_ge(y_sent[q], Y0 + EXP // 2 * SENT)

            @block.vector
            def _(dve):
                dve.sem_inc(o_done, O0)

                def slots_lo(e, ci):
                    c0, n = CHUNKS[ci]
                    dve.wait_ge(s_hi_done, e * NC + ci + 1)
                    nc.vector.tensor_tensor(s_lo[:, :, c0:c0 + n], tp[:, :, 0:n],
                                            s_hi[:, :, c0:c0 + n].bitcast(F32), ALU.subtract).then_inc(s_lo_done, 1)

                def body(i, u, more):
                    e = i * 2 + u

                    def hidden(ci):
                        n = CHUNKS[ci][1]
                        h = (u * NC + ci) % 2
                        c0 = CHUNKS[ci - 2][0] + CHUNKS[ci - 2][1] - (0 if ci >= 2 else CAP)
                        dve.wait_ge(o_done, e * ST + c0 // P + O0)
                        for f in range(KF):
                            m = e * NC * KF + ci * KF + f
                            q = m_(u, ci, f) % 2
                            dve.wait_ge(gelu_done, m + 1)
                            dve.wait_ge(g_done, m + 1)
                            dve.wait_ge(h_lo_done, m + 1)
                            nc.vector.tensor_tensor(hid[q][:, 0:n], act_a[q][:, 0:n], g_ps[q][:, 0:n],
                                                    ALU.mult).then_inc(hid_done, 1)
                            dve.wait_ge(hid_done, m + 1 + HID0)
                            nc.vector.tensor_copy(h_hi[h][:, f, 0:n], hid[q][:, 0:n]).then_inc(h_hi_done, 1)

                    def weights_rest(z):
                        a, b = W_PARTS[z]
                        dve.wait_ge(w_split, e * NW + z + 1)
                        nc.vector.tensor_tensor(w_lo[1 - u][:, a:b], w_raw[:, a:b], w_hi[1 - u][:, a:b].bitcast(F32),
                                                ALU.subtract).then_inc(w_rest, 1)

                    hidden(0)
                    slots_lo(e, 2)
                    if more:
                        weights_rest(0)
                    hidden(1)
                    if more:
                        weights_rest(1)
                        weights_rest(2)
                    hidden(2)
                    if more:
                        slots_lo(e + 1, 0)
                        slots_lo(e + 1, 1)

                slots_lo(0, 0)
                slots_lo(0, 1)
                in_turn(nc.vector, body)

            @block.scalar
            def _(act):
                act.sem_inc(hid_done, HID0)
                act.sem_inc(h_lo_done, HID0)

                def slots_hi(e, ci):
                    c0, n = CHUNKS[ci]
                    act.wait_ge(s_tposed, e * NC + ci + 1)
                    nc.scalar.copy(s_hi[:, :, c0:c0 + n], tp[:, :, 0:n]).then_inc(s_hi_done, 1)

                def body(i, u, more):
                    e = i * 2 + u

                    def gelu(ci):
                        n = CHUNKS[ci][1]
                        for f in range(KF):
                            m = e * NC * KF + ci * KF + f
                            q = m_(u, ci, f) % 2
                            act.wait_ge(a_done, m + 1)
                            act.wait_ge(hid_done, m + 1)
                            nc.scalar.activation(act_a[q][:, 0:n], a_ps[q][:, 0:n], ACT.Gelu).then_inc(gelu_done, 1)

                    def results(ci):
                        c0, n = CHUNKS[ci]
                        for j in range(c0 // P, (c0 + n) // P):
                            m = e * ST + j
                            act.wait_ge(o_done, m + 1 + O0)
                            b = u * ST + j
                            act.wait_ge(y_sent[b % RB], Y0 + SENT * i + b // RB * 16)
                            nc.scalar.copy(res[b % RB][:], o_ps[(u * ST + j) % 2][:, 0:D]).then_inc(res_ready, 1)

                    def weights_high(z):
                        a, b = W_PARTS[z]
                        if z == 0:
                            act.wait_ge(w_loaded, (e + 1) * 32)
                            act.wait_ge(o_done, e * ST + O0)
                        nc.scalar.copy(w_hi[1 - u][:, a:b], w_raw[:, a:b]).then_inc(w_split, 1)

                    gelu(0)
                    slots_hi(e, 2)
                    if more:
                        weights_high(0)
                    gelu(1)
                    if more:
                        weights_high(1)
                    results(0)
                    if more:
                        weights_high(2)
                    gelu(2)
                    if more:
                        slots_hi(e + 1, 0)
                    results(1)
                    if more:
                        slots_hi(e + 1, 1)
                    results(2)

                slots_hi(0, 0)
                slots_hi(0, 1)
                in_turn(nc.scalar, body)

            @block.tensor
            def _(pe):
                pe.sem_inc(s_lo_done, 1)
                pe.sem_inc(res_ready, RES0)

                def transposes(e, u, tile, ci):
                    c0, n = CHUNKS[ci]
                    if ci == 0:
                        pe.wait_ge(slots_in[u], (tile + 1) * 16)
                    pe.wait_ge(s_lo_done, e * NC + ci + 1)
                    for j in range(n // P):
                        for k in range(KD):
                            at = (c0 // P + j) * ROW + k * P
                            last = nc.tensor.transpose(tp[:, k, j * P:(j + 1) * P], slots[u][:, at:at + P], c["ident"][:])
                    last.then_inc(s_tposed, 1)

                def body(i, u, more):
                    e = i * 2 + u

                    def up(ci):
                        c0, n = CHUNKS[ci]
                        pe.wait_ge(s_lo_done, e * NC + ci + 2)
                        if ci == 0:
                            pe.wait_ge(w_rest, (e + 1) * NW)
                        for f in range(KF):
                            m = e * NC * KF + ci * KF + f
                            q = m_(u, ci, f) % 2
                            pe.wait_ge(hid_done, m + 1)
                            for half, bank, done in ((0, a_ps, a_done), (KF, g_ps, g_done)):
                                terms = [(w, s, k) for k in range(KD)
                                         for w, s in ((w_hi[u], s_hi), (w_hi[u], s_lo), (w_lo[u], s_hi))]
                                for z, (w, s, k) in enumerate(terms):
                                    last = nc.tensor.matmul(bank[q][:, 0:n], w_in_at(w, k, half + f),
                                                            s[:, k, c0:c0 + n], start=(z == 0),
                                                            stop=(z == len(terms) - 1))
                                last.then_inc(done, 1)

                    def down(ci):
                        c0, n = CHUNKS[ci]
                        h = (u * NC + ci) % 2
                        pe.wait_ge(h_lo_done, e * NC * KF + (ci + 1) * KF + HID0)
                        for j in range(n // P):
                            m = e * ST + c0 // P + j
                            pe.wait_ge(res_ready, m + 1)
                            terms = [(w, s, k) for k in range(KF)
                                     for w, s in ((w_hi[u], h_hi[h]), (w_lo[u], h_hi[h]), (w_hi[u], h_lo[h]))]
                            for z, (w, s, k) in enumerate(terms):
                                last = nc.tensor.matmul(o_ps[(u * ST + c0 // P + j) % 2][:, 0:D],
                                                        s[:, k, j * P:(j + 1) * P], w_out_at(w, k),
                                                        start=(z == 0), stop=(z == len(terms) - 1))
                            last.then_inc(o_done, 1)

                    next_tile = i + u
                    up(0)
                    transposes(e, u, i, 2)
                    up(1)
                    down(0)
                    up(2)
                    if more:
                        transposes(e + 1, 1 - u, next_tile, 0)
                    down(1)
                    if more:
                        transposes(e + 1, 1 - u, next_tile, 1)
                    down(2)

                transposes(0, 0, 0, 0)
                transposes(0, 0, 0, 1)
                in_turn(nc.tensor, body)


def combine(kit, c, r, ydram, gates, out_dram):
    nc, x = kit.nc, c["x"]
    U = 4
    with ExitStack() as ctx:
        y = [kit.sb(f"c{r}_y{u}", [P, TOPK, U, D], F32, ctx) for u in range(2)]
        mixed, first, stored = kit.sems(f"c{r}", "mixed first stored")
        y_in = kit.sems(f"c{r}_y_in", "0 1")
        with nc.Block() as block:

            @block.sync
            def _(sp):
                yv = ydram.rearrange("(k t p) d -> p k t d", k=TOPK, p=P)
                sp.sem_inc(mixed, 2 * U)
                with nc.sync.Fori(0, NT // U // 2) as i:
                    for u in range(2):
                        s = i * 2 + u
                        sp.wait_ge(mixed, (s + 1) * U)
                        for k in range(TOPK):
                            sp.dma_start(y[u][:, k, :, :], yv[:, k, bass.ds(s * U, U), :]).then_inc(y_in[u], 16)

            @block.vector
            def _(dve):
                with nc.vector.Fori(0, NT // U // 2) as i:
                    for u in range(2):
                        s = i * 2 + u
                        dve.wait_ge(y_in[u], (i + 1) * 16 * TOPK)
                        for k in range(TOPK):
                            if k:
                                dve.wait_ge(first, (s + 1) * U)
                            for v in range(U):
                                t = s * U + v
                                xt = x[:, bass.ds(t * D, D)]
                                nc.vector.scalar_tensor_tensor(
                                    xt, y[u][:, k, v, :], gates[:].rearrange("p k t -> p (k t)")[:, bass.ds(t + k * NT, 1)],
                                    xt, ALU.mult, ALU.add).then_inc(mixed if k else first, 1)

            if out_dram is not None:
                @block.scalar
                def _(act):
                    ov = out_dram.rearrange("(t p) d -> p t d", p=P)
                    with nc.scalar.Fori(0, NT // U) as i:
                        act.wait_ge(mixed, (i + 3) * U)
                        act.dma_start(ov[:, bass.ds(i * U, U), :],
                                      x[:].rearrange("p (t d) -> p t d", d=D)[:, bass.ds(i * U, U), :]).then_inc(stored, 16)
                    act.wait_ge(stored, NT // U * 16)



def project(kit, c, w, packs, v_dram):
    nc, x = kit.nc, c["x"]
    U = QC // P
    with ExitStack() as ctx:
        sb = lambda n, s, dt=F32: kit.sb(f"q_{n}", s, dt, ctx)
        ps = lambda n, s: kit.ps(f"q_{n}", s, ctx)
        stats = sb("stats", [P, NT, 6])
        mean, rstd = sb("mean", [P, NT]), sb("rstd", [P, NT])
        tmp = [sb(f"tmp{i}", [P, NT]) for i in range(3)]
        NW = 3 * KD * D
        w_raw = sb("w_raw", [P, NW + KD * P])
        w_hi, w_lo = (sb(n, [P, NW + KD * P], F32R) for n in ("w_hi", "w_lo"))
        bias = sb("bias", [P, 3, KD])
        bv = sb("bv", [P, D])
        lam = sb("lam", [P, 1])
        stage = [sb(f"stage{u}", [P, D]) for u in range(U)]
        x_hi, x_lo = (sb(n, [P, KD, QC], F32R) for n in ("x_hi", "x_lo"))
        full = {n: [sb(f"{n}{u}", [P, QC]) for u in range(KD)] for n in ("q", "tq", "t", "k", "tk")}
        tq_hi, tq_lo = ([sb(f"{n}{u}", [P, QC], F32R) for u in range(KD)] for n in ("tq_hi", "tq_lo"))
        pack = [sb(f"pack{u}", [P, 8, QC], F32R) for u in range(KD)]
        vals = sb("vals", [P, U, HEADS, HP])
        tp = ps("tp", [P, KD, QC])
        y_ps = [ps(f"y{u}", [P, QC]) for u in range(2)]
        t_ps = [ps(f"t{u}", [P, QC]) for u in range(KD)]
        v_ps = [ps(f"v{u}", [P, QC]) for u in range(2)]
        (w_in, w_split, j_zero, v_ready, bias_done, stats_done, root_ready, root_done, normed, tposed, x_hi_done, x_lo_done,
         y_done, y_read, full_done, hi_done, lo_done, tq_rest, t_done, t_read, v_done, v_read, chunk_out, v_out, pool_lo) = kit.sems(
            "q", "w_in w_split j_zero v_ready bias_done stats_done root_ready root_done normed tposed x_hi_done x_lo_done "
            "y_done y_read full_done hi_done lo_done tq_rest t_done t_read v_done v_read chunk_out v_out pool_lo")
        wt = lambda a, m, k, e0, n: a[:, (m * KD + k) * D + e0:(m * KD + k) * D + e0 + n]
        jt = lambda a, g: a[:, NW + g * P:NW + (g + 1) * P]
        N_W = 3 + 2 * KD + 2 + HEADS
        Q_HI, Q_LO, T_HI, T_LO, K_HI, K_LO, TK_HI, TK_LO = range(8)

        with nc.Block() as block:

            @block.sync
            def _(sp):
                for m, name in enumerate(("WqT", "WkT", "WvT")):
                    sp.dma_start(w_raw[:, m * KD * D:(m + 1) * KD * D].rearrange("p (k e) -> p k e", k=KD),
                                 w[name].rearrange("(k p) e -> p k e", p=P)).then_inc(w_in, 16)
                for m, name in enumerate(("bq", "bk")):
                    for k in range(KD):
                        sp.dma_start(bias[:, m, k:k + 1], w[name][k * P:(k + 1) * P].rearrange("(p o) -> p o", o=1)).then_inc(w_in, 16)
                sp.dma_start(bv[:], w["bv"].partition_broadcast(P)).then_inc(w_in, 16)
                sp.dma_start(lam[:], w["lam"].partition_broadcast(P)).then_inc(w_in, 16)
                sp.wait_ge(j_zero, 1)
                for h in range(HEADS):
                    r0 = h * HD % P
                    sp.dma_start(w_raw[r0:r0 + HD, NW + h * HD:NW + (h + 1) * HD], w["J"][h]).then_inc(w_in, 16)
                for sem, n in ((pool_lo, 6), (tq_rest, 2), (lo_done, 2), (t_read, 2), (full_done, 8), (chunk_out, 16), (v_out, 16)):
                    sp.sem_inc(sem, n)
                with nc.sync.Fori(0, BATCH) as b:
                    for half in range(2):
                        i = b * 2 + half
                        for g in range(KD):
                            sp.wait_ge(pool_lo, 6 + (i + 1) * 6 - (3 if g == 0 else 0))
                            kit.part(sp)
                            sp.wait_ge(lo_done, 2 + (i + 1) * 2 - (1 if g == 0 else 0))
                            sp.dma_start(packs.rearrange("a b (g p) c -> b g p a c", p=P)[bass.ds(b, 1), g, :, :, half * QC:(half + 1) * QC]
                                         .rearrange("o p a c -> (o p) a c"),
                                         pack[g][:].bitcast(F32)).then_inc(chunk_out, 16)
                        sp.wait_ge(v_read, (i + 1) * U + 2)
                        for g in range(NG):
                            sp.dma_start(v_dram.rearrange("(b g) t p c -> b g t p c", g=NG)
                                         [bass.ds(b, 1), g, half * U:(half + 1) * U, :, :].rearrange("o t p c -> p (o t) c"),
                                         vals[:, :, g * GH:(g + 1) * GH, :].rearrange("p u h c -> p u (h c)")).then_inc(v_out, 16)
                sp.wait_ge(chunk_out, 16 + 2 * BATCH * KD * 16)
                sp.wait_ge(v_out, 16 + 2 * BATCH * NG * 16)

            @block.gpsimd
            def _(pool):
                nc.gpsimd.memset(w_raw[:, NW:], 0.0).then_inc(j_zero, 1)
                nc.gpsimd.memset(vals[:], 0.0).then_inc(v_ready, 1)
                pool.wait_ge(v_ready, 1)
                nc.gpsimd.memset(vals[:, :, :, HD:HD + 1], 1.0).then_inc(v_ready, 1)
                with nc.gpsimd.Fori(0, 2 * BATCH) as i:
                    for g in range(KD):
                        for n, (name, hi, lo) in enumerate((("q", Q_HI, Q_LO), ("k", K_HI, K_LO), ("tk", TK_HI, TK_LO))):
                            pool.wait_ge(hi_done, i * 10 + g * 5 + (1, 3, 4)[n])
                            nc.gpsimd.tensor_tensor(pack[g][:, lo, :], full[name][g][:], pack[g][:, hi, :].bitcast(F32),
                                                    ALU.subtract).then_inc(pool_lo, 1)

            @block.vector
            def _(dve):
                link = chain(kit, dve, "dve_step")
                with nc.vector.Fori(0, NT // 4) as i:
                    for u in range(4):
                        t = i * 4 + u
                        nc.vector.bn_stats(stats[:].rearrange("p t s -> p (t s)")[:, bass.ds(t * 6, 6)],
                                           x[:, bass.ds(t * D, D)]).then_inc(stats_done, 1)
                dve.wait_ge(stats_done, NT)
                rstd_of(nc, link, mean[:], rstd[:], stats, [a[:] for a in tmp], root_ready, root_done)
                dve.wait_ge(w_in, N_W * 16)
                link(nc.vector.tensor_copy(w_hi[:], w_raw[:]))
                nc.vector.tensor_tensor(w_lo[:], w_raw[:], w_hi[:].bitcast(F32), ALU.subtract).then_inc(w_split, 1)
                nc.vector.tensor_scalar(bias[:, 2, :], bias[:, 0, :], 0.25, None, ALU.mult).then_inc(bias_done, 1)
                dve.wait_ge(v_ready, 2)
                dve.sem_inc(tposed, 1)
                with nc.vector.Fori(0, 2 * BATCH) as i:
                    dve.wait_ge(tposed, i + 1)
                    for u in range(U):
                        t = i * U + u
                        nc.vector.tensor_scalar(stage[u][:], x[:, bass.ds(t * D, D)], mean[:, bass.ds(t, 1)],
                                                rstd[:, bass.ds(t, 1)], ALU.subtract, ALU.mult).then_inc(normed, 1)
                    dve.wait_ge(x_hi_done, i + 1)
                    nc.vector.tensor_tensor(x_lo[:], tp[:], x_hi[:].bitcast(F32), ALU.subtract).then_inc(x_lo_done, 1)
                    dve.wait_ge(chunk_out, 16 + i * KD * 16)
                    for g in range(KD):
                        for n, (name, to) in enumerate((("q", pack[g][:, Q_HI, :]), ("tq", tq_hi[g][:]),
                                                        ("k", pack[g][:, K_HI, :]), ("tk", pack[g][:, TK_HI, :]))):
                            dve.wait_ge(full_done, 8 + i * 8 + g * 4 + n + 1)
                            nc.vector.tensor_copy(to, full[name][g][:]).then_inc(hi_done, 1)
                            if name == "tq":
                                dve.wait_ge(hi_done, i * 10 + g * 5 + 2)
                                nc.vector.tensor_tensor(tq_lo[g][:], full["tq"][g][:], tq_hi[g][:].bitcast(F32),
                                                        ALU.subtract).then_inc(tq_rest, 1)
                        dve.wait_ge(t_done, i * 2 + g + 1)
                        dve.wait_ge(lo_done, i * 2 + 2)
                        nc.vector.tensor_scalar(full["t"][g][:], t_ps[g][:], lam[:, 0:1], None, ALU.mult).then_inc(t_read, 1)
                        dve.wait_ge(t_read, i * 2 + g + 1 + 2)
                        nc.vector.tensor_copy(pack[g][:, T_HI, :], full["t"][g][:]).then_inc(hi_done, 1)
                        dve.wait_ge(hi_done, i * 10 + g * 5 + 5)
                        nc.vector.tensor_tensor(pack[g][:, T_LO, :], full["t"][g][:], pack[g][:, T_HI, :].bitcast(F32),
                                                ALU.subtract).then_inc(lo_done, 1)
                    dve.wait_ge(v_out, 16 + i * NG * 16)
                    for u in range(U):
                        dve.wait_ge(v_done, i * U + u + 1)
                        nc.vector.tensor_tensor(vals[:, u, :, 0:HD], v_ps[u % 2][:, 0:D].rearrange("p (h c) -> p h c", c=HD),
                                                bv[:].rearrange("p (h c) -> p h c", c=HD), ALU.add).then_inc(v_read, 1)

            @block.scalar
            def _(act):
                act.wait_ge(root_ready, 1)
                nc.scalar.activation(rstd[:], tmp[2][:], ACT.Sqrt).then_inc(root_done, 1)
                act.wait_ge(bias_done, 1)
                with nc.scalar.Fori(0, 2 * BATCH) as i:
                    act.wait_ge(tposed, i + 2)
                    nc.scalar.copy(x_hi[:], tp[:]).then_inc(x_hi_done, 1)
                    for g in range(KD):
                        for m in range(2):
                            n = g * 2 + m
                            names = (("q", "tq"), ("k", "tk"))[m]
                            act.wait_ge(y_done, i * 4 + n + 1)
                            act.wait_ge(pool_lo, i * 6 + 6)
                            act.wait_ge(tq_rest, i * 2 + 2)
                            if m == 0:
                                nc.scalar.activation(full["q"][g][:], y_ps[n % 2][:], ACT.Identity, bias=bias[:, 2, g:g + 1],
                                                     scale=0.25).then_inc(full_done, 1)
                            else:
                                nc.scalar.activation(full["k"][g][:], y_ps[n % 2][:], ACT.Identity,
                                                     bias=bias[:, 1, g:g + 1]).then_inc(full_done, 1)
                            nc.scalar.activation(full[names[1]][g][:], y_ps[n % 2][:], ACT.Tanh,
                                                 bias=bias[:, m, g:g + 1]).then_inc(full_done, 1)

            @block.tensor
            def _(pe):
                pe.wait_ge(w_split, 1)
                pe.sem_inc(x_lo_done, 1)
                pe.sem_inc(v_read, 2)

                def split_product(out, terms, last_sem):
                    for z, (a, b) in enumerate(terms):
                        last = nc.tensor.matmul(out, a, b, start=(z == 0), stop=(z == len(terms) - 1))
                    last.then_inc(last_sem, 1)

                with nc.tensor.Fori(0, 2 * BATCH) as i:
                    pe.wait_ge(x_lo_done, i + 1)
                    for u in range(U):
                        pe.wait_ge(normed, i * U + u + 1)
                        for k in range(KD):
                            last = nc.tensor.transpose(tp[:, k, u * P:(u + 1) * P], stage[u][:, k * P:(k + 1) * P], c["ident"][:])
                    last.then_inc(tposed, 1)
                    pe.wait_ge(x_lo_done, i + 2)

                    def q_or_k(g, m):
                        n = g * 2 + m
                        if n >= 2:
                            pe.wait_ge(full_done, 8 + i * 8 + (n - 1) * 2)
                        else:
                            pe.wait_ge(full_done, 8 + i * 8)
                        split_product(y_ps[n % 2][:], [(wt(a, m, k, g * P, P), b[:, k, :]) for k in range(KD)
                                                       for a, b in ((w_hi, x_hi), (w_hi, x_lo), (w_lo, x_hi))], y_done)

                    def tangents(g):
                        pe.wait_ge(tq_rest, 2 + i * 2 + g + 1)
                        pe.wait_ge(t_read, i * 2 + 2)
                        split_product(t_ps[g][:], [(jt(w_hi, g), tq_hi[g][:]), (jt(w_hi, g), tq_lo[g][:]),
                                                   (jt(w_lo, g), tq_hi[g][:])], t_done)

                    def values(u):
                        pe.wait_ge(v_read, i * U + u + 1)
                        split_product(v_ps[u % 2][:, 0:D], [(a[:, k, u * P:(u + 1) * P], wt(b, 2, k, 0, D)) for k in range(KD)
                                                            for a, b in ((x_hi, w_hi), (x_lo, w_hi), (x_hi, w_lo))], v_done)

                    q_or_k(0, 0)
                    q_or_k(0, 1)
                    tangents(0)
                    q_or_k(1, 0)
                    q_or_k(1, 1)
                    tangents(1)
                    for u in range(U):
                        values(u)


def attend(kit, c, packs, v_dram, o_dram, bo_dram):
    nc, x = kit.nc, c["x"]
    GROUPS = BATCH * NG
    NB = 3
    def diagonal(k0):
        return [(k0, 0, 0, QC, 0), (k0 + 3, 7 * P, 3 * P, P, P), (k0 + 1, 4 * P, P, 3 * P, 0)], [(k0 + 2, 0, 2 * P, 2 * P, 0)]
    A0, B0 = diagonal(0)
    A1, B1 = diagonal(4)
    full_pair = lambda k0: [(k0, 0, 0, QC, 0), (k0 + 1, QC, 0, QC, 0)]
    STEPS = [(0, A0), (0, B0), (1, full_pair(0)), (1, full_pair(2)), (1, A1), (1, B1)]
    WIDTH = [1024, 256, 1024, 1024, 1024, 256]
    NS = len(STEPS)
    UNITS = [(qt, part) for qt in range(KT) for part in range(1 + (qt >= 4))]
    NU = len(UNITS)
    with ExitStack() as ctx:
        sb = lambda n, s, dt=F32: kit.sb(f"a_{n}", s, dt, ctx)
        ps = lambda n, s: kit.ps(f"a_{n}", s, ctx)
        qp = [sb(f"qp{u}", [PACK + 1, GH, SEQ], F32R) for u in range(NB)]
        kp = [sb(f"kp{u}", [PACK + 1, GH, SEQ], F32R) for u in range(NB)]
        vg = [sb(f"vg{u}", [P, KT, GH, HP]) for u in range(NB)]
        wts = [sb(f"wts{u}", [P, GH, 2 * QC]) for u in range(2)]
        parts = [sb(f"parts{u}", [P, KT, 2]) for u in range(2)]
        tops = [sb(f"tops{u}", [P, KT]) for u in range(2)]
        neg = [sb(f"neg{u}", [KT, P], F32R) for u in range(2)]
        o_sb = [sb(f"o_sb{u}", [P, QC]) for u in range(2)]
        masked = [sb(f"masked{u}", [P, QC], BF16) for u in range(2)]
        bo = sb("bo", [P, D])
        s_ps = [ps(f"s{u}", [P, 2 * QC]) for u in range(2)]
        m_ps = [ps(f"m{u}", [P, QC]) for u in range(2)]
        o_ps = ps("o", [P, QC])
        t_ps = ps("t", [P, QC])
        (made, bo_in, scored, weighed, cleared, mixed, maxed, max_read, topped, turned, negated, o_taken,
         bo_added) = kit.sems(
            "a", "made bo_in scored weighed cleared mixed maxed max_read topped turned negated o_taken bo_added")
        loaded = kit.sems("a_loaded", "0 1 2")
        row_in = kit.sems("a_row_in", "0 1 2 3")
        stored = kit.sems("a_stored", "0 1")
        NL = 13
        MIX0, OUT0 = 2, 16
        on_diagonal = lambda s: [b for b in STEPS[s][1] if b[0] // 4 == STEPS[s][0]]
        clears = [sum(len(on_diagonal(z)) for z in range(s)) for s in range(NS + 1)]
        m_b = lambda h, z: (h * NU + z) % 2
        TURNS = (8, 15, 20)

        def groups(eng, body):
            assert GROUPS % NB == 1
            with eng.Fori(0, GROUPS // NB) as i:
                for u in range(NB):
                    body(i, u, False)
            body(GROUPS // NB, 0, True)

        with nc.Block() as block:

            @block.sync
            def _(sp):
                sp.dma_start(bo[:], bo_dram.partition_broadcast(P)).then_inc(bo_in, 16)

                def load(gi, u):
                    for block_row, (qa, ka) in enumerate(((0, 4), (0, 5), (1, 4), (2, 6), (2, 7), (3, 6))):
                        for t, a in ((qp, qa), (kp, ka)):
                            sp.dma_start(t[u][block_row * HD:(block_row + 1) * HD, :, :].bitcast(F32),
                                         packs[a].rearrange("b (g j r) c -> (b g) r j c", g=NG, j=GH)[bass.ds(gi, 1), :, :, :]
                                         .rearrange("o r j c -> (o r) j c")).then_inc(loaded[u], 16)
                    sp.dma_start(vg[u][:].rearrange("p t h c -> p t (h c)"),
                                 v_dram[bass.ds(gi, 1), :, :, :].rearrange("o t p c -> p (o t) c")).then_inc(loaded[u], 16)

                def rows(gi, u):
                    for h in range(GH):
                        sp.wait_ge(negated, gi * GH + h + 1)
                        sp.dma_start(qp[u][PACK:PACK + 1, h, :].bitcast(F32), neg[h % 2][:].bitcast(F32)).then_inc(row_in[h], 16)

                def store(g):
                    for ch in range(2):
                        sp.wait_ge(o_taken, 1 + g * 2 + ch + 1)
                        sp.dma_start(o_dram.rearrange("g p c -> (g p) c")[bass.ds(g * P, P), ch * QC:(ch + 1) * QC],
                                     o_sb[ch][:]).then_inc(stored[ch], 16)

                def next_groups(g, u, more):
                    rows(g + 1, (u + 1) % NB)
                    if more:
                        sp.wait_ge(mixed, MIX0 + (g + 1) * NS)
                        load(g + NB, u)
                    store(g)

                for g in range(NB):
                    load(g, g)
                for ch in range(2):
                    sp.sem_inc(stored[ch], OUT0)
                rows(0, 0)
                FULL = (GROUPS - NB) // NB
                with nc.sync.Fori(0, FULL) as i:
                    for u in range(NB):
                        next_groups(i * NB + u, u, True)
                for g in range(FULL * NB, GROUPS - 1):
                    next_groups(g, g % NB, g + NB < GROUPS)
                store(GROUPS - 1)
                for ch in range(2):
                    sp.wait_ge(stored[ch], OUT0 + GROUPS * 16)

            @block.gpsimd
            def _(pool):
                link = chain(kit, pool, "pool_step")
                for u in range(NB):
                    link(nc.gpsimd.memset(kp[u][PACK:PACK + 1, :, :].bitcast(F32), 1.0))
                for u in range(2):
                    link(nc.gpsimd.memset(parts[u][:], -3e38))
                pool.sem_inc(made, 1)
                pool.wait_ge(bo_in, 16)
                xv = x[:].rearrange("p (t d) -> p t d", d=D)
                nc.gpsimd.tensor_tensor(xv, xv, bo[:].unsqueeze(1).to_broadcast([P, NT, D]), ALU.add).then_inc(bo_added, 1)

                def body(i, u, last):
                    g = i * NB + u
                    for s in range(NS):
                        for z, (kt, col, q0, w, lead) in enumerate(on_diagonal(s)):
                            if z == 0:
                                pool.wait_ge(weighed, 2 + g * NS * GH + (s + 1) * GH)
                                kit.part(pool)
                            block_w = wts[(u * NS + s) % 2][:, :, col:col + P]
                            nc.gpsimd.affine_select(out=block_w, in_=block_w, compare_op=ALU.is_ge, fill=0.0, base=0,
                                                    pattern=[[0, GH], [1, P]], channel_multiplier=-1).then_inc(cleared, 1)

                groups(nc.gpsimd, body)

            @block.vector
            def _(dve):
                dve.wait_ge(made, 1)
                dve.sem_inc(turned, 2)

                def maxima(n, h, units):
                    for z in units:
                        qt, part = UNITS[z]
                        m = n * GH * NU + h * NU + z
                        dve.wait_ge(maxed, m + 1)
                        width = (qt + 1) * P - part * QC if part or qt < 4 else QC
                        top, seen = parts[h % 2][:, qt, part:part + 1], m_ps[m_b(h, z)][:, 0:width]
                        if (qt + 1) * P == part * QC + width:
                            kit.part(dve)
                            nc.vector.tensor_tensor_reduce(masked[m_b(h, z)][:, 0:width], seen, c["mask"][:, QC - width:], 1.0, MASKED,
                                                           ALU.add, ALU.max, top).then_inc(max_read, 1)
                        else:
                            nc.vector.reduce_max(top, seen, AX.X).then_inc(max_read, 1)
                        if z == NU - 1:
                            dve.wait_ge(max_read, m + 1 + 2)
                            dve.wait_ge(turned, n * GH + h + 1)
                            nc.vector.reduce_max(tops[h % 2][:], parts[h % 2][:], AX.X).then_inc(topped, 1)
                            dve.wait_ge(topped, n * GH + h + 1)

                def body(i, u, last):
                    g = i * NB + u
                    for s in range(NS):
                        for j in range(GH):
                            q = s * GH + j
                            if not last:
                                maxima(g + 1, q // 6, (2 * (q % 6), 2 * (q % 6) + 1))

                for h in range(GH):
                    maxima(0, h, range(NU))
                groups(nc.vector, body)

            @block.scalar
            def _(act):
                act.sem_inc(mixed, 2)

                def negate(n, h):
                    act.wait_ge(turned, n * GH + h + 1 + 2)
                    if h >= 2:
                        act.wait_ge(row_in[h - 2], (n + 1) * 16)
                    else:
                        act.wait_ge(row_in[h + 2], n * 16)
                    nc.scalar.activation(neg[h % 2][:], t_ps[0:KT, 0:P], ACT.Copy, scale=-1.0).then_inc(negated, 1)

                def take(g, ch):
                    act.wait_ge(mixed, 2 + g * NS + (2, 6)[ch])
                    act.wait_ge(stored[ch], OUT0 + g * 16)
                    nc.scalar.copy(o_sb[ch][:], o_ps[:]).then_inc(o_taken, 1)

                def body(i, u, last):
                    g = i * NB + u
                    for s in range(NS):
                        for j in range(GH):
                            q = s * GH + j
                            act.wait_ge(scored, g * NS * GH + q + 1)
                            if j == 0:
                                act.wait_ge(mixed, g * NS + s + 1)
                            w = WIDTH[s]
                            nc.scalar.activation(wts[(u * NS + s) % 2][:, j, 0:w], s_ps[q % 2][:, 0:w], ACT.Exp).then_inc(weighed, 1)
                            if s == 2 and j == 3:
                                take(g, 0)
                            if not last and q in TURNS:
                                negate(g + 1, TURNS.index(q))
                    take(g, 1)
                    if not last:
                        negate(g + 1, 3)

                for h in range(GH):
                    negate(0, h)
                groups(nc.scalar, body)

            @block.tensor
            def _(pe):
                pe.wait_ge(made, 1)
                pe.sem_inc(weighed, 2)
                pe.sem_inc(max_read, 2)
                pe.sem_inc(o_taken, 1)

                def max_unit(n, ub, h, z):
                    qt, part = UNITS[z]
                    m = n * GH * NU + h * NU + z
                    pe.wait_ge(max_read, m + 1)
                    bank = m_ps[m_b(h, z)]
                    width = (qt + 1) * P - part * QC if part or qt < 4 else QC
                    stream = max(width, 2 * P)
                    last = nc.tensor.matmul(bank[:, 0:stream], qp[ub][0:PACK, h, qt * P:(qt + 1) * P],
                                            kp[ub][0:PACK, h, part * QC:part * QC + stream], start=True, stop=True)
                    last.then_inc(maxed, 1)

                def turn(n, h):
                    pe.wait_ge(topped, n * GH + h + 1)
                    pe.wait_ge(negated, n * GH + h)
                    nc.tensor.transpose(t_ps[0:KT, 0:P], tops[h % 2][:], c["ident"][:]).then_inc(turned, 1)

                def score(g, u, s, j):
                    ch, blocks = STEPS[s]
                    q = s * GH + j
                    if s == 0:
                        pe.wait_ge(row_in[j], (g + 1) * 16)
                    pe.wait_ge(weighed, g * NS * GH + q + 1)
                    for kt, col, q0, w, lead in blocks:
                        at = ch * QC + q0
                        last = nc.tensor.matmul(s_ps[q % 2][:, col - lead:col + w], kp[u][:, j, kt * P:(kt + 1) * P],
                                                qp[u][:, j, at - lead:at + w], start=True, stop=True)
                    last.then_inc(scored, 1)

                def mix(g, u, s, blocks, done):
                    ch = STEPS[s][0]
                    for kt, col, q0, w, lead in blocks:
                        if kt == 0:
                            pe.wait_ge(o_taken, 1 + g * 2 + ch)
                        if kt // 4 == ch:
                            pe.wait_ge(cleared, g * clears[NS] + clears[s + 1])
                        for j in range(GH):
                            pe.wait_ge(weighed, 2 + g * NS * GH + s * GH + j + 1)
                            last = nc.tensor.matmul(o_ps[j * HP:(j + 1) * HP, q0:q0 + w], vg[u][:, kt, j, :],
                                                    wts[(u * NS + s) % 2][:, j, col:col + w], start=(kt == 0),
                                                    stop=(kt == ch * 4 + 2), skip_group_check=True)
                    if done:
                        last.then_inc(mixed, 1)

                def body(i, u, last):
                    g = i * NB + u
                    if not last:
                        pe.wait_ge(loaded[(u + 1) % NB], (i + (u + 1) // NB + 1) * NL * 16)
                    for s in range(NS):
                        for j in range(GH):
                            q = s * GH + j
                            score(g, u, s, j)
                            if not last:
                                for z in (2 * (q % 6), 2 * (q % 6) + 1):
                                    max_unit(g + 1, (u + 1) % NB, q // 6, z)
                            if s and j % 2:
                                blocks = STEPS[s - 1][1]
                                cut = (len(blocks) + 1) // 2
                                part = blocks[:cut] if j == 1 else blocks[cut:]
                                if len(blocks) == 1:
                                    part = blocks if j == 3 else []
                                if part:
                                    mix(g, u, s - 1, part, j == 3)
                            if not last and q in TURNS:
                                turn(g + 1, TURNS.index(q))
                    mix(g, u, NS - 1, STEPS[NS - 1][1], True)
                    if not last:
                        turn(g + 1, 3)

                pe.wait_ge(loaded[0], NL * 16)
                for h in range(GH):
                    for z in range(NU):
                        max_unit(0, 0, h, z)
                    turn(0, h)
                groups(nc.tensor, body)


def project_out(kit, c, o_dram, inv_dram, wo_dram):
    nc, x = kit.nc, c["x"]
    U = QC // P
    with ExitStack() as ctx:
        wo = kit.sb("p_wo", [P, KD, D], F32, ctx)
        sums = kit.sb("p_sums", [P, QC], F32, ctx)
        o, inv, mean = ([kit.sb(f"p_{n}{u}", [P, KD, QC], F32, ctx) for u in range(2)] for n in ("o", "inv", "mean"))
        y_ps = [kit.ps(f"p_y{u}", [P, QC], ctx) for u in range(2)]
        wo_in, sums_in, inverted, inv_out, averaged, y_done, y_read = kit.sems(
            "p", "wo_in sums_in inverted inv_out averaged y_done y_read")
        o_in = kit.sems("p_o_in", "0 1")
        NL = KD * 2
        assert BATCH * HEADS * SEQ == P * QC
        with nc.Block() as block:

            @block.sync
            def _(sp):
                of_heads = o_dram.rearrange("g (j r) (a c) -> (g j) r a c", j=GH, a=2)
                sp.dma_start(sums[:], of_heads[:, HD, :, :]).then_inc(sums_in, 16)
                sp.dma_start(wo[:], wo_dram.rearrange("(k p) d -> p k d", p=P)).then_inc(wo_in, 16)
                sp.wait_ge(inverted, 1)
                sp.dma_start(inv_dram, sums[:]).then_inc(inv_out, 16)
                sp.wait_ge(inv_out, 16)
                sp.sem_inc(averaged, 2)
                inv_of = inv_dram.rearrange("(h a) c -> h a c", a=2)
                HK = P // HD
                with nc.sync.Fori(0, BATCH) as b:
                    for half in range(2):
                        sp.wait_ge(averaged, b * 2 + half + 1)
                        for k in range(KD):
                            heads = bass.ds(b * HEADS + k * HK, HK)
                            sp.dma_start(o[half][:, k, :], of_heads[heads, 0:HD, half, :]).then_inc(o_in[half], 16)
                            sp.dma_start(inv[half][:, k, :], inv_of[heads, half:half + 1, :]
                                         .to_broadcast([HK, HD, QC])).then_inc(o_in[half], 16)

            @block.vector
            def _(dve):
                dve.wait_ge(sums_in, 16)
                nc.vector.reciprocal(sums[:], sums[:]).then_inc(inverted, 1)
                dve.sem_inc(y_done, 2 * U)
                with nc.vector.Fori(0, BATCH) as b:
                    def average(half):
                        i = b * 2 + half
                        dve.wait_ge(o_in[half], (b + 1) * NL * 16)
                        dve.wait_ge(y_done, (i + 1) * U)
                        nc.vector.tensor_tensor(mean[half][:], o[half][:], inv[half][:], ALU.mult).then_inc(averaged, 1)

                    def add(half):
                        for u in range(U):
                            t = (b * 2 + half) * U + u
                            dve.wait_ge(y_done, 2 * U + t + 1)
                            xt = x[:, bass.ds(t * D, D)]
                            nc.vector.tensor_tensor(xt, y_ps[u % 2][:, 0:D], xt, ALU.add).then_inc(y_read, 1)

                    average(0)
                    average(1)
                    add(0)
                    add(1)
                dve.wait_ge(y_read, NT + 2)

            @block.tensor
            def _(pe):
                pe.wait_ge(wo_in, 16)
                pe.sem_inc(y_read, 2)
                with nc.tensor.Fori(0, BATCH) as b:
                    for half in range(2):
                        i = b * 2 + half
                        pe.wait_ge(averaged, i + 1 + 2)
                        for u in range(U):
                            t = i * U + u
                            pe.wait_ge(y_read, t + 1)
                            for k in range(KD):
                                last = nc.tensor.matmul(y_ps[u % 2][:, 0:D], mean[half][:, k, u * P:(u + 1) * P], wo[:, k, :],
                                                        start=(k == 0), stop=(k == KD - 1))
                            last.then_inc(y_done, 1)


def program(nc, x, w, out):
    with ExitStack() as ctx:
        kit = Kit(nc, ctx)
        c = constants(kit)
        gates = kit.sb("gates", [P, TOPK, NT])
        scratch = lambda name, shape: nc.dram_tensor(name, shape, F32, kind="Internal").ap()
        disp = [scratch(f"disp{r}", (EXP * CAP, ROW)) for r in range(2)]
        ydram = scratch("choice_rows", (TOPK * TOK, D))
        spare = scratch("spare", (4, P, 16))
        packs = scratch("packs", (8, BATCH, D, SEQ))
        v_dram = scratch("values", (BATCH * NG, KT, P, GH * HP))
        o_dram = scratch("attended", (BATCH * NG, P, SEQ))
        inv_dram = scratch("inverse_sums", (P, QC))
        build_constants(kit, c, x)

        def mixture(r, to):
            with ExitStack() as both:
                weights = expert_weights(kit, both, r)
                route(kit, c, r, w["Wg"], w["W_in"], w["W_out"], disp[r], ydram, gates, weights)
                experts(kit, c, r, w["W_in"], w["W_out"], disp[r], ydram, spare, weights)
            combine(kit, c, r, ydram, gates, to)

        mixture(0, None)
        project(kit, c, w, packs, v_dram)
        attend(kit, c, packs, v_dram, o_dram, w["bo"])
        project_out(kit, c, o_dram, inv_dram, w["WoT"])
        mixture(1, out)


_NAMES = ["Wg", "W_in", "W_out", "WqT", "WkT", "WvT", "WoT", "bq", "bk", "bv", "bo", "J", "lam"]


def kernel(**inputs):
    import numpy as np
    import concourse.bacc as bacc
    from concourse.bass_utils import run_bass_kernel_spmd

    a = lambda n: np.asarray(inputs[n])
    arrays = {"x": a("L0_attn_x").reshape(TOK, D), "Wg": a("L0_ffn_Wg"), "W_in": a("L0_ffn_W_in"), "W_out": a("L0_ffn_W_out"),
              "J": a("L0_attn_J_attn"), "lam": a("L0_attn_lambda_attn").reshape(1)}
    for n in ("q", "k", "v", "o"):
        arrays[f"W{n}T"] = a(f"L0_attn_W{n}").T
        arrays[f"b{n}"] = a(f"L0_attn_b{n}")
    arrays = {n: np.ascontiguousarray(v) for n, v in arrays.items()}
    nc = bacc.Bacc("TRN2", target_bir_lowering=False, num_devices=1)
    dram = {n: nc.dram_tensor(f"in_{n}", v.shape, mybir.dt.from_np(v.dtype), kind="ExternalInput").ap() for n, v in arrays.items()}
    out = nc.dram_tensor("out", (TOK, D), F32, kind="ExternalOutput").ap()
    program(nc, dram["x"], {n: dram[n] for n in _NAMES}, out)
    got = run_bass_kernel_spmd(nc, [{f"in_{n}": v for n, v in arrays.items()}], core_ids=[0])
    return got.results[0]["out"].reshape(BATCH, SEQ, D)
```

```python
from contextlib import ExitStack

import concourse.bass as bass
from concourse import mybir

F32 = mybir.dt.float32
F32R = mybir.dt.float32r
BF16 = mybir.dt.bfloat16
I32 = mybir.dt.int32
ALU = mybir.AluOpType
ACT = mybir.ActivationFunctionType
AX = mybir.AxisListType

P = 128
BATCH, SEQ, D = 4, 1024, 256
TOK = BATCH * SEQ
NT = TOK // P
KD = D // P
EXP, TOPK, FF = 8, 2, 512
CAP = 1280
ST = CAP // P
KF = FF // P
ROW = D + 1
NOWHERE = 1 << 20
LN_EPS = 1e-5
CHUNKS = [(0, 512), (512, 512), (1024, 256)]


class Kit:

    def __init__(self, nc, ctx):
        self.nc, self.ctx = nc, ctx
        self.kept = {}
        self.steps, self.step_sems = {}, {}

    def step_sem(self, name):
        if name not in self.step_sems:
            self.step_sems[name] = self.sem(name)
        return self.step_sems[name]

    def part(self, eng):
        eng.sem_inc(self.step_sem("parted"), 1)

    def sb(self, name, shape, dt=F32, ctx=None):
        return (ctx or self.ctx).enter_context(self.nc.sbuf_tensor(name, shape, dt))

    def ps(self, name, shape, ctx=None, dt=F32):
        return (ctx or self.ctx).enter_context(self.nc.psum_tensor(f"{name}_psum", shape, dt))

    def sems_again(self, prefix, names):
        if prefix not in self.kept:
            self.kept[prefix] = self.sems(prefix, names)
        return self.kept[prefix]

    def clear_again(self, eng):
        for sems in self.kept.values():
            for sem in sems:
                eng.sem_clear(sem)

    def sem(self, name):
        return self.ctx.enter_context(self.nc.semaphore(name))

    def sems(self, prefix, names):
        return [self.sem(f"{prefix}_{n}") for n in names.split()]


def chain(kit, eng, sem):

    def link(ins):
        kit.steps[sem] = kit.steps.get(sem, 0) + 1
        ins.then_inc(kit.step_sem(sem), 1)
        eng.wait_ge(kit.step_sem(sem), kit.steps[sem])

    return link


def loop_chain(kit, eng, sem, i, steps):
    start = kit.steps.get(sem, 0)

    def link(ins):
        link.done += 1
        ins.then_inc(kit.step_sem(sem), 1)
        eng.wait_ge(kit.step_sem(sem), i * steps + (start + link.done))

    link.done = 0
    return link


def loop_done(kit, sem, link, trips, steps):
    assert link.done == steps
    kit.steps[sem] = kit.steps.get(sem, 0) + trips * steps


def constants(kit):
    nc = kit.nc
    c = {
        "ident": kit.sb("ident", [P, P]),
        "before_bf": kit.sb("before_bf", [P, P], BF16),
        "ones_bf": kit.sb("ones_bf", [P, P], BF16),
        "mask": kit.sb("mask", [P, QC]),
        "rank": kit.sb("rank", [P, EXP]),
        "rank_i": kit.sb("rank_i", [P, EXP], I32),
        "wg": kit.sb("wg", [P, KD, EXP]),
        "x": kit.sb("x_res", [P, NT * D]),
        "stats": kit.sb("stats", [P, NT, 6]),
    }
    return c


MASKED = -1e38
HEADS, HD = 16, 16
GH = 4
NG = HEADS // GH
HP = 32
PACK = 6 * HD
KT = SEQ // P
QC = 512


def empty_slots(eng, c, disp, e, sem):
    eng.dma_start(disp.rearrange("(q j) c -> q (j c)", j=ST)[bass.ds(e * P, P), :], c["blank"][:]).then_inc(sem, 16)


def tile_stats(nc, c, t):
    return nc.vector.bn_stats(c["stats"][:].rearrange("p t s -> p (t s)")[:, bass.ds(t * 6, 6)], c["x"][:, bass.ds(t * D, D)])


def build_constants(kit, c, x_dram, wg_dram, disp):
    nc = kit.nc
    stats_done, wg_in, blank_ready = kit.sems("const", "stats_done wg_in blank_ready")
    c["emptied"] = kit.sem("emptied")
    x_in = kit.sems("const_x_in", "0 1 2 3")
    rank_i = c["rank_i"]
    with nc.Block() as block:

        @block.sync
        def _(sp):
            xv = x_dram.rearrange("(t p) d -> p t d", p=P)
            for q in range(4):
                n = NT // 4
                sp.dma_start(c["x"][:, q * n * D:(q + 1) * n * D].rearrange("p (t d) -> p t d", d=D),
                             xv[:, q * n:(q + 1) * n, :]).then_inc(x_in[q], 16)
            sp.dma_start(c["wg"][:], wg_dram.rearrange("(k p) e -> p k e", p=P)).then_inc(wg_in, 16)
            sp.wait_ge(blank_ready, 2)
            for e in range(EXP):
                empty_slots(nc.sync, c, disp, e, c["emptied"])
            sp.wait_ge(wg_in, 16)

        @block.vector
        def _(dve):
            for q in range(4):
                dve.wait_ge(x_in[q], 16)
                with nc.vector.Fori(0, NT // 4 // 4) as i:
                    for u in range(4):
                        tile_stats(nc, c, i * 4 + (q * NT // 4 + u)).then_inc(stats_done, 1)
            dve.wait_ge(stats_done, NT)

        @block.gpsimd
        def _(pool):
            link = chain(kit, pool, "pool_step")
            nc.gpsimd.memset(c["blank"][:], 0.0).then_inc(blank_ready, 1)
            pool.wait_ge(blank_ready, 1)
            nc.gpsimd.memset(c["blank"][:].rearrange("p (j c) -> p j c", c=ROW)[:, :, D].bitcast(I32),
                             NOWHERE).then_inc(blank_ready, 1)
            for name, v in (("ident", 0.0), ("before_bf", 1.0), ("ones_bf", 1.0),
                            ("mask", 0.0)):
                link(nc.gpsimd.memset(c[name][:], v))
            link(nc.gpsimd.affine_select(out=c["ident"][:], in_=c["ident"][:], compare_op=ALU.not_equal, fill=1.0,
                                         base=0, pattern=[[-1, P]], channel_multiplier=1))
            link(nc.gpsimd.affine_select(out=c["before_bf"][:], in_=c["before_bf"][:], compare_op=ALU.is_ge, fill=0.0,
                                         base=-1, pattern=[[1, P]], channel_multiplier=-1))
            link(nc.gpsimd.affine_select(out=c["mask"][:, QC - P:], in_=c["mask"][:, QC - P:], compare_op=ALU.is_ge,
                                         fill=MASKED, base=0, pattern=[[-1, P]], channel_multiplier=1))
            link(nc.gpsimd.iota(rank_i[:], pattern=[[-1, EXP]], base=EXP, channel_multiplier=0))
            link(nc.gpsimd.tensor_copy(c["rank"][:], rank_i[:]))


def rstd_of(nc, link, mean, rstd, stats, tmp, root_ready, act_ready):
    me, qe, mo, qo = stats[:, :, 1], stats[:, :, 2], stats[:, :, 4], stats[:, :, 5]
    a, b, ve = tmp
    link(nc.vector.tensor_tensor(mean, me, mo, ALU.add))
    link(nc.vector.tensor_scalar(mean, mean, 0.5, None, ALU.mult))
    link(nc.vector.tensor_tensor(a, me, mo, ALU.subtract))
    link(nc.vector.tensor_tensor(a, a, a, ALU.mult))
    link(nc.vector.tensor_tensor(b, qe, qo, ALU.add))
    link(nc.vector.tensor_scalar(b, b, 1.0 / D, LN_EPS, ALU.mult, ALU.add))
    nc.vector.scalar_tensor_tensor(ve, a, 0.25, b, ALU.mult, ALU.add).then_inc(root_ready, 1)
    nc.vector.wait_ge(act_ready, 1)
    link(nc.vector.reciprocal(a, rstd))
    link(nc.vector.tensor_tensor(b, a, a, ALU.mult))
    link(nc.vector.tensor_tensor(b, b, ve, ALU.mult))
    link(nc.vector.tensor_scalar(b, b, -0.5, 1.5, ALU.mult, ALU.add))
    link(nc.vector.tensor_tensor(rstd, a, b, ALU.mult))


NIN, NOUT = KD * 2 * FF, KF * D
W_PARTS = [(z * NIN // 2, (z + 1) * NIN // 2) for z in range(2)] + [(NIN, NIN + NOUT)]


def expert_weights(kit, ctx, r):
    sb = lambda n, dt=F32: kit.sb(f"e{r}_{n}", [P, NIN + NOUT], dt, ctx)
    return {"raw": sb("w_raw"), "hi": [sb(f"w_hi{u}", F32R) for u in range(2)], "lo": [sb(f"w_lo{u}", F32R) for u in range(2)]}


def load_weights(eng, weights, w_in_dram, w_out_dram, e, sem):
    eng.dma_start(weights["raw"][:, 0:NIN].rearrange("p (k f) -> p k f", k=KD),
                  w_in_dram.rearrange("e (k p) f -> p (e k) f", p=P)[:, bass.ds(e * KD, KD), :]).then_inc(sem, 16)
    eng.dma_start(weights["raw"][:, NIN:].rearrange("p (k d) -> p k d", k=KF),
                  w_out_dram.rearrange("e (k p) d -> p (e k) d", p=P)[:, bass.ds(e * KF, KF), :]).then_inc(sem, 16)


def route(kit, c, r, w_in_dram, w_out_dram, disp, ydram, gates, weights):
    nc, x, wg = kit.nc, c["x"], c["wg"]
    U = 8
    NCH, R = NT // U, 4
    with ExitStack() as ctx:
        sb = lambda n, s, dt=F32: kit.sb(f"r{r}_{n}", s, dt, ctx)
        ps = lambda n, s: kit.ps(f"r{r}_{n}", s, ctx)
        mean, rstd = sb("mean", [P, NT]), sb("rstd", [P, NT])
        tmp = [sb(f"tmp{i}", [P, NT]) for i in range(3)]
        stage = [sb(f"stage{u}", [P, D]) for u in range(U)]
        rows = sb("rows", [P, NT * TOPK * ROW])
        rows4 = rows[:].rearrange("p (t k c) -> p t k c", k=TOPK, c=ROW)
        xnT = [sb(f"xnT{u}", [P, KD, P]) for u in range(R)]
        prob, pick = sb("prob", [P, U, EXP]), sb("pick", [P, U, EXP])
        hot, spot = (sb(n, [P, TOPK, U, EXP]) for n in ("hot", "spot"))
        hot_bf = sb("hot_bf", [P, TOPK, U, EXP], BF16)
        taken = sb("taken", [P, TOPK, EXP])
        best, rk, slot, keep, dest = (sb(n, [P, TOPK, U]) for n in ("best", "rk", "slot", "keep", "dest"))
        den = sb("den", [P, U])
        dest_i = sb("dest_i", [P, NCH * TOPK * U], I32)
        top = [sb(f"top{k}", [P, NT]) for k in range(TOPK)]
        second, place = sb("second", [P, NT * EXP]), sb("place", [P, NT])
        ahead, sums = sb("ahead", [P, NT, EXP]), sb("sums", [P, NT])
        tp = [ps(f"tp{u}", [P, 512]) for u in range(R)]
        lg_ps, within_ps, total_ps = ps("lg", [P, 512]), ps("within", [P, 512]), ps("total", [P, 512])
        lg = lg_ps[:, 0:U * EXP].rearrange("p (t e) -> p t e", e=EXP)
        within = within_ps[:, 0:TOPK * U * EXP].rearrange("p (k t e) -> p k t e", k=TOPK, e=EXP)
        total = total_ps[:, 0:TOPK * EXP].rearrange("p (k e) -> p k e", e=EXP)

        (root_ready, root_done, normed, row_kept, tposed, xnT_ready, logits_done, centred, powered,
         hot_ready, counted, dest_ready, w_loaded, w_split, w_rest, zeroed) = kit.sems_again(
            "route", "root_ready root_done normed row_kept tposed xnT_ready logits_done centred "
            "powered hot_ready counted dest_ready w_loaded w_split w_rest zeroed")
        sent0, sent1 = kit.sems(f"r{r}_sent", "0 1")

        with nc.Block() as block:

            @block.sync
            def _(sp):
                load_weights(nc.sync, weights, w_in_dram, w_out_dram, 0, w_loaded)
                if r == 0:
                    zero = c["blank"][:].rearrange("p (j c) -> p j c", c=ROW)[:, 0:8, 0:D]
                    for q in range(TOPK * NT // 8):
                        sp.wait_ge(dest_ready, q * NCH // (TOPK * NT // 8) + 1)
                        sp.dma_start(ydram[q * 8 * P:(q + 1) * 8 * P, :].rearrange("(p j) c -> p j c", p=P),
                                     zero).then_inc(zeroed, 16)
                    sp.wait_ge(zeroed, 16 * (TOPK * NT // 8))

            @block.gpsimd
            def _(pool):
                link = chain(kit, pool, "pool_step")
                for k in range(TOPK):
                    link(nc.gpsimd.iota(rows4[:, :, k, D].bitcast(I32), pattern=[[P, NT]], base=k * TOK, channel_multiplier=1))
                pool.wait_ge(c["emptied"], 16 * EXP * (r + 1))
                for ch in range(NCH):
                    pool.wait_ge(dest_ready, ch + 1)
                    pool.wait_ge(row_kept, U + (ch + 1) * U)
                    if ch:
                        pool.wait_ge(sent1, 16 * ch * U)
                    for k, sent in enumerate((sent0, sent1)):
                        for u in range(U):
                            at = (ch * TOPK + k) * U + u
                            nc.gpsimd.indirect_dma_start(
                                disp, bass.IndirectOffsetOnAxis(ap=dest_i[:, at:at + 1], axis=0),
                                rows4[:, ch * U + u, k, :], None, bounds_check=EXP * CAP - 1, oob_is_err=False).then_inc(sent, 16)
                for sent in (sent0, sent1):
                    pool.wait_ge(sent, 16 * NT)

            @block.vector
            def _(dve):
                link = chain(kit, dve, "dve_step")
                link(nc.vector.memset(taken[:], 0.0))
                rstd_of(nc, link, mean[:], rstd[:], c["stats"], [a[:] for a in tmp], root_ready, root_done)
                dve.sem_inc(tposed, U)
                dve.sem_inc(row_kept, U)

                def norm(i):
                    for u in range(U):
                        t = i * U + u
                        dve.wait_ge(tposed, t + 1)
                        dve.wait_ge(row_kept, t + 1)
                        nc.vector.tensor_scalar(stage[u][:], x[:, bass.ds(t * D, D)], mean[:, bass.ds(t, 1)],
                                                rstd[:, bass.ds(t, 1)], ALU.subtract, ALU.mult).then_inc(normed, 1)

                def choose(i, link, more):
                    dve.wait_ge(logits_done, R + (i + 1) * U)
                    wide = lambda a: a.unsqueeze(2).to_broadcast([P, U, EXP])
                    link(nc.vector.reduce_max(den[:], lg, AX.X))
                    nc.vector.tensor_tensor(prob[:], lg, wide(den[:]), ALU.subtract).then_inc(centred, 1)
                    dve.wait_ge(powered, i + 1)
                    link(nc.vector.reduce_sum(den[:], prob[:], AX.X))
                    link(nc.vector.reciprocal(den[:], den[:]))
                    link(nc.vector.tensor_tensor(prob[:], prob[:], wide(den[:]), ALU.mult))
                    rank = c["rank"][:].unsqueeze(1).to_broadcast([P, U, EXP])
                    for k in range(TOPK):
                        link(nc.vector.reduce_max(best[:, k, :], prob[:], AX.X))
                        link(nc.vector.tensor_tensor(pick[:], prob[:], wide(best[:, k, :]), ALU.is_ge))
                        link(nc.vector.tensor_tensor(pick[:], pick[:], rank, ALU.mult))
                        link(nc.vector.reduce_max(rk[:, k, :], pick[:], AX.X))
                        link(nc.vector.tensor_tensor(hot[:, k, :, :], rank, wide(rk[:, k, :]), ALU.is_equal))
                        if k == 0:
                            link(nc.vector.scalar_tensor_tensor(prob[:], hot[:, 0, :, :], -2.0, prob[:], ALU.mult, ALU.add))
                    nc.vector.tensor_copy(hot_bf[:], hot[:]).then_inc(hot_ready, 1)
                    if more:
                        norm(i + 1)
                    dve.wait_ge(counted, i + 1)
                    link(nc.vector.tensor_tensor(spot[:], within, taken[:].unsqueeze(2).to_broadcast([P, TOPK, U, EXP]), ALU.add))
                    link(nc.vector.tensor_tensor(taken[:], taken[:], total, ALU.add))
                    link(nc.vector.tensor_tensor(spot[:], spot[:], hot[:], ALU.mult))
                    link(nc.vector.reduce_sum(slot[:], spot[:], AX.X))
                    link(nc.vector.tensor_tensor(pick[:], hot[:, 1, :, :], taken[:, 0, :].unsqueeze(1).to_broadcast([P, U, EXP]), ALU.mult))
                    link(nc.vector.reduce_sum(den[:], pick[:], AX.X))
                    link(nc.vector.tensor_tensor(den[:], den[:], slot[:, 1, :], ALU.add))
                    link(nc.vector.tensor_scalar(keep[:, 0, :], slot[:, 0, :], float(CAP), None, ALU.is_lt))
                    link(nc.vector.tensor_scalar(keep[:, 1, :], den[:], float(CAP), None, ALU.is_lt))
                    none = float(EXP * CAP + NOWHERE)
                    link(nc.vector.tensor_scalar(dest[:, 0, :], rk[:, 0, :], -float(CAP), none, ALU.mult, ALU.add))
                    link(nc.vector.tensor_scalar(dest[:, 1, :], rk[:, 1, :], -float(CAP), none + CAP - 1, ALU.mult, ALU.add))
                    link(nc.vector.tensor_tensor(dest[:, 0, :], dest[:, 0, :], slot[:, 0, :], ALU.add))
                    link(nc.vector.tensor_tensor(dest[:, 1, :], dest[:, 1, :], slot[:, 1, :], ALU.subtract))
                    link(nc.vector.scalar_tensor_tensor(dest[:], keep[:], -float(NOWHERE), dest[:], ALU.mult, ALU.add))
                    flat = lambda a: a.rearrange("p a b -> p (a b)")
                    nc.vector.tensor_scalar(dest_i[:, bass.ds(i * (TOPK * U), TOPK * U)], flat(dest[:]), 1.0, None,
                                            ALU.mult).then_inc(dest_ready, 1)
                    tiles = bass.ds(i * U, U)
                    link(nc.vector.tensor_tensor(top[0][:, tiles], best[:, 0, :], keep[:, 0, :], ALU.mult))
                    link(nc.vector.tensor_scalar(top[1][:, tiles], best[:, 1, :], 1.0, None, ALU.mult))
                    link(nc.vector.tensor_scalar(place[:, tiles], slot[:, 1, :], 1.0, None, ALU.mult))
                    link(nc.vector.tensor_scalar(second[:, bass.ds(i * (U * EXP), U * EXP)], flat(hot[:, 1, :, :]), 1.0, None, ALU.mult))

                STEPS = 33
                norm(0)
                with nc.vector.Fori(0, NCH - 1) as i:
                    link = loop_chain(kit, dve, "dve_step", i, STEPS)
                    choose(i, link, True)
                loop_done(kit, "dve_step", link, NCH - 1, STEPS)
                choose(NCH - 1, chain(kit, dve, "dve_step"), False)
                link = chain(kit, dve, "dve_step")
                link(nc.vector.tensor_tensor(ahead[:], second[:].rearrange("p (t e) -> p t e", e=EXP),
                                             taken[:, 0, :].unsqueeze(1).to_broadcast([P, NT, EXP]), ALU.mult))
                link(nc.vector.reduce_sum(sums[:], ahead[:], AX.X))
                link(nc.vector.tensor_tensor(place[:], place[:], sums[:], ALU.add))
                link(nc.vector.tensor_scalar(place[:], place[:], float(CAP), None, ALU.is_lt))
                link(nc.vector.tensor_tensor(top[1][:], top[1][:], place[:], ALU.mult))
                link(nc.vector.tensor_tensor(sums[:], top[0][:], top[1][:], ALU.add))
                link(nc.vector.tensor_scalar(sums[:], sums[:], 1e-9, None, ALU.max))
                link(nc.vector.reciprocal(sums[:], sums[:]))
                link(nc.vector.tensor_scalar(sums[:], sums[:], 0.5, None, ALU.mult))
                for k in range(TOPK):
                    link(nc.vector.tensor_tensor(gates[:, k, :], top[k][:], sums[:], ALU.mult))
                dve.wait_ge(w_split, 1)
                nc.vector.tensor_tensor(weights["lo"][0][:], weights["raw"][:], weights["hi"][0][:].bitcast(F32),
                                        ALU.subtract).then_inc(w_rest, 1)

            @block.scalar
            def _(act):
                act.wait_ge(root_ready, 1)
                nc.scalar.activation(rstd[:], tmp[2][:], ACT.Sqrt).then_inc(root_done, 1)
                act.sem_inc(logits_done, R)
                with nc.scalar.Fori(0, NCH) as i:
                    for u in range(U):
                        t = i * U + u
                        act.wait_ge(tposed, t + 1 + U)
                        act.wait_ge(logits_done, t + 1)
                        nc.scalar.copy(xnT[u % R][:].rearrange("p k q -> p (k q)"), tp[u % R][:, 0:D]).then_inc(xnT_ready, 1)
                        nc.scalar.copy(rows[:, bass.ds(t * (TOPK * ROW), TOPK * ROW)].rearrange("p (k c) -> p k c", k=TOPK)[:, :, 0:D],
                                       stage[u][:].unsqueeze(1).to_broadcast([P, TOPK, D])).then_inc(row_kept, 1)
                    act.wait_ge(centred, i + 2)
                    nc.scalar.activation(prob[:], prob[:], ACT.Exp).then_inc(powered, 1)
                act.wait_ge(w_loaded, 32)
                nc.scalar.copy(weights["hi"][0][:], weights["raw"][:]).then_inc(w_split, 1)

            @block.tensor
            def _(pe):
                pe.sem_inc(xnT_ready, R)
                pe.sem_inc(centred, 1)

                def transposes(t, u):
                    pe.wait_ge(normed, t + 1)
                    pe.wait_ge(xnT_ready, t + 1)
                    for k in range(KD):
                        last = nc.tensor.transpose(tp[u % R][:, k * P:(k + 1) * P], stage[u][:, k * P:(k + 1) * P], c["ident"][:])
                    last.then_inc(tposed, 1)

                def project(t, u):
                    pe.wait_ge(xnT_ready, t + R + 1)
                    for k in range(KD):
                        last = nc.tensor.matmul(lg[:, u, :], xnT[u % R][:, k, :], wg[:, k, :], start=(k == 0), stop=(k == KD - 1))
                    last.then_inc(logits_done, 1)

                with nc.tensor.Fori(0, NCH) as i:
                    transposes(i * U, 0)
                    transposes(i * U + 1, 1)
                    pe.wait_ge(centred, i + 1)
                    for u in range(U):
                        if u + 2 < U:
                            transposes(i * U + u + 2, u + 2)
                        project(i * U + u, u)
                    pe.wait_ge(hot_ready, i + 1)
                    nc.tensor.matmul(within, c["before_bf"][:], hot_bf[:], start=True, stop=False)
                    for u in range(U - 1):
                        nc.tensor.matmul(within[:, :, u + 1:, :], c["ones_bf"][:],
                                         hot_bf[:, :, u, :].unsqueeze(2).to_broadcast([P, TOPK, U - 1 - u, EXP]),
                                         start=False, stop=(u == U - 2))
                    for u in range(U):
                        last = nc.tensor.matmul(total, c["ones_bf"][:], hot_bf[:, :, u, :], start=(u == 0), stop=(u == U - 1))
                    last.then_inc(counted, 1)


def experts(kit, c, r, w_in_dram, w_out_dram, disp, next_disp, ydram, spare, weights):
    nc = kit.nc
    with ExitStack() as ctx:
        sb = lambda n, s, dt=F32: kit.sb(f"e{r}_{n}", s, dt, ctx)
        ps = lambda n, s: kit.ps(f"e{r}_{n}", s, ctx)
        w_raw, w_hi, w_lo = weights["raw"], weights["hi"], weights["lo"]
        slots = [sb(f"slots{u}", [P, ST * ROW]) for u in range(2)]
        s_hi, s_lo = sb("s_hi", [P, KD, CAP], F32R), sb("s_lo", [P, KD, CAP], F32R)
        act_a = [sb(f"act_a{u}", [P, 512]) for u in range(2)]
        hid = [sb(f"hid{u}", [P, 512]) for u in range(2)]
        h_hi = [sb(f"h_hi{u}", [P, KF, 512], F32R) for u in range(2)]
        h_lo = [sb(f"h_lo{u}", [P, KF, 512], F32R) for u in range(2)]
        res = [sb(f"res{u}", [P, D]) for u in range(4)]
        tp = ps("tp", [P, KD, 512])
        a_ps = [ps(f"a{u}", [P, 512]) for u in range(2)]
        g_ps = [ps(f"g{u}", [P, 512]) for u in range(2)]
        o_ps = [ps(f"o{u}", [P, 512]) for u in range(2)]
        (w_loaded, w_split, w_rest, s_tposed, s_hi_done, s_lo_done, a_done, g_done, gelu_done, hid_done,
         h_hi_done, h_lo_done, o_done, res_ready, slots_free) = kit.sems_again(
            "experts", "w_loaded w_split w_rest s_tposed s_hi_done s_lo_done a_done g_done gelu_done hid_done "
            "h_hi_done h_lo_done o_done res_ready slots_free")
        slots_in = kit.sems_again("experts_slots_in", "0 1")
        y_sent = kit.sems(f"e{r}_y_sent", "0 1 2 3")
        NC, NW = len(CHUNKS), len(W_PARTS)
        w_in_at = lambda w, k, f: w[:, k * 2 * FF + f * P:k * 2 * FF + (f + 1) * P]
        w_out_at = lambda w, k: w[:, NIN + k * D:NIN + (k + 1) * D]
        HID0, O0, RES0, Y0 = 2, 2 * ST, 2, 16
        RB = len(res)
        sent_in = lambda q, n: len([m for m in range(n) if m % RB == q])
        BODY = 2 * ST
        SENT = sent_in(0, BODY) * 16
        assert all(sent_in(q, BODY) * 16 == SENT for q in range(RB))
        m_ = lambda u, ci, f: (u * NC + ci) * KF + f

        def in_turn(eng, body):
            with eng.Fori(0, EXP // 2 - 1) as i:
                body(i, 0, True)
                body(i, 1, True)
            body(EXP // 2 - 1, 0, True)
            body(EXP // 2 - 1, 1, False)

        with nc.Block() as block:

            @block.sync
            def _(sp):
                sp.sem_inc(w_rest, NW)
                disp_v = disp.rearrange("(q j) c -> q (j c)", j=ST)

                def load_slots(e, u):
                    sp.dma_start(slots[u][:], disp_v[bass.ds(e * P, P), :]).then_inc(slots_in[u], 16)

                def load_next(e, u, first=False):
                    sp.wait_ge(w_rest, e * NW)
                    load_weights(nc.sync, weights, w_in_dram, w_out_dram, e, w_loaded)
                    if not first:
                        sp.wait_ge(slots_free, e)
                    load_slots(e, u)

                load_slots(0, 0)
                def empty_next(e):
                    if next_disp is not None:
                        empty_slots(nc.sync, c, next_disp, e, c["emptied"])

                load_next(1, 1, first=True)
                with nc.sync.Fori(0, EXP // 2 - 1) as i:
                    load_next(i * 2 + 2, 0)
                    empty_next(i * 2)
                    load_next(i * 2 + 3, 1)
                    empty_next(i * 2 + 1)
                for e in range(EXP - 2, EXP):
                    empty_next(e)

            @block.gpsimd
            def _(pool):
                last_row = nc.gpsimd.to_reg(TOPK * TOK - 1)
                link = chain(kit, pool, "pool_step")
                for q in range(RB):
                    link(nc.gpsimd.memset(res[q][:], 0.0))
                for q in range(RB):
                    nc.gpsimd.dma_start(spare[q], res[q][:, 0:16]).then_inc(y_sent[q], Y0)

                def body(i, u, more):
                    e = i * 2 + u

                    def rests(ci):
                        n = CHUNKS[ci][1]
                        for f in range(KF):
                            m = e * NC * KF + ci * KF + f
                            pool.wait_ge(h_hi_done, m + 1)
                            hh = h_hi[(u * NC + ci) % 2][:, f, 0:n]
                            nc.gpsimd.tensor_tensor(h_lo[(u * NC + ci) % 2][:, f, 0:n], hid[m_(u, ci, f) % 2][:, 0:n],
                                                    hh.bitcast(F32), ALU.subtract).then_inc(h_lo_done, 1)

                    def send(ci):
                        c0, n = CHUNKS[ci]
                        for j in range(c0 // P, (c0 + n) // P):
                            pool.wait_ge(res_ready, e * ST + j + 1 + RES0)
                            kit.part(pool)
                            at = bass.IndirectOffsetOnAxis(
                                ap=slots[u][:, j * ROW + D:j * ROW + D + 1].bitcast(I32), axis=0)
                            nc.gpsimd.indirect_dma_start(ydram, at, res[(u * ST + j) % RB][:], None,
                                                         bounds_check=last_row,
                                                         oob_is_err=False).then_inc(y_sent[(u * ST + j) % RB], 16)

                    rests(0)
                    for q in range(RB):
                        pool.wait_ge(y_sent[q], Y0 + i * SENT + sent_in(q, u * ST) * 16)
                    pool.sem_inc(slots_free, 1)
                    rests(1)
                    send(0)
                    rests(2)
                    send(1)
                    send(2)

                in_turn(nc.gpsimd, body)
                for q in range(RB):
                    pool.wait_ge(y_sent[q], Y0 + EXP // 2 * SENT)

            @block.vector
            def _(dve):
                dve.sem_inc(o_done, O0)

                def slots_lo(e, ci):
                    c0, n = CHUNKS[ci]
                    dve.wait_ge(s_hi_done, e * NC + ci + 1)
                    nc.vector.tensor_tensor(s_lo[:, :, c0:c0 + n], tp[:, :, 0:n],
                                            s_hi[:, :, c0:c0 + n].bitcast(F32), ALU.subtract).then_inc(s_lo_done, 1)

                def body(i, u, more):
                    e = i * 2 + u

                    def hidden(ci):
                        n = CHUNKS[ci][1]
                        h = (u * NC + ci) % 2
                        c0 = CHUNKS[ci - 2][0] + CHUNKS[ci - 2][1] - (0 if ci >= 2 else CAP)
                        dve.wait_ge(o_done, e * ST + c0 // P + O0)
                        for f in range(KF):
                            m = e * NC * KF + ci * KF + f
                            q = m_(u, ci, f) % 2
                            dve.wait_ge(gelu_done, m + 1)
                            dve.wait_ge(g_done, m + 1)
                            dve.wait_ge(h_lo_done, m + 1)
                            nc.vector.tensor_tensor(hid[q][:, 0:n], act_a[q][:, 0:n], g_ps[q][:, 0:n],
                                                    ALU.mult).then_inc(hid_done, 1)
                            dve.wait_ge(hid_done, m + 1 + HID0)
                            nc.vector.tensor_copy(h_hi[h][:, f, 0:n], hid[q][:, 0:n]).then_inc(h_hi_done, 1)

                    def weights_rest(z):
                        a, b = W_PARTS[z]
                        dve.wait_ge(w_split, e * NW + z + 1)
                        nc.vector.tensor_tensor(w_lo[1 - u][:, a:b], w_raw[:, a:b], w_hi[1 - u][:, a:b].bitcast(F32),
                                                ALU.subtract).then_inc(w_rest, 1)

                    hidden(0)
                    slots_lo(e, 2)
                    if more:
                        weights_rest(0)
                    hidden(1)
                    if more:
                        weights_rest(1)
                        weights_rest(2)
                    hidden(2)
                    if more:
                        slots_lo(e + 1, 0)
                        slots_lo(e + 1, 1)

                slots_lo(0, 0)
                slots_lo(0, 1)
                in_turn(nc.vector, body)

            @block.scalar
            def _(act):
                act.sem_inc(hid_done, HID0)
                act.sem_inc(h_lo_done, HID0)

                def slots_hi(e, ci):
                    c0, n = CHUNKS[ci]
                    act.wait_ge(s_tposed, e * NC + ci + 1)
                    nc.scalar.copy(s_hi[:, :, c0:c0 + n], tp[:, :, 0:n]).then_inc(s_hi_done, 1)

                def body(i, u, more):
                    e = i * 2 + u

                    def gelu(ci):
                        n = CHUNKS[ci][1]
                        for f in range(KF):
                            m = e * NC * KF + ci * KF + f
                            q = m_(u, ci, f) % 2
                            act.wait_ge(a_done, m + 1)
                            act.wait_ge(hid_done, m + 1)
                            nc.scalar.activation(act_a[q][:, 0:n], a_ps[q][:, 0:n], ACT.Gelu).then_inc(gelu_done, 1)

                    def results(ci):
                        c0, n = CHUNKS[ci]
                        for j in range(c0 // P, (c0 + n) // P):
                            m = e * ST + j
                            act.wait_ge(o_done, m + 1 + O0)
                            b = u * ST + j
                            act.wait_ge(y_sent[b % RB], Y0 + SENT * i + b // RB * 16)
                            nc.scalar.copy(res[b % RB][:], o_ps[(u * ST + j) % 2][:, 0:D]).then_inc(res_ready, 1)

                    def weights_high(z):
                        a, b = W_PARTS[z]
                        if z == 0:
                            act.wait_ge(w_loaded, (e + 1) * 32)
                            act.wait_ge(o_done, e * ST + O0)
                        nc.scalar.copy(w_hi[1 - u][:, a:b], w_raw[:, a:b]).then_inc(w_split, 1)

                    gelu(0)
                    slots_hi(e, 2)
                    if more:
                        weights_high(0)
                    gelu(1)
                    if more:
                        weights_high(1)
                    results(0)
                    if more:
                        weights_high(2)
                    gelu(2)
                    if more:
                        slots_hi(e + 1, 0)
                    results(1)
                    if more:
                        slots_hi(e + 1, 1)
                    results(2)

                slots_hi(0, 0)
                slots_hi(0, 1)
                in_turn(nc.scalar, body)

            @block.tensor
            def _(pe):
                pe.sem_inc(s_lo_done, 1)
                pe.sem_inc(res_ready, RES0)

                def transposes(e, u, tile, ci):
                    c0, n = CHUNKS[ci]
                    if ci == 0:
                        pe.wait_ge(slots_in[u], (tile + 1) * 16)
                    pe.wait_ge(s_lo_done, e * NC + ci + 1)
                    for j in range(n // P):
                        for k in range(KD):
                            at = (c0 // P + j) * ROW + k * P
                            last = nc.tensor.transpose(tp[:, k, j * P:(j + 1) * P], slots[u][:, at:at + P], c["ident"][:])
                    last.then_inc(s_tposed, 1)

                def body(i, u, more):
                    e = i * 2 + u

                    def up(ci):
                        c0, n = CHUNKS[ci]
                        pe.wait_ge(s_lo_done, e * NC + ci + 2)
                        if ci == 0:
                            pe.wait_ge(w_rest, (e + 1) * NW)
                        for f in range(KF):
                            m = e * NC * KF + ci * KF + f
                            q = m_(u, ci, f) % 2
                            pe.wait_ge(hid_done, m + 1)
                            for half, bank, done in ((0, a_ps, a_done), (KF, g_ps, g_done)):
                                terms = [(w, s, k) for k in range(KD)
                                         for w, s in ((w_hi[u], s_hi), (w_hi[u], s_lo), (w_lo[u], s_hi))]
                                for z, (w, s, k) in enumerate(terms):
                                    last = nc.tensor.matmul(bank[q][:, 0:n], w_in_at(w, k, half + f),
                                                            s[:, k, c0:c0 + n], start=(z == 0),
                                                            stop=(z == len(terms) - 1))
                                last.then_inc(done, 1)

                    def down(ci):
                        c0, n = CHUNKS[ci]
                        h = (u * NC + ci) % 2
                        pe.wait_ge(h_lo_done, e * NC * KF + (ci + 1) * KF + HID0)
                        for j in range(n // P):
                            m = e * ST + c0 // P + j
                            pe.wait_ge(res_ready, m + 1)
                            terms = [(w, s, k) for k in range(KF)
                                     for w, s in ((w_hi[u], h_hi[h]), (w_lo[u], h_hi[h]), (w_hi[u], h_lo[h]))]
                            for z, (w, s, k) in enumerate(terms):
                                last = nc.tensor.matmul(o_ps[(u * ST + c0 // P + j) % 2][:, 0:D],
                                                        s[:, k, j * P:(j + 1) * P], w_out_at(w, k),
                                                        start=(z == 0), stop=(z == len(terms) - 1))
                            last.then_inc(o_done, 1)

                    next_tile = i + u
                    up(0)
                    transposes(e, u, i, 2)
                    up(1)
                    down(0)
                    up(2)
                    if more:
                        transposes(e + 1, 1 - u, next_tile, 0)
                    down(1)
                    if more:
                        transposes(e + 1, 1 - u, next_tile, 1)
                    down(2)

                transposes(0, 0, 0, 0)
                transposes(0, 0, 0, 1)
                in_turn(nc.tensor, body)


def combine(kit, c, r, ydram, gates, out_dram, proj=None):
    nc, x = kit.nc, c["x"]
    U, NB = 4, 4
    with ExitStack() as ctx:
        y = [kit.sb(f"c{r}_y{u}", [P, TOPK, U, D], F32, ctx) for u in range(NB)]
        scaled, first, mixed, stored, stats_done = kit.sems_again("combine", "scaled first mixed stored stats_done")
        y_in = kit.sems_again("combine_y_in", "0 1 2 3")
        gate = lambda k, t: gates[:].rearrange("p k t -> p (k t)")[:, bass.ds(t + k * NT, 1)]
        with nc.Block() as block:

            @block.sync
            def _(sp):
                yv = ydram.rearrange("(k t p) d -> p k t d", k=TOPK, p=P)

                def load(s, u):
                    for k in range(TOPK):
                        sp.dma_start(y[u][:, k, :, :], yv[:, k, bass.ds(s * U, U), :]).then_inc(y_in[u], 16)

                def store(s):
                    if out_dram is not None:
                        sp.dma_start(out_dram.rearrange("(t p) d -> p t d", p=P)[:, bass.ds(s * U, U), :],
                                     x[:].rearrange("p (t d) -> p t d", d=D)[:, bass.ds(s * U, U), :]).then_inc(stored, 16)

                for u in range(NB):
                    load(u, u)
                if proj is not None:
                    load_projections(sp, proj)
                with nc.sync.Fori(0, NT // U // NB - 1) as i:
                    for u in range(NB):
                        s = i * NB + u
                        sp.wait_ge(mixed, (s + 1) * U)
                        load(s + NB, u)
                        store(s)
                for s in range(NT // U - NB, NT // U):
                    sp.wait_ge(mixed, (s + 1) * U)
                    store(s)
                if out_dram is not None:
                    sp.wait_ge(stored, NT // U * 16)

            @block.gpsimd
            def _(pool):
                if proj is not None:
                    nc.gpsimd.memset(proj["raw"][:, PROJ_W:], 0.0).then_inc(proj["j_zero"], 1)
                with nc.gpsimd.Fori(0, NT // U // NB) as i:
                    for u in range(NB):
                        s = i * NB + u
                        pool.wait_ge(scaled, (s + 1) * U)
                        kit.part(pool)
                        xs = x[:, bass.ds(s * (U * D), U * D)]
                        nc.gpsimd.tensor_tensor(xs, xs, y[u][:, 0, :, :].rearrange("p t d -> p (t d)"), ALU.add).then_inc(first, 1)

            @block.vector
            def _(dve):
                with nc.vector.Fori(0, NT // U // NB) as i:
                    for u in range(NB):
                        s = i * NB + u
                        dve.wait_ge(y_in[u], (i + 1) * 16 * TOPK)
                        dve.wait_ge(first, s + 1)
                        for v in range(U):
                            t = s * U + v
                            xt = x[:, bass.ds(t * D, D)]
                            nc.vector.scalar_tensor_tensor(xt, y[u][:, 1, v, :], gate(1, t), xt, ALU.mult, ALU.add).then_inc(mixed, 1)
                        if out_dram is None:
                            dve.wait_ge(mixed, (s + 1) * U)
                            for v in range(U):
                                tile_stats(nc, c, s * U + v).then_inc(stats_done, 1)
                if out_dram is None:
                    dve.wait_ge(stats_done, NT)
                if proj is not None:
                    dve.wait_ge(proj["split"], 1)
                    nc.vector.tensor_tensor(proj["lo"][:], proj["raw"][:], proj["hi"][:].bitcast(F32), ALU.subtract).then_inc(proj["split"], 1)
                    nc.vector.tensor_scalar(proj["bias"][:, 2, :], proj["bias"][:, 0, :], 0.25, None, ALU.mult).then_inc(proj["split"], 1)

            @block.scalar
            def _(act):
                with nc.scalar.Fori(0, NT // U // NB) as i:
                    for u in range(NB):
                        s = i * NB + u
                        act.wait_ge(y_in[u], (i + 1) * 16 * TOPK)
                        for v in range(U):
                            nc.scalar.activation(y[u][:, 0, v, :], y[u][:, 0, v, :], ACT.Copy, scale=gate(0, s * U + v)).then_inc(scaled, 1)
                if proj is not None:
                    act.wait_ge(proj["in"], proj["loads"] * 16)
                    nc.scalar.copy(proj["hi"][:], proj["raw"][:]).then_inc(proj["split"], 1)


PROJ_W = 3 * KD * D


def projections(kit, ctx, w):
    sb = lambda n, s, dt=F32: kit.sb(f"q_{n}", s, dt, ctx)
    proj = {"w": w, "raw": sb("w_raw", [P, PROJ_W + KD * P]), "loads": 3 + 2 * KD + 2 + HEADS,
            "hi": sb("w_hi", [P, PROJ_W + KD * P], F32R), "lo": sb("w_lo", [P, PROJ_W + KD * P], F32R),
            "bias": sb("bias", [P, 3, KD]),
            "bv": sb("bv", [P, D]), "lam": sb("lam", [P, 1])}
    proj["in"], proj["split"], proj["j_zero"] = kit.sems("q", "w_in w_split j_zero")
    return proj


def load_projections(eng, proj):
    w, loaded = proj["w"], proj["in"]
    for m, name in enumerate(("WqT", "WkT", "WvT")):
        eng.dma_start(proj["raw"][:, m * KD * D:(m + 1) * KD * D].rearrange("p (k e) -> p k e", k=KD),
                      w[name].rearrange("(k p) e -> p k e", p=P)).then_inc(loaded, 16)
    for m, name in enumerate(("bq", "bk")):
        for k in range(KD):
            eng.dma_start(proj["bias"][:, m, k:k + 1], w[name][k * P:(k + 1) * P].rearrange("(p o) -> p o", o=1)).then_inc(loaded, 16)
    eng.dma_start(proj["bv"][:], w["bv"].partition_broadcast(P)).then_inc(loaded, 16)
    eng.dma_start(proj["lam"][:], w["lam"].partition_broadcast(P)).then_inc(loaded, 16)
    eng.wait_ge(proj["j_zero"], 1)
    for h in range(HEADS):
        r0 = h * HD % P
        eng.dma_start(proj["raw"][r0:r0 + HD, PROJ_W + h * HD:PROJ_W + (h + 1) * HD], w["J"][h]).then_inc(loaded, 16)


def load_group(eng, group, packs, v_dram, gi, sem):
    qp, kp, vg = group
    for block_row, (qa, ka) in enumerate(((0, 4), (0, 5), (1, 4), (2, 6), (2, 7), (3, 6))):
        for t, a in ((qp, qa), (kp, ka)):
            eng.dma_start(t[block_row * HD:(block_row + 1) * HD, :, :].bitcast(F32),
                          packs[a].rearrange("b (g j r) c -> (b g) r j c", g=NG, j=GH)[bass.ds(gi, 1), :, :, :]
                          .rearrange("o r j c -> (o r) j c")).then_inc(sem, 16)
    eng.dma_start(vg[:].rearrange("p t h c -> p t (h c)"),
                  v_dram[bass.ds(gi, 1), :, :, :].rearrange("o t p c -> p (o t) c")).then_inc(sem, 16)


GROUP_LOADS = 13


def group_tiles(kit, ctx, u):
    return (kit.sb(f"a_qp{u}", [PACK + 1, GH, SEQ], F32R, ctx), kit.sb(f"a_kp{u}", [PACK + 1, GH, SEQ], F32R, ctx),
            kit.sb(f"a_vg{u}", [P, KT, GH, HP], F32, ctx))


def project(kit, c, proj, packs, v_dram, group, group_in):
    nc, x = kit.nc, c["x"]
    U = QC // P
    with ExitStack() as ctx:
        sb = lambda n, s, dt=F32: kit.sb(f"q_{n}", s, dt, ctx)
        ps = lambda n, s: kit.ps(f"q_{n}", s, ctx)
        mean, rstd = sb("mean", [P, NT]), sb("rstd", [P, NT])
        tmp = [sb(f"tmp{i}", [P, NT]) for i in range(3)]
        w_hi, w_lo, bias, bv, lam = (proj[n] for n in ("hi", "lo", "bias", "bv", "lam"))
        stage = [sb(f"stage{u}", [P, D]) for u in range(U)]
        x_hi, x_lo = ([sb(f"{n}{u}", [P, KD, QC], F32R) for u in range(2)] for n in ("x_hi", "x_lo"))
        full = {n: [sb(f"{n}{u}", [P, QC]) for u in range(KD)] for n in ("q", "tq", "t", "k", "tk")}
        tq_hi, tq_lo = ([sb(f"{n}{u}", [P, QC], F32R) for u in range(KD)] for n in ("tq_hi", "tq_lo"))
        pack = [sb(f"pack{u}", [P, 8, QC], F32R) for u in range(KD)]
        vals = sb("vals", [P, U, HEADS, HP])
        tp = ps("tp", [P, KD, QC])
        y_ps = [ps(f"y{u}", [P, QC]) for u in range(2)]
        t_ps = [ps(f"t{u}", [P, QC]) for u in range(KD)]
        v_ps = [ps(f"v{u}", [P, QC]) for u in range(2)]
        (v_ready, root_ready, root_done, normed, tposed, x_hi_done, x_lo_done,
         y_done, full_done, hi_done, lo_done, tq_rest, t_done, t_read, v_done, v_read, v_out, pool_lo) = kit.sems(
            "q", "v_ready root_ready root_done normed tposed x_hi_done x_lo_done "
            "y_done full_done hi_done lo_done tq_rest t_done t_read v_done v_read v_out pool_lo")
        q_out, k_out = kit.sems("q_q_out", "0 1"), kit.sems("q_k_out", "0 1")
        wt = lambda a, m, k, e0, n: a[:, (m * KD + k) * D + e0:(m * KD + k) * D + e0 + n]
        jt = lambda a, g: a[:, PROJ_W + g * P:PROJ_W + (g + 1) * P]
        Q_HI, Q_LO, T_HI, T_LO, K_HI, K_LO, TK_HI, TK_LO = range(8)

        def in_turn(eng, body):
            with eng.Fori(0, BATCH - 1) as b:
                body(b, True)
            body(BATCH - 1, False)

        with nc.Block() as block:

            @block.sync
            def _(sp):
                for sem, n in ((pool_lo, 6), (tq_rest, 2), (lo_done, 2), (t_read, 2), (full_done, 8), (v_out, 16)) + tuple((out, 16) for out in q_out + k_out):
                    sp.sem_inc(sem, n)
                def body(b):
                    for half in range(2):
                        i = b * 2 + half
                        for g in range(KD):
                            to = packs.rearrange("a b (g p) c -> b g p a c", p=P)[bass.ds(b, 1), g, :, :, half * QC:(half + 1) * QC]
                            sp.wait_ge(pool_lo, 6 + (i + 1) * 6 - (3 if g == 0 else 0))
                            kit.part(sp)
                            sp.dma_start(to[:, :, K_HI:, :].rearrange("o p a c -> (o p) a c"),
                                         pack[g][:, K_HI:, :].bitcast(F32)).then_inc(k_out[g], 16)
                            sp.wait_ge(lo_done, 2 + (i + 1) * 2 - (1 if g == 0 else 0))
                            kit.part(sp)
                            sp.dma_start(to[:, :, :K_HI, :].rearrange("o p a c -> (o p) a c"),
                                         pack[g][:, :K_HI, :].bitcast(F32)).then_inc(q_out[g], 16)
                        sp.wait_ge(v_read, (i + 1) * U + 2)
                        for g in range(NG):
                            sp.dma_start(v_dram.rearrange("(b g) t p c -> b g t p c", g=NG)
                                         [bass.ds(b, 1), g, half * U:(half + 1) * U, :, :].rearrange("o t p c -> p (o t) c"),
                                         vals[:, :, g * GH:(g + 1) * GH, :].rearrange("p u h c -> p u (h c)")).then_inc(v_out, 16)

                with nc.sync.Fori(0, BATCH // 2) as b:
                    body(b)
                for out in q_out + k_out:
                    sp.wait_ge(out, 16 + BATCH // 2 * 2 * 16)
                sp.wait_ge(v_out, 16 + BATCH // 2 * 2 * NG * 16)
                load_group(nc.sync, group, packs, v_dram, 0, group_in)
                with nc.sync.Fori(BATCH // 2, BATCH) as b:
                    body(b)
                for out in q_out + k_out:
                    sp.wait_ge(out, 16 + 2 * BATCH * 16)
                sp.wait_ge(v_out, 16 + 2 * BATCH * NG * 16)

            @block.gpsimd
            def _(pool):
                nc.gpsimd.memset(vals[:], 0.0).then_inc(v_ready, 1)
                pool.wait_ge(v_ready, 1)
                nc.gpsimd.memset(vals[:, :, :, HD:HD + 1], 1.0).then_inc(v_ready, 1)
                with nc.gpsimd.Fori(0, 2 * BATCH) as i:
                    for g in range(KD):
                        for n, (name, hi, lo) in enumerate((("q", Q_HI, Q_LO), ("k", K_HI, K_LO), ("tk", TK_HI, TK_LO))):
                            pool.wait_ge(hi_done, i * 10 + g * 5 + (1, 3, 4)[n])
                            nc.gpsimd.tensor_tensor(pack[g][:, lo, :], full[name][g][:], pack[g][:, hi, :].bitcast(F32),
                                                    ALU.subtract).then_inc(pool_lo, 1)

            @block.vector
            def _(dve):
                link = chain(kit, dve, "dve_step")
                rstd_of(nc, link, mean[:], rstd[:], c["stats"], [a[:] for a in tmp], root_ready, root_done)
                dve.wait_ge(v_ready, 2)
                dve.sem_inc(tposed, 1)

                def norm(i):
                    dve.wait_ge(tposed, i + 1)
                    for u in range(U):
                        t = i * U + u
                        nc.vector.tensor_scalar(stage[u][:], x[:, bass.ds(t * D, D)],
                                                mean[:, bass.ds(t, 1)], rstd[:, bass.ds(t, 1)],
                                                ALU.subtract, ALU.mult).then_inc(normed, 1)

                def x_rest(i, half):
                    dve.wait_ge(x_hi_done, i + 1)
                    nc.vector.tensor_tensor(x_lo[half][:], tp[:], x_hi[half][:].bitcast(F32), ALU.subtract).then_inc(x_lo_done, 1)

                def splits(i, g):
                    for n, (name, to) in enumerate((("q", pack[g][:, Q_HI, :]), ("tq", tq_hi[g][:]),
                                                    ("k", pack[g][:, K_HI, :]), ("tk", pack[g][:, TK_HI, :]))):
                        dve.wait_ge(full_done, 8 + i * 8 + g * 4 + n + 1)
                        if name in "qk":
                            kit.part(dve)
                            dve.wait_ge((q_out if name == "q" else k_out)[g], 16 + i * 16)
                        nc.vector.tensor_copy(to, full[name][g][:]).then_inc(hi_done, 1)
                        if name == "tq":
                            dve.wait_ge(hi_done, i * 10 + g * 5 + 2)
                            nc.vector.tensor_tensor(tq_lo[g][:], full["tq"][g][:], tq_hi[g][:].bitcast(F32),
                                                    ALU.subtract).then_inc(tq_rest, 1)

                def tangents(i, g):
                    dve.wait_ge(t_done, i * 2 + g + 1)
                    dve.wait_ge(lo_done, i * 2 + 2)
                    nc.vector.tensor_scalar(full["t"][g][:], t_ps[g][:], lam[:, 0:1], None, ALU.mult).then_inc(t_read, 1)
                    dve.wait_ge(t_read, i * 2 + g + 1 + 2)
                    nc.vector.tensor_copy(pack[g][:, T_HI, :], full["t"][g][:]).then_inc(hi_done, 1)
                    dve.wait_ge(hi_done, i * 10 + g * 5 + 5)
                    nc.vector.tensor_tensor(pack[g][:, T_LO, :], full["t"][g][:], pack[g][:, T_HI, :].bitcast(F32),
                                            ALU.subtract).then_inc(lo_done, 1)

                def body(b, more):
                    for half in range(2):
                        i = b * 2 + half
                        go_on = more or half == 0
                        if go_on:
                            norm(i + 1)
                        splits(i, 0)
                        tangents(i, 0)
                        if go_on:
                            x_rest(i + 1, 1 - half)
                        splits(i, 1)
                        tangents(i, 1)
                        dve.wait_ge(v_out, 16 + i * NG * 16)
                        for u in range(U):
                            dve.wait_ge(v_done, i * U + u + 1)
                            nc.vector.tensor_tensor(vals[:, u, :, 0:HD], v_ps[u % 2][:, 0:D].rearrange("p (h c) -> p h c", c=HD),
                                                    bv[:].rearrange("p (h c) -> p h c", c=HD), ALU.add).then_inc(v_read, 1)

                norm(0)
                x_rest(0, 0)
                in_turn(nc.vector, body)

            @block.scalar
            def _(act):
                act.wait_ge(root_ready, 1)
                nc.scalar.activation(rstd[:], tmp[2][:], ACT.Sqrt).then_inc(root_done, 1)

                def x_high(i, half):
                    act.wait_ge(tposed, i + 2)
                    nc.scalar.copy(x_hi[half][:], tp[:]).then_inc(x_hi_done, 1)

                def body(b, more):
                    for half in range(2):
                        i = b * 2 + half
                        for g in range(KD):
                            if g == 1 and (more or half == 0):
                                x_high(i + 1, 1 - half)
                            for m in range(2):
                                n = g * 2 + m
                                names = (("q", "tq"), ("k", "tk"))[m]
                                act.wait_ge(y_done, i * 4 + n + 1)
                                act.wait_ge(pool_lo, i * 6 + 6)
                                act.wait_ge(tq_rest, i * 2 + 2)
                                if m == 0:
                                    nc.scalar.activation(full["q"][g][:], y_ps[n % 2][:], ACT.Identity, bias=bias[:, 2, g:g + 1],
                                                         scale=0.25).then_inc(full_done, 1)
                                else:
                                    nc.scalar.activation(full["k"][g][:], y_ps[n % 2][:], ACT.Identity,
                                                         bias=bias[:, 1, g:g + 1]).then_inc(full_done, 1)
                                nc.scalar.activation(full[names[1]][g][:], y_ps[n % 2][:], ACT.Tanh,
                                                     bias=bias[:, m, g:g + 1]).then_inc(full_done, 1)

                x_high(0, 0)
                in_turn(nc.scalar, body)

            @block.tensor
            def _(pe):
                pe.wait_ge(proj["split"], 3)
                pe.sem_inc(x_lo_done, 1)
                pe.sem_inc(v_read, 2)

                def split_product(out, terms, last_sem):
                    for z, (a, b) in enumerate(terms):
                        last = nc.tensor.matmul(out, a, b, start=(z == 0), stop=(z == len(terms) - 1))
                    last.then_inc(last_sem, 1)

                def transposes(i):
                    pe.wait_ge(x_lo_done, i + 1)
                    for u in range(U):
                        pe.wait_ge(normed, i * U + u + 1)
                        for k in range(KD):
                            last = nc.tensor.transpose(tp[:, k, u * P:(u + 1) * P], stage[u][:, k * P:(k + 1) * P], c["ident"][:])
                    last.then_inc(tposed, 1)

                def q_or_k(i, half, g, m):
                    n = g * 2 + m
                    if n >= 2:
                        pe.wait_ge(full_done, 8 + i * 8 + (n - 1) * 2)
                    else:
                        pe.wait_ge(full_done, 8 + i * 8)
                    split_product(y_ps[n % 2][:], [(wt(a, m, k, g * P, P), b[half][:, k, :]) for k in range(KD)
                                                   for a, b in ((w_hi, x_hi), (w_hi, x_lo), (w_lo, x_hi))], y_done)

                def tangents(i, g):
                    pe.wait_ge(tq_rest, 2 + i * 2 + g + 1)
                    pe.wait_ge(t_read, i * 2 + 2)
                    split_product(t_ps[g][:], [(jt(w_hi, g), tq_hi[g][:]), (jt(w_hi, g), tq_lo[g][:]),
                                               (jt(w_lo, g), tq_hi[g][:])], t_done)

                def values(i, half, u):
                    pe.wait_ge(v_read, i * U + u + 1)
                    split_product(v_ps[u % 2][:, 0:D], [(a[half][:, k, u * P:(u + 1) * P], wt(b, 2, k, 0, D)) for k in range(KD)
                                                        for a, b in ((x_hi, w_hi), (x_lo, w_hi), (x_hi, w_lo))], v_done)

                def body(b, more):
                    for half in range(2):
                        i = b * 2 + half
                        go_on = more or half == 0
                        first_products(i, half)
                        if go_on:
                            transposes(i + 1)
                        q_or_k(i, half, 1, 0)
                        tangents(i, 0)
                        q_or_k(i, half, 1, 1)
                        tangents(i, 1)
                        for u in range(U):
                            values(i, half, u)

                def first_products(i, half):
                    pe.wait_ge(x_lo_done, i + 2)
                    q_or_k(i, half, 0, 0)
                    q_or_k(i, half, 0, 1)

                transposes(0)
                in_turn(nc.tensor, body)


EARLY = (BATCH - 1) * HEADS * 2


def of_heads(o_dram):
    return o_dram.rearrange("g (j r) (a c) -> (g j) r a c", j=GH, a=2)


def attend(kit, c, packs, v_dram, o_dram, inv_dram, bo_dram, group, group_in):
    nc, x = kit.nc, c["x"]
    GROUPS = BATCH * NG
    NB = 3
    def diagonal(k0):
        return [(k0, 0, 0, QC, 0), (k0 + 3, 7 * P, 3 * P, P, P), (k0 + 1, 4 * P, P, 3 * P, 0)], [(k0 + 2, 0, 2 * P, 2 * P, 0)]
    A0, B0 = diagonal(0)
    A1, B1 = diagonal(4)
    full_pair = lambda k0: [(k0, 0, 0, QC, 0), (k0 + 1, QC, 0, QC, 0)]
    STEPS = [(0, A0), (0, B0), (1, full_pair(0)), (1, full_pair(2)), (1, A1), (1, B1)]
    WIDTH = [1024, 256, 1024, 1024, 1024, 256]
    NS = len(STEPS)
    UNITS = [(0, 0), (3, 0), (1, 0), (4, 0), (2, 0), (5, 0), (4, 1), (6, 0), (5, 1), (7, 0), (6, 1), (7, 1)]
    NU = len(UNITS)
    with ExitStack() as ctx:
        sb = lambda n, s, dt=F32: kit.sb(f"a_{n}", s, dt, ctx)
        ps = lambda n, s: kit.ps(f"a_{n}", s, ctx)
        tiles = [group] + [group_tiles(kit, ctx, u) for u in range(1, NB)]
        qp, kp, vg = zip(*tiles)
        wts = [sb(f"wts{u}", [P, GH, 2 * QC]) for u in range(2)]
        parts = [sb(f"parts{u}", [P, KT, 2]) for u in range(2)]
        tops = [sb(f"tops{u}", [P, KT]) for u in range(2)]
        neg = [sb(f"neg{u}", [KT, P], F32R) for u in range(2)]
        o_sb = [sb(f"o_sb{u}", [P, QC]) for u in range(2)]
        masked = [sb(f"masked{u}", [P, QC], BF16) for u in range(3)]
        bo = sb("bo", [P, D])
        sums = sb("sums", [EARLY, QC])
        s_ps = [ps(f"s{u}", [P, 2 * QC]) for u in range(2)]
        NM = 3
        m_ps = [ps(f"m{u}", [P, QC]) for u in range(NM)]
        o_ps = ps("o", [P, QC])
        (made, bo_in, scored, weighed, cleared, mixed, maxed, max_read, topped, turned, negated, o_taken,
         bo_added, sums_in, inverted, inv_out) = kit.sems(
            "a", "made bo_in scored weighed cleared mixed maxed max_read topped turned negated o_taken bo_added sums_in inverted inv_out")
        loaded = [group_in] + kit.sems("a_loaded", "1 2")
        row_in = kit.sems("a_row_in", "0 1 2 3")
        stored = kit.sems("a_stored", "0 1")
        NL = GROUP_LOADS
        MIX0, OUT0 = 2, 16
        on_diagonal = lambda s: [b for b in STEPS[s][1] if b[0] // 4 == STEPS[s][0]]
        clears = [sum(len(on_diagonal(z)) for z in range(s)) for s in range(NS + 1)]
        TURNS = (7, 15, 22)
        UNITS_AT = lambda q: [(q // 6, 2 * (q % 6) + d) for d in range(2)]
        FIRST = [(h, z) for h in range(GH) for z in (*range(NU), None)]
        ORDER = [e for q in range(NS * GH) for e in UNITS_AT(q) + ([(TURNS.index(q), None)] if q in TURNS else [])]
        ORDER.append((GH - 1, None))
        assert len(ORDER) % NM == 1 and FIRST[-NM:] == ORDER[-NM:]

        def bank(ub, order, entry):
            return (ub + order.index(entry)) % NM

        def before(n, order, entry):
            at = order.index(entry) - NM
            return (n, order[at]) if at >= 0 else (n - 1, ORDER[at])

        def groups(eng, body):
            assert GROUPS % NB == 1
            with eng.Fori(0, GROUPS // NB) as i:
                for u in range(NB):
                    body(i, u, False)
            body(GROUPS // NB, 0, True)

        with nc.Block() as block:

            @block.sync
            def _(sp):
                sp.dma_start(bo[:], bo_dram.partition_broadcast(P)).then_inc(bo_in, 16)

                def rows(gi, u):
                    for h in range(GH):
                        sp.wait_ge(negated, gi * GH + h + 1)
                        sp.dma_start(qp[u][PACK:PACK + 1, h, :].bitcast(F32), neg[h % 2][:].bitcast(F32)).then_inc(row_in[h], 16)

                def store(g):
                    for ch in range(2):
                        sp.wait_ge(o_taken, 1 + g * 2 + ch + 1)
                        sp.dma_start(o_dram.rearrange("g p c -> (g p) c")[bass.ds(g * P, P), ch * QC:(ch + 1) * QC],
                                     o_sb[ch][:]).then_inc(stored[ch], 16)

                def next_groups(g, u, more):
                    rows(g + 1, (u + 1) % NB)
                    if more:
                        sp.wait_ge(mixed, MIX0 + (g + 1) * NS)
                        load_group(nc.sync, tiles[u], packs, v_dram, g + NB, loaded[u])
                    store(g)

                for g in range(1, NB):
                    load_group(nc.sync, tiles[g], packs, v_dram, g, loaded[g])
                for ch in range(2):
                    sp.sem_inc(stored[ch], OUT0)
                rows(0, 0)
                FULL = (GROUPS - NB) // NB
                with nc.sync.Fori(0, FULL) as i:
                    for u in range(NB):
                        next_groups(i * NB + u, u, True)
                for g in range(FULL * NB, GROUPS - 1):
                    next_groups(g, g % NB, g + NB < GROUPS)
                    if g == (BATCH - 1) * NG:
                        for ch in range(2):
                            sp.wait_ge(stored[ch], OUT0 + (g + 1) * 16)
                        sp.dma_start(sums[:], of_heads(o_dram)[0:EARLY // 2, HD, :, :]).then_inc(sums_in, 16)
                sp.wait_ge(inverted, 1)
                sp.dma_start(inv_dram[0:EARLY, :], sums[:]).then_inc(inv_out, 16)
                store(GROUPS - 1)
                sp.wait_ge(inv_out, 16)
                for ch in range(2):
                    sp.wait_ge(stored[ch], OUT0 + GROUPS * 16)

            @block.gpsimd
            def _(pool):
                link = chain(kit, pool, "pool_step")
                for u in range(2):
                    link(nc.gpsimd.memset(parts[u][:], -3e38))
                pool.sem_inc(made, 1)
                for u in range(NB):
                    link(nc.gpsimd.memset(kp[u][PACK:PACK + 1, :, :].bitcast(F32), 1.0))
                pool.sem_inc(made, 1)
                pool.wait_ge(bo_in, 16)
                xv = x[:].rearrange("p (t d) -> p t d", d=D)
                nc.gpsimd.tensor_tensor(xv, xv, bo[:].unsqueeze(1).to_broadcast([P, NT, D]), ALU.add).then_inc(bo_added, 1)

                def body(i, u, last):
                    g = i * NB + u
                    for s in range(NS):
                        for z, (kt, col, q0, w, lead) in enumerate(on_diagonal(s)):
                            if z == 0:
                                pool.wait_ge(weighed, 2 + g * NS * GH + (s + 1) * GH)
                                kit.part(pool)
                            block_w = wts[(u * NS + s) % 2][:, :, col:col + P]
                            nc.gpsimd.affine_select(out=block_w, in_=block_w, compare_op=ALU.is_ge, fill=0.0, base=0,
                                                    pattern=[[0, GH], [1, P]], channel_multiplier=-1).then_inc(cleared, 1)

                groups(nc.gpsimd, body)

            @block.vector
            def _(dve):
                dve.wait_ge(made, 1)
                dve.sem_inc(turned, 2)

                def maxima(n, ub, order, units):
                    for h, z in units:
                        qt, part = UNITS[z]
                        m = n * GH * NU + h * NU + z
                        dve.wait_ge(maxed, m + 1)
                        width = (qt + 1) * P - part * QC if part or qt < 4 else QC
                        top, seen = parts[h % 2][:, qt, part:part + 1], m_ps[bank(ub, order, (h, z))][:, 0:width]
                        if (qt + 1) * P == part * QC + width:
                            kit.part(dve)
                            nc.vector.tensor_tensor_reduce(masked[bank(ub, order, (h, z))][:, 0:width], seen, c["mask"][:, QC - width:], 1.0, MASKED,
                                                           ALU.add, ALU.max, top).then_inc(max_read, 1)
                        else:
                            nc.vector.reduce_max(top, seen, AX.X).then_inc(max_read, 1)
                        if z == NU - 1:
                            dve.wait_ge(max_read, m + 1)
                            dve.wait_ge(turned, n * GH + h + 1)
                            nc.vector.reduce_max(tops[h % 2][:], parts[h % 2][:], AX.X).then_inc(topped, 1)
                            dve.wait_ge(topped, n * GH + h + 1)

                def body(i, u, last):
                    g = i * NB + u
                    for s in range(NS):
                        for j in range(GH):
                            q = s * GH + j
                            if not last:
                                maxima(g + 1, (u + 1) % NB, ORDER, UNITS_AT(q))

                maxima(0, 0, FIRST, [e for e in FIRST if e[1] is not None])
                groups(nc.vector, body)
                dve.wait_ge(sums_in, 16)
                nc.vector.reciprocal(sums[:], sums[:]).then_inc(inverted, 1)

            @block.scalar
            def _(act):
                act.sem_inc(mixed, 2)

                def negate(n, ub, order, h):
                    act.wait_ge(turned, n * GH + h + 1 + 2)
                    if h >= 2:
                        act.wait_ge(row_in[h - 2], (n + 1) * 16)
                    elif order is ORDER:
                        act.wait_ge(row_in[h + 2], n * 16)
                    nc.scalar.activation(neg[h % 2][:], m_ps[bank(ub, order, (h, None))][0:KT, 0:P], ACT.Copy, scale=-1.0).then_inc(negated, 1)

                def take(g, ch):
                    act.wait_ge(mixed, 2 + g * NS + (2, 6)[ch])
                    act.wait_ge(stored[ch], OUT0 + g * 16)
                    nc.scalar.copy(o_sb[ch][:], o_ps[:]).then_inc(o_taken, 1)

                def body(i, u, last):
                    g = i * NB + u
                    for s in range(NS):
                        for j in range(GH):
                            q = s * GH + j
                            act.wait_ge(scored, g * NS * GH + q + 1)
                            if j == 0:
                                act.wait_ge(mixed, g * NS + s + 1)
                            w = WIDTH[s]
                            nc.scalar.activation(wts[(u * NS + s) % 2][:, j, 0:w], s_ps[q % 2][:, 0:w], ACT.Exp).then_inc(weighed, 1)
                            if s == 2 and j == 3:
                                take(g, 0)
                            if not last and q in TURNS:
                                negate(g + 1, (u + 1) % NB, ORDER, TURNS.index(q))
                    take(g, 1)
                    if not last:
                        negate(g + 1, (u + 1) % NB, ORDER, GH - 1)

                for h in range(GH):
                    negate(0, 0, FIRST, h)
                groups(nc.scalar, body)

            @block.tensor
            def _(pe):
                pe.sem_inc(weighed, 2)
                pe.sem_inc(o_taken, 1)

                def free_bank(n, order, entry, first):
                    if first and order.index(entry) < NM:
                        return
                    n, (h, z) = before(n, order, entry)
                    if z is None:
                        pe.wait_ge(negated, n * GH + h + 1)
                    else:
                        pe.wait_ge(max_read, n * GH * NU + h * NU + z + 1)

                def max_unit(n, ub, order, h, z, first=False):
                    qt, part = UNITS[z]
                    free_bank(n, order, (h, z), first)
                    width = (qt + 1) * P - part * QC if part or qt < 4 else QC
                    stream = max(width, 2 * P)
                    nc.tensor.matmul(m_ps[bank(ub, order, (h, z))][:, 0:stream], qp[ub][0:PACK, h, qt * P:(qt + 1) * P],
                                     kp[ub][0:PACK, h, part * QC:part * QC + stream], start=True, stop=True).then_inc(maxed, 1)

                def turn(n, ub, order, h):
                    pe.wait_ge(topped, n * GH + h + 1)
                    free_bank(n, order, (h, None), False)
                    nc.tensor.transpose(m_ps[bank(ub, order, (h, None))][0:KT, 0:P], tops[h % 2][:], c["ident"][:]).then_inc(turned, 1)

                def score(g, u, s, j):
                    ch, blocks = STEPS[s]
                    q = s * GH + j
                    if s == 0:
                        pe.wait_ge(row_in[j], (g + 1) * 16)
                    pe.wait_ge(weighed, g * NS * GH + q + 1)
                    for kt, col, q0, w, lead in blocks:
                        at = ch * QC + q0
                        last = nc.tensor.matmul(s_ps[q % 2][:, col - lead:col + w], kp[u][:, j, kt * P:(kt + 1) * P],
                                                qp[u][:, j, at - lead:at + w], start=True, stop=True)
                    last.then_inc(scored, 1)

                def mix(g, u, s, blocks, done):
                    ch = STEPS[s][0]
                    for kt, col, q0, w, lead in blocks:
                        if kt == 0:
                            pe.wait_ge(o_taken, 1 + g * 2 + ch)
                        if kt // 4 == ch:
                            pe.wait_ge(cleared, g * clears[NS] + clears[s + 1])
                        for j in range(GH):
                            pe.wait_ge(weighed, 2 + g * NS * GH + s * GH + j + 1)
                            last = nc.tensor.matmul(o_ps[j * HP:(j + 1) * HP, q0:q0 + w], vg[u][:, kt, j, :],
                                                    wts[(u * NS + s) % 2][:, j, col:col + w], start=(kt == 0),
                                                    stop=(kt == ch * 4 + 2), skip_group_check=True)
                    if done:
                        last.then_inc(mixed, 1)

                def body(i, u, last):
                    g = i * NB + u
                    if not last:
                        pe.wait_ge(loaded[(u + 1) % NB], (i + (u + 1) // NB + 1) * NL * 16)
                    for s in range(NS):
                        for j in range(GH):
                            q = s * GH + j
                            units = [] if last else UNITS_AT(q)
                            for h, z in units[:1]:
                                max_unit(g + 1, (u + 1) % NB, ORDER, h, z)
                            score(g, u, s, j)
                            for h, z in units[1:]:
                                max_unit(g + 1, (u + 1) % NB, ORDER, h, z)
                            if s:
                                blocks = STEPS[s - 1][1]
                                when = {1: (3,), 2: (1, 3), 3: (2, 3)}[len(blocks)]
                                part = {j_: blocks[n:n + 1] if n + 1 < len(when) else blocks[n:] for n, j_ in enumerate(when)}.get(j)
                                if part:
                                    mix(g, u, s - 1, part, j == 3)
                            if not last and q in TURNS:
                                turn(g + 1, (u + 1) % NB, ORDER, TURNS.index(q))
                    mix(g, u, NS - 1, STEPS[NS - 1][1], True)
                    if not last:
                        turn(g + 1, (u + 1) % NB, ORDER, GH - 1)

                pe.wait_ge(loaded[0], NL * 16)
                for h in range(GH):
                    for z in range(NU):
                        max_unit(0, 0, FIRST, h, z, first=True)
                    turn(0, 0, FIRST, h)
                pe.wait_ge(made, 2)
                groups(nc.tensor, body)


def project_out(kit, c, o_dram, inv_dram, wo_dram):
    nc, x = kit.nc, c["x"]
    U = QC // P
    with ExitStack() as ctx:
        wo = kit.sb("p_wo", [P, KD, D], F32, ctx)
        sums = kit.sb("p_sums", [P, QC], F32, ctx)
        o, inv, mean = ([kit.sb(f"p_{n}{u}", [P, KD, QC], F32, ctx) for u in range(2)] for n in ("o", "inv", "mean"))
        NY = U
        y_ps = [kit.ps(f"p_y{u}", [P, QC], ctx) for u in range(NY)]
        wo_in, sums_in, inverted, inv_out, averaged, y_done, y_read, stats_done = kit.sems(
            "p", "wo_in sums_in inverted inv_out averaged y_done y_read stats_done")
        o_in = kit.sems("p_o_in", "0 1")
        NL = KD * 2
        assert BATCH * HEADS * SEQ == P * QC
        with nc.Block() as block:

            @block.sync
            def _(sp):
                sp.dma_start(sums[EARLY:, :], of_heads(o_dram)[EARLY // 2:, HD, :, :]).then_inc(sums_in, 16)
                sp.dma_start(wo[:], wo_dram.rearrange("(k p) d -> p k d", p=P)).then_inc(wo_in, 16)
                sp.sem_inc(averaged, 2)
                inv_of = inv_dram.rearrange("(h a) c -> h a c", a=2)
                HK = P // HD

                def load(b, half):
                    sp.wait_ge(averaged, b * 2 + half + 1)
                    for k in range(KD):
                        heads = bass.ds(b * HEADS + k * HK, HK)
                        sp.dma_start(o[half][:, k, :], of_heads(o_dram)[heads, 0:HD, half, :]).then_inc(o_in[half], 16)
                        sp.dma_start(inv[half][:, k, :], inv_of[heads, half:half + 1, :]
                                     .to_broadcast([HK, HD, QC])).then_inc(o_in[half], 16)

                for half in range(2):
                    load(0, half)
                sp.wait_ge(inverted, 1)
                sp.dma_start(inv_dram[EARLY:, :], sums[EARLY:, :]).then_inc(inv_out, 16)
                sp.wait_ge(inv_out, 16)
                with nc.sync.Fori(1, BATCH) as b:
                    for half in range(2):
                        load(b, half)
                kit.clear_again(sp)

            @block.vector
            def _(dve):
                dve.wait_ge(sums_in, 16)
                nc.vector.reciprocal(sums[EARLY:, :], sums[EARLY:, :]).then_inc(inverted, 1)
                with nc.vector.Fori(0, BATCH) as b:
                    def add(half):
                        for u in range(U):
                            t = (b * 2 + half) * U + u
                            dve.wait_ge(y_done, 2 * U + t + 1)
                            xt = x[:, bass.ds(t * D, D)]
                            nc.vector.tensor_tensor(xt, y_ps[u % NY][:, 0:D], xt, ALU.add).then_inc(y_read, 1)
                        for u in range(U):
                            t = (b * 2 + half) * U + u
                            dve.wait_ge(y_read, NY + t + 1)
                            tile_stats(nc, c, t).then_inc(stats_done, 1)

                    add(0)
                    add(1)
                dve.wait_ge(stats_done, NT)

            @block.gpsimd
            def _(pool):
                pool.sem_inc(y_done, 2 * U)
                with nc.gpsimd.Fori(0, BATCH) as b:
                    for half in range(2):
                        pool.wait_ge(o_in[half], (b + 1) * NL * 16)
                        kit.part(pool)
                        pool.wait_ge(y_done, (b * 2 + half + 1) * U)
                        nc.gpsimd.tensor_tensor(mean[half][:], o[half][:], inv[half][:], ALU.mult).then_inc(averaged, 1)

            @block.tensor
            def _(pe):
                pe.wait_ge(wo_in, 16)
                pe.sem_inc(y_read, NY)
                with nc.tensor.Fori(0, BATCH) as b:
                    for half in range(2):
                        i = b * 2 + half
                        pe.wait_ge(averaged, i + 1 + 2)
                        for u in range(U):
                            t = i * U + u
                            pe.wait_ge(y_read, t + 1)
                            for k in range(KD):
                                last = nc.tensor.matmul(y_ps[u % NY][:, 0:D], mean[half][:, k, u * P:(u + 1) * P], wo[:, k, :],
                                                        start=(k == 0), stop=(k == KD - 1))
                            last.then_inc(y_done, 1)


def program(nc, x, w, out):
    with ExitStack() as ctx:
        kit = Kit(nc, ctx)
        c = constants(kit)
        gates = kit.sb("gates", [P, TOPK, NT])
        scratch = lambda name, shape: nc.dram_tensor(name, shape, F32, kind="Internal").ap()
        disp = [scratch(f"disp{r}", (EXP * CAP, ROW)) for r in range(2)]
        ydram = scratch("choice_rows", (TOPK * TOK, D))
        spare = scratch("spare", (4, P, 16))
        packs = scratch("packs", (8, BATCH, D, SEQ))
        v_dram = scratch("values", (BATCH * NG, KT, P, GH * HP))
        o_dram = scratch("attended", (BATCH * NG, P, SEQ))
        inv_dram = scratch("inverse_sums", (P, QC))

        def mixture(r):
            with ExitStack() as both:
                weights = expert_weights(kit, both, r)
                route(kit, c, r, w["W_in"], w["W_out"], disp[r], ydram, gates, weights)
                experts(kit, c, r, w["W_in"], w["W_out"], disp[r], None if r else disp[1], ydram, spare, weights)

        with ExitStack() as first:
            c["blank"] = kit.sb("blank", [P, ST * ROW], F32, first)
            build_constants(kit, c, x, w["Wg"], disp[0])
            mixture(0)
        with ExitStack() as attention:
            group = group_tiles(kit, attention, 0)
            group_in = kit.sem("a_loaded_0")
            with ExitStack() as projecting:
                proj = projections(kit, projecting, w)
                combine(kit, c, 0, ydram, gates, None, proj)
                project(kit, c, proj, packs, v_dram, group, group_in)
            attend(kit, c, packs, v_dram, o_dram, inv_dram, w["bo"], group, group_in)
        project_out(kit, c, o_dram, inv_dram, w["WoT"])
        mixture(1)
        combine(kit, c, 1, ydram, gates, out)


_NAMES = ["Wg", "W_in", "W_out", "WqT", "WkT", "WvT", "WoT", "bq", "bk", "bv", "bo", "J", "lam"]


def kernel(**inputs):
    import numpy as np
    import concourse.bacc as bacc
    from concourse.bass_utils import run_bass_kernel_spmd

    a = lambda n: np.asarray(inputs[n])
    arrays = {"x": a("L0_attn_x").reshape(TOK, D), "Wg": a("L0_ffn_Wg"), "W_in": a("L0_ffn_W_in"), "W_out": a("L0_ffn_W_out"),
              "J": a("L0_attn_J_attn"), "lam": a("L0_attn_lambda_attn").reshape(1)}
    for n in ("q", "k", "v", "o"):
        arrays[f"W{n}T"] = a(f"L0_attn_W{n}").T
        arrays[f"b{n}"] = a(f"L0_attn_b{n}")
    arrays = {n: np.ascontiguousarray(v) for n, v in arrays.items()}
    nc = bacc.Bacc("TRN2", target_bir_lowering=False, num_devices=1)
    dram = {n: nc.dram_tensor(f"in_{n}", v.shape, mybir.dt.from_np(v.dtype), kind="ExternalInput").ap() for n, v in arrays.items()}
    out = nc.dram_tensor("out", (TOK, D), F32, kind="ExternalOutput").ap()
    program(nc, dram["x"], {n: dram[n] for n in _NAMES}, out)
    got = run_bass_kernel_spmd(nc, [{f"in_{n}": v for n, v in arrays.items()}], core_ids=[0])
    return got.results[0]["out"].reshape(BATCH, SEQ, D)
```
